# Optimizing a Trainium2 kernel written in Bass

```python
import numpy as np
import jax
import jax.numpy as jnp

def _softmax(x, axis=-1):
    return jax.nn.softmax(x, axis=axis)

def _gelu(x):
    return jax.nn.gelu(x, approximate=True)

def _silu(x):
    return jax.nn.silu(x)

def _sigmoid(x):
    return jax.nn.sigmoid(x)

def _layernorm(x, axis=-1, eps=1e-05):
    m = jnp.mean(x, axis=axis, keepdims=True)
    v = jnp.var(x, axis=axis, keepdims=True)
    return (x - m) / jnp.sqrt(v + eps)

def _scatter_add(tgt, idx, src, axis=0):
    return tgt.at[idx].add(src)

def _segment_sum(src, seg, n):
    return jax.ops.segment_sum(src, seg, n)
kernel_name = 'mk_gnn_preln_d2_gnn_r32_037309'

def setup_inputs(seed: int=0):
    np.random.seed(seed)
    _w = jnp.asarray

    def _rec_inputs():
        import jax
        import jax.numpy as jnp
        _gk = jax.random.key(seed)
        x = -0.000202 + 1 * jax.random.normal(jax.random.fold_in(_gk, 1), (50000, 128), jnp.float32)
        src = jax.random.randint(jax.random.fold_in(_gk, 2), (50000,), 0, 50000, jnp.int32)
        dst = jnp.minimum((50000 * jax.random.uniform(jax.random.fold_in(_gk, 3), (50000,)) ** 2.0).astype(jnp.int32), 49999)
        _o = jnp.argsort(dst, stable=True)
        src = src[_o]
        dst = dst[_o]
        edge_attr_64 = 0.000196303 + 1.00016 * jax.random.normal(jax.random.fold_in(_gk, 12), (50000, 64), jnp.float32)
        return (x, src, dst, edge_attr_64)
    x, src, dst, edge_attr_64 = _rec_inputs()

    def _L0_gnn_setup():
        import jax, jax.numpy as jnp
        import numpy as np
        N_NODES = 50000
        N_EDGES = 12500
        NODE_F = 128
        EDGE_F = 64
        HID = 128
        N_LAYERS = 2

        def _mlp(x, w1, b1, w2, b2):
            return jnp.maximum(x @ w1 + b1, 0.0) @ w2 + b2
        key = jax.random.key(seed)
        ks = jax.random.split(key, 24)
        s = 0.02
        inp = {'node_features': jax.random.normal(ks[0], (N_NODES, NODE_F), jnp.float32), 'edge_list': jax.random.randint(ks[1], (N_EDGES, 2), 0, N_NODES, jnp.int32), 'edge_features': jax.random.normal(ks[2], (N_EDGES, EDGE_F), jnp.float32), 'num_nodes': N_NODES, 'ne_w1': jax.random.normal(ks[3], (NODE_F, HID), jnp.float32) * s, 'ne_b1': jnp.zeros((HID,), jnp.float32), 'ne_w2': jax.random.normal(ks[4], (HID, HID), jnp.float32) * s, 'ne_b2': jnp.zeros((HID,), jnp.float32), 'ee_w1': jax.random.normal(ks[5], (EDGE_F, HID), jnp.float32) * s, 'ee_b1': jnp.zeros((HID,), jnp.float32), 'ee_w2': jax.random.normal(ks[6], (HID, HID), jnp.float32) * s, 'ee_b2': jnp.zeros((HID,), jnp.float32), 'ml_w1': jax.random.normal(ks[7], (N_LAYERS, 3 * HID, HID), jnp.float32) * s, 'ml_b1': jnp.zeros((N_LAYERS, HID), jnp.float32), 'ml_w2': jax.random.normal(ks[8], (N_LAYERS, HID, HID), jnp.float32) * s, 'ml_b2': jnp.zeros((N_LAYERS, HID), jnp.float32), 'agg_w1': jax.random.normal(ks[9], (HID, HID), jnp.float32) * s, 'agg_b1': jnp.zeros((HID,), jnp.float32), 'agg_w2': jax.random.normal(ks[10], (HID, HID), jnp.float32) * s, 'agg_b2': jnp.zeros((HID,), jnp.float32)}
        return inp
    _L0_gnn_all = _L0_gnn_setup()
    _L0_gnn_in = {k: v for k, v in _L0_gnn_all.items() if k in ('ne_w1', 'ne_b1', 'ne_w2', 'ne_b2', 'ee_w1', 'ee_b1', 'ee_w2', 'ee_b2', 'ml_w1', 'ml_b1', 'ml_w2', 'ml_b2', 'agg_w1', 'agg_b1', 'agg_w2', 'agg_b2')}
    del _L0_gnn_all

    def _L1_gnn_setup():
        import jax, jax.numpy as jnp
        import numpy as np
        N_NODES = 3125
        key = jax.random.key(seed)
        k1, k2, k3 = jax.random.split(key, 3)
        x = jax.random.normal(k1, (N_NODES, 128), dtype=jnp.float32)
        src_idx = jax.random.randint(k2, (62500,), 0, N_NODES, dtype=jnp.int64)
        dst_idx = jax.random.randint(k3, (62500,), 0, N_NODES, dtype=jnp.int64)
        return {'x': x, 'src_idx': src_idx, 'dst_idx': dst_idx}
    _L1_gnn_all = _L1_gnn_setup()
    _L1_gnn_in = {k: v for k, v in _L1_gnn_all.items() if k in ()}
    del _L1_gnn_all
    return {'x': x, 'src': src, 'dst': dst, 'edge_attr_64': edge_attr_64, 'L0_gnn_ne_w1': _L0_gnn_in['ne_w1'], 'L0_gnn_ne_b1': _L0_gnn_in['ne_b1'], 'L0_gnn_ne_w2': _L0_gnn_in['ne_w2'], 'L0_gnn_ne_b2': _L0_gnn_in['ne_b2'], 'L0_gnn_ee_w1': _L0_gnn_in['ee_w1'], 'L0_gnn_ee_b1': _L0_gnn_in['ee_b1'], 'L0_gnn_ee_w2': _L0_gnn_in['ee_w2'], 'L0_gnn_ee_b2': _L0_gnn_in['ee_b2'], 'L0_gnn_ml_w1': _L0_gnn_in['ml_w1'], 'L0_gnn_ml_b1': _L0_gnn_in['ml_b1'], 'L0_gnn_ml_w2': _L0_gnn_in['ml_w2'], 'L0_gnn_ml_b2': _L0_gnn_in['ml_b2'], 'L0_gnn_agg_w1': _L0_gnn_in['agg_w1'], 'L0_gnn_agg_b1': _L0_gnn_in['agg_b1'], 'L0_gnn_agg_w2': _L0_gnn_in['agg_w2'], 'L0_gnn_agg_b2': _L0_gnn_in['agg_b2']}

def reference(x, src, dst, edge_attr_64, L0_gnn_ne_w1, L0_gnn_ne_b1, L0_gnn_ne_w2, L0_gnn_ne_b2, L0_gnn_ee_w1, L0_gnn_ee_b1, L0_gnn_ee_w2, L0_gnn_ee_b2, L0_gnn_ml_w1, L0_gnn_ml_b1, L0_gnn_ml_w2, L0_gnn_ml_b2, L0_gnn_agg_w1, L0_gnn_agg_b1, L0_gnn_agg_w2, L0_gnn_agg_b2):
    import jax
    import jax.numpy as jnp

    def _L0_gnn_ref(node_features, edge_list, edge_features, num_nodes, ne_w1, ne_b1, ne_w2, ne_b2, ee_w1, ee_b1, ee_w2, ee_b2, ml_w1, ml_b1, ml_w2, ml_b2, agg_w1, agg_b1, agg_w2, agg_b2):
        import jax, jax.numpy as jnp
        import numpy as np
        N_NODES = 50000
        N_EDGES = 12500
        NODE_F = 128
        EDGE_F = 64
        HID = 128
        N_LAYERS = 2

        def _mlp(x, w1, b1, w2, b2):
            return jnp.maximum(x @ w1 + b1, 0.0) @ w2 + b2
        node_emb = _mlp(node_features, ne_w1, ne_b1, ne_w2, ne_b2)
        edge_emb = _mlp(edge_features, ee_w1, ee_b1, ee_w2, ee_b2)
        src = edge_list[:, 0]
        dst = edge_list[:, 1]
        for l in range(ml_w1.shape[0]):
            h_s = node_emb[src]
            h_d = node_emb[dst]
            m_fwd = _mlp(jnp.concatenate([h_s, edge_emb, h_d], axis=-1), ml_w1[l], ml_b1[l], ml_w2[l], ml_b2[l])
            m_bwd = _mlp(jnp.concatenate([h_d, edge_emb, h_s], axis=-1), ml_w1[l], ml_b1[l], ml_w2[l], ml_b2[l])
            new_node_emb = node_emb.at[dst].add(m_fwd).at[src].add(m_bwd)
            node_emb = _mlp(new_node_emb, agg_w1, agg_b1, agg_w2, agg_b2)
        return node_emb

    def _L1_gnn_ref(x, src_idx, dst_idx):
        import jax, jax.numpy as jnp
        import numpy as np
        N_NODES = 3125
        x_j = x[src_idx]
        agg = jax.ops.segment_sum(x_j, dst_idx, num_segments=x.shape[0])
        return x + agg
    edge_index_t = jnp.stack([src, dst], axis=1)
    h = jnp.maximum(_layernorm(x, axis=-1), 0.0)
    x = x + _L0_gnn_ref(h, edge_index_t, edge_attr_64, 50000, L0_gnn_ne_w1, L0_gnn_ne_b1, L0_gnn_ne_w2, L0_gnn_ne_b2, L0_gnn_ee_w1, L0_gnn_ee_b1, L0_gnn_ee_w2, L0_gnn_ee_b2, L0_gnn_ml_w1, L0_gnn_ml_b1, L0_gnn_ml_w2, L0_gnn_ml_b2, L0_gnn_agg_w1, L0_gnn_agg_b1, L0_gnn_agg_w2, L0_gnn_agg_b2)
    h = jnp.maximum(_layernorm(x, axis=-1), 0.0)
    x = x + _L1_gnn_ref(h, src, dst)
    return x

_drawn_inputs = setup_inputs


def setup_inputs(seed=0):
    import zlib

    import numpy as np

    out = dict(_drawn_inputs(seed))
    spreads = {'L0_gnn_ne_b1': (0.0, 0.8),
     'L0_gnn_ne_b2': (0.0, 0.8),
     'L0_gnn_ee_b1': (0.0, 0.8),
     'L0_gnn_ee_b2': (0.0, 0.8),
     'L0_gnn_ml_b1': (0.0, 0.8),
     'L0_gnn_ml_b2': (0.0, 0.662),
     'L0_gnn_agg_b1': (0.0, 0.433),
     'L0_gnn_agg_b2': (0.0, 0.1)}
    factors = {'edge_attr_64': 8.0,
     'L0_gnn_ne_w1': 8.0,
     'L0_gnn_ne_w2': 8.0,
     'L0_gnn_ee_w1': 8.0,
     'L0_gnn_ee_w2': 8.0,
     'L0_gnn_ml_w1': 8.0,
     'L0_gnn_ml_w2': 8.0,
     'L0_gnn_agg_w1': 4.494}
    for name, (base, spread) in spreads.items():
        noise = np.random.default_rng([zlib.crc32(name.encode()), seed]).standard_normal(out[name].shape)
        drawn = base * np.exp(spread * noise) if base else spread * noise
        out[name] = jnp.asarray(drawn.astype(out[name].dtype))
    for name, factor in factors.items():
        out[name] = (out[name] * factor).astype(out[name].dtype)
    return out
```

```python
import concourse.bass as bass
from concourse import mybir
from contextlib import ExitStack

FP32 = mybir.dt.float32
BF16 = mybir.dt.bfloat16
I32 = mybir.dt.int32
ALU = mybir.AluOpType
ACT = mybir.ActivationFunctionType

P = 128
N = 50000
FE = 64
BLK = 256
NB = -(-N // BLK)
NP = NB * BLK
EC = NP // P
IT = NP // (4 * P)
MINCH = 4
GRP = 4
UNR = 16
TMAX = -(-(2 * NP // P + MINCH * NB) // UNR) * UNR
REC = 260
META = 128
E1AT = 132
PRIME = 4
AHEAD = 2
EPS = 1e-5


def positive(count):
    return not isinstance(count, int) or count > 0




class Pools:

    def __init__(self, nc, ctx):
        self.nc, self.ctx = nc, ctx

    def sb(self, name, shape, dt=FP32):
        return self.ctx.enter_context(self.nc.sbuf_tensor(name, shape, dt))

    def ps(self, name, shape, dt=FP32):
        return self.ctx.enter_context(self.nc.psum_tensor(name, shape, dt))

    def sem(self, name):
        return self.ctx.enter_context(self.nc.semaphore(name))


def setup_phase(nc, w, g, he):
    with ExitStack() as ctx:
        q = Pools(nc, ctx)
        src_i = q.sb("src_i", [P, EC], I32)
        dst_i = q.sb("dst_i", [P, EC], I32)
        wide = q.sb("wide", [P, UNR * REC])
        tmp_i = q.sb("tmp_i", [P, BLK], I32)
        lower = q.sb("lower", [P, P])
        ones = q.sb("ones", [P, P])
        r0 = q.sb("r0", [P, 384])
        r1 = q.sb("r1", [P, 384])
        re = q.sb("re", [P, 256])
        raw = q.sb("raw", [P, 5, P])
        rawt = q.sb("rawt", [P, 5, P])
        cols = q.sb("cols", [P, 6])
        bcol = q.sb("bcol", [P, 3, P])
        rows = q.sb("rows", [1, 2, P])
        work = q.sb("work", [P, 6, NB])
        work_i = q.sb("work_i", [P, 6, NB], I32)
        tps = q.ps("tps", [P, 4, P])
        tps2 = q.ps("tps2", [P, P])
        fps = q.ps("fps", [P, 5, 512])
        hps = q.ps("hps", [P, 2, 256])

        idx_clear, idx_in = q.sem("idx_clear"), q.sem("idx_in")
        w_in, const_done = q.sem("w_in"), q.sem("const_done")
        vec, act_done = q.sem("vec"), q.sem("act_done")
        wt_ps, wt_sb, fold_ps, col_sb = q.sem("wt_ps"), q.sem("wt_sb"), q.sem("fold_ps"), q.sem("col_sb")
        hist_done, hist_ps = q.sem("hist_done"), q.sem("hist_ps")
        zero_done, count_done, he_zeroed = q.sem("zero_done"), q.sem("count_done"), q.sem("he_zeroed")
        tail = NP - N
        full_p = P - 1
        last_c = EC - tail
        block = ctx.enter_context(nc.Block())

        @block.sync
        def _(sp):
            sp.wait_ge(idx_clear, 2)
            sp.nop(nofuse=True)
            for t, a in ((dst_i, w["dst"]), (src_i, w["src"])):
                sp.dma_start(t[0:full_p, :], a[0:full_p * EC].rearrange("(p c) -> p c", p=full_p)).then_inc(idx_in, 16)
                sp.dma_start(t[full_p:P, 0:last_c],
                             a[full_p * EC:N].rearrange("(p c) -> p c", p=1)).then_inc(idx_in, 16)
            sp.wait_ge(count_done, 1)
            sp.nop(nofuse=True)
            turns = sp.value_load(g["turns"][0:1, 0:1], min_val=1, max_val=TMAX // UNR)
            sp.wait_ge(zero_done, 1)
            sp.nop(nofuse=True)
            with sp.Fori(0, turns) as k:
                sp.dma_start(he[bass.ds(k * (UNR * P), UNR * P), :].rearrange("(p r) f -> p (r f)", p=P),
                             wide[:, :]).then_inc(he_zeroed, 16)
            sp.wait_ge(he_zeroed, turns * 16)
            sp.nop(nofuse=True)

        @block.scalar
        def _(act):
            loads = [(g["ne1"][:, :], w["ne_w1"]), (g["ee1"][:, :], w["ee_w1"]), (g["agw2"][:, :], w["agg_w2"]),
                     (r0[:, 0:128], w["ml_w1"][0, 0:128, :]), (r0[:, 128:256], w["ml_w1"][0, 256:384, :]),
                     (r0[:, 256:384], w["agg_w1"]),
                     (r1[:, 0:128], w["ml_w1"][1, 0:128, :]), (r1[:, 128:256], w["ml_w1"][1, 256:384, :]),
                     (r1[:, 256:384], w["agg_w1"]),
                     (re[:, 0:128], w["ml_w1"][0, 128:256, :]), (re[:, 128:256], w["ml_w1"][1, 128:256, :]),
                     (raw[:, 0, :], w["ne_w2"]), (raw[:, 1, :], w["agg_w2"]), (raw[:, 2, :], w["ee_w2"]),
                     (raw[:, 3, :], w["ml_w2"][0]), (raw[:, 4, :], w["ml_w2"][1])]
            columns = [w["ne_b2"], w["agg_b2"], w["ee_b2"], w["ml_b2"][0], w["ml_b2"][1], w["agg_b1"]]
            loads += [(cols[:, k:k + 1], c.rearrange("(p a) -> p a", a=1)) for k, c in enumerate(columns)]
            loads += [(g["ne_b1"][:, :], w["ne_b1"].rearrange("(p a) -> p a", a=1)),
                      (g["ee_b1"][:, :], w["ee_b1"].rearrange("(p a) -> p a", a=1)),
                      (rows[:, 0, :], w["ml_b1"][0:1, :]), (rows[:, 1, :], w["ml_b1"][1:2, :]),
                      (g["agb2"][0:1, :], w["agg_b2"].rearrange("(a n) -> a n", a=1))]
            for to, frm in loads:
                act.dma_start(to, frm).then_inc(w_in, 16)
            act.wait_ge(w_in, 16 * len(loads))
            act.wait_ge(const_done, 5)
            for k in range(3):
                nc.scalar.activation(bcol[:, k, :], ones[:, :], ACT.Copy, scale=cols[:, k:k + 1]).then_inc(col_sb, 1)
            act.wait_ge(wt_ps, 1)
            nc.scalar.activation(rawt[:, 0:4, :], tps[:, :, :], ACT.Copy).then_inc(wt_sb, 1)
            nc.scalar.activation(rawt[:, 4, :], tps2[:, :], ACT.Copy).then_inc(wt_sb, 1)
            act.wait_ge(fold_ps, 1)
            nc.scalar.activation(g["f0"][:, :], fps[:, 0, 0:384], ACT.Copy)
            nc.scalar.activation(g["f1"][:, :], fps[:, 1, 0:384], ACT.Copy)
            nc.scalar.activation(g["fe"][:, :], fps[:, 2, 0:256], ACT.Copy)
            nc.scalar.activation(g["fq"][:, 0, :], fps[:, 2, 256:384], ACT.Copy)
            nc.scalar.activation(g["fq"][:, 1, :], fps[:, 2, 384:512], ACT.Copy)
            nc.scalar.activation(g["ebias"][:, :], fps[:, 3, 0:256], ACT.Copy)
            nc.scalar.activation(g["crow"][:, 0, :], fps[0:1, 3, 256:384], ACT.Copy)
            nc.scalar.activation(g["crow"][:, 1, :], fps[0:1, 3, 384:512], ACT.Copy)
            nc.scalar.activation(g["agb2b"][:, :], fps[:, 4, 128:256], ACT.Copy)
            for k in range(2):
                nc.scalar.activation(g["pbias"][:, k:k + 1], fps[:, 4, k:k + 1], ACT.Identity,
                                     bias=cols[:, 5:6]).then_inc(act_done, 1)

        @block.tensor
        def _(pe):
            pe.wait_ge(w_in, 16 * 27)
            pe.wait_ge(const_done, 5)
            for k in range(4):
                nc.tensor.transpose(tps[:, k, :], raw[:, k, :], g["ident"][:, :])
            nc.tensor.transpose(tps2[:, :], raw[:, 4, :], g["ident"][:, :]).then_inc(wt_ps, 1)
            pe.wait_ge(wt_sb, 2)
            pe.wait_ge(col_sb, 3)

            def mm(out, a, b, start=True, stop=True):
                return nc.tensor.matmul(out, a, b, start=start, stop=stop)

            mm(fps[:, 0, 0:384], rawt[:, 0, :], r0[:, :])
            mm(fps[:, 1, 0:384], rawt[:, 1, :], r1[:, :])
            mm(fps[:, 2, 0:256], rawt[:, 2, :], re[:, :])
            mm(fps[:, 2, 256:384], rawt[:, 3, :], r0[:, 256:384])
            mm(fps[:, 2, 384:512], rawt[:, 4, :], r0[:, 256:384])
            for k, (r, b) in enumerate(((r0, 0), (r1, 1))):
                o = fps[:, 3, 128 * k:128 * k + 128]
                mm(o, bcol[:, 2, :], re[:, 128 * k:128 * k + 128], True, False)
                mm(o, bcol[:, b, :], r[:, 0:128], False, False)
                mm(o, bcol[:, b, :], r[:, 128:256], False, False)
                mm(o, ones[0:1, :], rows[:, k, :], False, True)
            for k in range(2):
                mm(fps[0:1, 3, 256 + 128 * k:384 + 128 * k], cols[:, 3 + k:4 + k], r0[:, 256:384])
            mm(fps[:, 4, 0:1], r0[:, 256:384], cols[:, 0:1])
            mm(fps[:, 4, 1:2], r0[:, 256:384], cols[:, 1:2])
            mm(fps[:, 4, 128:256], ones[0:1, :], g["agb2"][0:1, :]).then_inc(fold_ps, 1)
            pe.wait_ge(hist_done, 2 * EC)
            mm(hps[:, 0, 0:NB], lower[:, :], g["run_d"][:, :])
            mm(hps[:, 1, 0:NB], lower[:, :], g["run_s"][:, :])
            pe.wait_ge(act_done, 2)
            mm(fps[:, 0, 0:NB], ones[:, :], g["run_d"][:, :])
            mm(fps[:, 1, 0:NB], ones[:, :], g["run_s"][:, :]).then_inc(hist_ps, 1)

        @block.gpsimd
        def _(pool):
            made = q.sem("made")
            nc.gpsimd.memset(dst_i[:, :], NP - 1).then_inc(idx_clear, 1)
            nc.gpsimd.memset(src_i[:, :], NP - 1).then_inc(idx_clear, 1)
            nc.gpsimd.iota(tmp_i[:, :], pattern=[[1, BLK]], base=0, channel_multiplier=0).then_inc(const_done, 1)
            nc.gpsimd.memset(g["ident"][:, :], 0.0).then_inc(made, 1)
            nc.gpsimd.memset(g["identb"][:, :], 0.0).then_inc(made, 1)
            nc.gpsimd.memset(lower[:, :], 1.0).then_inc(made, 1)
            nc.gpsimd.memset(ones[:, :], 1.0).then_inc(const_done, 1)
            pool.wait_ge(made, 3)
            for m in (g["ident"], g["identb"]):
                nc.gpsimd.affine_select(out=m[:, :], in_=m[:, :], compare_op=ALU.not_equal, fill=1.0, base=0,
                                        pattern=[[-1, P]], channel_multiplier=1).then_inc(const_done, 1)
            nc.gpsimd.affine_select(out=lower[:, :], in_=lower[:, :], compare_op=ALU.is_gt, fill=0.0, base=0,
                                    pattern=[[1, P]], channel_multiplier=-1).then_inc(const_done, 1)
            nc.gpsimd.memset(wide[:, :], 0.0).then_inc(zero_done, 1)
            nc.gpsimd.memset(g["onecol"][:, :], 1.0)
            nc.gpsimd.memset(g["xlast"][:, :, :], 0.0)
            nc.gpsimd.memset(g["ealast"][:, :, :, :], 0.0)
            nc.gpsimd.memset(g["meta_d"][:, :, 3:4], 0)
            nc.gpsimd.memset(g["meta_s"][:, :, 2:4], 0).then_inc(made, 1)
            pool.wait_ge(made, 4)

        @block.vector
        def _(dve):
            v = nc.vector
            n = [0]

            def step(ins):
                n[0] += 1
                ins.then_inc(vec, 1)
                dve.wait_ge(vec, n[0])

            v.memset(g["run_d"][:, :], 0.0)
            v.memset(g["run_s"][:, :], 0.0)
            dve.wait_ge(const_done, 1)
            step(v.tensor_copy(g["iota0"][:, :], tmp_i[:, :]))
            v.tensor_scalar(g["iota1"][:, :], g["iota0"][:, :], 1.0, None, ALU.add)
            step(v.tensor_scalar(g["iota1b"][:, :], g["iota0"][:, :], 1.0, None, ALU.add))
            dve.wait_ge(idx_in, 64)
            work_c = q.sb("work_c", [P, EC], I32)
            for m, own, other, blk in (("meta_d", dst_i, src_i, "blk_d"), ("meta_s", src_i, dst_i, "blk_s")):
                step(v.tensor_scalar(work_c[:, :], own[:, :], BLK.bit_length() - 1, None, ALU.logical_shift_right))
                v.tensor_copy(g[blk][:, :], work_c[:, :])
                v.tensor_copy(g[m][:, :, 0], other[:, :])
                step(v.scalar_tensor_tensor(work_c[:, :], work_c[:, :], float(-BLK), own[:, :], ALU.mult, ALU.add))
                step(v.tensor_scalar(g[m][:, :, 1], work_c[:, :], 1.0, None, ALU.add))
            step(v.tensor_copy(g["meta_d"][:, :, 2], g["meta_d"][:, :, 1]))
            with dve.Fori(0, EC // 4) as m:
                for k in range(4):
                    for j, (run, blk) in enumerate((("run_d", "blk_d"), ("run_s", "blk_s"))):
                        if k > 0:
                            dve.wait_ge(hist_done, m * 8 + k * 2 + j - 1)
                        v.scalar_tensor_tensor(g[run][:, :], g["iota0"][:, 0:NB], g[blk][:, bass.ds(m * 4 + k, 1)],
                                               g[run][:, :], ALU.is_equal, ALU.add).then_inc(hist_done, 1)
                dve.wait_ge(hist_done, m * 8 + 8)
            dve.wait_ge(hist_ps, 1)
            step(v.tensor_copy(work[:, 0, :], fps[:, 0, 0:NB]))
            step(v.tensor_tensor(work_i[:, 0, :], work[:, 0, :], fps[:, 1, 0:NB], ALU.add))
            step(v.tensor_scalar(work_i[:, 1, :], work_i[:, 0, :], 7, None, ALU.logical_shift_right))
            step(v.tensor_scalar(work[:, 1, :], work_i[:, 1, :], 1.0, float(MINCH), ALU.add, ALU.max))
            v.memset(work[:, 3, :], 1.0)
            step(v.memset(work[:, 5, :], 0.0))
            step(v.tensor_tensor_scan(work[:, 2, :], work[:, 3, :], work[:, 1, :], 0.0, ALU.mult, ALU.add))
            step(v.tensor_tensor(work[:, 4, :], work[:, 2, :], work[:, 1, :], ALU.subtract))
            step(v.scalar_tensor_tensor(g["run_d"][:, :], work[:, 4, :], float(P), hps[:, 0, 0:NB], ALU.mult, ALU.add))
            step(v.scalar_tensor_tensor(work[:, 3, :], work[:, 4, :], float(P), hps[:, 1, 0:NB], ALU.mult, ALU.add))
            step(v.tensor_tensor(g["run_s"][:, :], work[:, 3, :], work[:, 0, :], ALU.add))
            step(v.tensor_copy(work_i[:, 2, :], work[:, 2, :]))
            step(v.tensor_scalar(work_i[:, 3, 0:1], work_i[:, 2, NB - 1:NB], float(UNR - 1), None, ALU.add))
            step(v.tensor_scalar(work_i[:, 4, 0:1], work_i[:, 3, 0:1], UNR.bit_length() - 1, None,
                                 ALU.logical_shift_right))
            v.tensor_copy(g["turns"][:, 0:1], work_i[:, 4, 0:1])
            v.tensor_scalar(g["turns"][:, 1:2], work_i[:, 4, 0:1], -1.0, None, ALU.add)
            step(v.tensor_scalar(work_i[:, 2, NB - 1:NB], work_i[:, 4, 0:1], float(UNR), None, ALU.mult))
            v.tensor_copy(g["ends"][:, 1:NB + 1], work_i[:, 2, :])
            v.memset(g["ends"][:, 0:1], 0)
            step(v.tensor_scalar(work_i[:, 5, :], work_i[:, 2, :], float(GRP - 1), None, ALU.add))
            v.memset(g["gends"][:, 0:1], 0)
            step(v.tensor_scalar(g["gends"][:, 1:NB + 1], work_i[:, 5, :], GRP.bit_length() - 1, None,
                                 ALU.logical_shift_right))
            v.tensor_copy(work[:, 5, 0:1], work[:, 4, 0:1]).then_inc(count_done, 1)
            dve.wait_ge(count_done, 1)


def dense_phase(nc, w, g, he, a_tab, br_tab):
    with ExitStack() as ctx:
        q = Pools(nc, ctx)
        x = [q.sb(f"x{s}", [P, 4, P]) for s in range(2)]
        ea = [q.sb(f"ea{s}", [P, 4, FE]) for s in range(2)]
        stats = q.sb("stats", [P, 4, 6])
        mv = q.sb("mv", [P, 4, 2])
        rstd = q.sb("rstd", [P, 2, 4])
        var, std = q.sb("var", [P, 2, 4]), q.sb("std", [P, 2, 4])
        var_done, std_done = q.sem("var_done"), q.sem("std_done")
        shift = q.sb("shift", [P, 2, 4])
        h = q.sb("h", [P, 4, P])
        ht = q.sb("ht", [P, 512])
        eat = q.sb("eat", [FE, 512])
        ret = q.sb("ret", [P, 512])
        a_sb = [q.sb(f"a_sb{s}", [P, 4, P]) for s in range(2)]
        br_sb = [q.sb(f"br_sb{s}", [P, 2, 512]) for s in range(2)]
        rec_d = [q.sb(f"rec_d{s}", [P, 4, REC]) for s in range(2)]
        rec_s = [q.sb(f"rec_s{s}", [P, 4, REC]) for s in range(2)]
        junk = q.sb("junk", [P, 2, NB])
        warm = q.sb("warm", [P, 1])
        posf = q.sb("posf", [P, 8])
        pos = [q.sb(f"pos{s}", [P, 8], I32) for s in range(2)]
        ht_ps = q.ps("ht_ps", [P, 512])
        r1_ps = q.ps("r1_ps", [P, 512])
        eat_ps = q.ps("eat_ps", [FE, 512])
        re_ps = q.ps("re_ps", [P, 512])
        ab_ps = q.ps("ab_ps", [P, 2, 2, 256])
        e_ps = q.ps("e_ps", [P, 2, 2, 256])

        x_in = [q.sem(f"x_in{s}") for s in range(2)]
        ea_in = [q.sem(f"ea_in{s}") for s in range(2)]
        ealast_in = [q.sem(f"ealast_in{s}") for s in range(2)]
        xlast_in = q.sem("xlast_in")
        a_out = [q.sem(f"a_out{s}") for s in range(2)]
        br_out = [q.sem(f"br_out{s}") for s in range(2)]
        sd_out = [q.sem(f"sd_out{s}") for s in range(2)]
        ss_out = [q.sem(f"ss_out{s}") for s in range(2)]
        stats_done, aggr_done, rstd_done = q.sem("stats_done"), q.sem("aggr_done"), q.sem("rstd_done")
        shift_done, norm_done = q.sem("shift_done"), q.sem("norm_done")
        ht_t, ht_c, r1_m, r1_c = q.sem("ht_t"), q.sem("ht_c"), q.sem("r1_m"), q.sem("r1_c")
        eat_t, eat_c, re_m, re_c = q.sem("eat_t"), q.sem("eat_c"), q.sem("re_m"), q.sem("re_c")
        ab_m, ab_c, e_m, e_c = q.sem("ab_m"), q.sem("ab_c"), q.sem("e_m"), q.sem("e_c")
        rank, pos_done, meta_done, recs_done = q.sem("rank"), q.sem("pos_done"), q.sem("meta_done"), q.sem("recs_done")

        x_v = w["x"]
        ea_v = w["ea"][0:(P - 1) * EC, :].rearrange("(p c) f -> p c f", p=P - 1)
        a_v = a_tab.rearrange("(i t p) f -> i p t f", t=4, p=P)
        br_v = br_tab.rearrange("(i k) p f -> i p k f", k=2)
        last_c = EC - (NP - N)
        m_full = last_c // 8
        assert last_c % 8 == 0 and IT % 2 == 0

        def turns(eng, body):
            for s in range(2):
                body(0, s, ea[s], ea_in[s], 1, x[s])
            with eng.Fori(1, m_full) as m:
                for s in range(2):
                    body(m, s, ea[s], ea_in[s], m + 1, x[s])
            with eng.Fori(m_full, IT // 2 - 1) as m:
                for s in range(2):
                    body(m, s, g["ealast"][:, s], ealast_in[s], (m - m_full) * 2 + 2, x[s])
            m = IT // 2 - 1
            for s in range(2):
                body(m, s, g["ealast"][:, s], ealast_in[s], (m - m_full) * 2 + 2, x[s] if s == 0 else g["xlast"])

        block = ctx.enter_context(nc.Block())

        @block.sync
        def _(sp):
            def store(m, s):
                i = m * 2 + s
                sp.wait_ge(ab_c, i * 4 + 4)
                sp.nop(nofuse=True)
                sp.dma_start(a_v[bass.ds(i, 1)].rearrange("a p t f -> (a p) t f"), a_sb[s][:, :, :]).then_inc(a_out[s], 16)
                sp.dma_start(br_v[bass.ds(i, 1)].rearrange("a p k f -> (a p) k f"), br_sb[s][:, :, :]).then_inc(br_out[s], 16)

            def body(m, s, ea_t, ea_sem, _, x_t):
                i = m * 2 + s
                if positive(i * 4 - 4):
                    sp.wait_ge(norm_done, i * 4 - 4)
                    sp.nop(nofuse=True)
                if x_t is x[s]:
                    sp.dma_start(x_t[:, :, :], x_v[bass.ds(i * 512, 512), :].rearrange("(t p) f -> p t f", p=P)).then_inc(x_in[s], 16)
                else:
                    at, part = i * 512, N - i * 512 - 256
                    sp.dma_start(x_t[:, 0:2, :], x_v[at:at + 256, :].rearrange("(t p) f -> p t f", p=P)).then_inc(xlast_in, 16)
                    sp.dma_start(x_t[0:part, 2, :], x_v[at + 256:N, :]).then_inc(xlast_in, 16)
                if positive(i - 1):
                    sp.wait_ge(eat_t, i - 1)
                    sp.nop(nofuse=True)
                if ea_sem is ea_in[s]:
                    sp.dma_start(ea_t[0:P - 1, :, :], ea_v[:, bass.ds(i * 4, 4), :]).then_inc(ea_sem, 16)
                    sp.dma_start(ea_t[P - 1:P, :, :], w["ea"][bass.ds(i * 4 + (P - 1) * EC, 4), :].rearrange("(p c) f -> p c f", p=1)).then_inc(ea_sem, 16)
                else:
                    sp.dma_start(ea_t[0:112, :, :], ea_v[0:112, bass.ds(i * 4, 4), :]).then_inc(ea_sem, 16)
                    sp.dma_start(ea_t[112:P - 1, :, :], ea_v[112:P - 1, bass.ds(i * 4, 4), :]).then_inc(ea_sem, 16)
                if s == 1:
                    store(m, 0)
                elif not (isinstance(m, int) and m == 0):
                    store(m - 1, 1)

            turns(sp, body)
            store(IT // 2 - 1, 1)
            for s in range(2):
                sp.wait_ge(a_out[s], 16 * (IT // 2))
                sp.nop(nofuse=True)
                sp.wait_ge(br_out[s], 16 * (IT // 2))
                sp.nop(nofuse=True)

        @block.scalar
        def _(act):
            nc.scalar.activation(warm[:, :], g["iota0"][:, 0:1], ACT.Sqrt)

            def body(m, s, *_):
                x_t = _[3]
                i = m * 2 + s
                act.wait_ge(var_done, i + 1)
                nc.scalar.activation(std[:, s, :], var[:, s, :], ACT.Sqrt).then_inc(std_done, 1)
                act.wait_ge(shift_done, i + 1)
                if positive(i):
                    act.wait_ge(ht_t, i)
                for t in range(4):
                    nc.scalar.activation(h[:, t, :], x_t[:, t, :], ACT.Relu, bias=shift[:, s, t:t + 1],
                                         scale=rstd[:, s, t:t + 1]).then_inc(norm_done, 1)
                act.wait_ge(ht_t, i + 1)
                nc.scalar.activation(ht[:, :], ht_ps[:, :], ACT.Copy).then_inc(ht_c, 1)
                act.wait_ge(eat_t, i + 1)
                nc.scalar.activation(eat[:, :], eat_ps[:, :], ACT.Copy).then_inc(eat_c, 1)
                act.wait_ge(r1_m, i + 1)
                if positive(m * 16):
                    act.wait_ge(br_out[s], m * 16)
                nc.scalar.activation(br_sb[s][:, :, 256:512], r1_ps[:, :].rearrange("p (k n) -> p k n", k=2),
                                     ACT.Relu, bias=g["ne_b1"][:, 0:1]).then_inc(r1_c, 1)
                act.wait_ge(re_m, i + 1)
                if positive(i * 2):
                    act.wait_ge(e_m, i * 2)
                nc.scalar.activation(ret[:, :], re_ps[:, :], ACT.Relu, bias=g["ee_b1"][:, 0:1]).then_inc(re_c, 1)
                if positive(m * 16):
                    act.wait_ge(a_out[s], m * 16)
                for k in range(2):
                    act.wait_ge(ab_m, i * 2 + k + 1)
                    nc.scalar.activation(a_sb[s][:, 2 * k:2 * k + 2, :], ab_ps[:, k, :, 0:128], ACT.Copy).then_inc(ab_c, 1)
                    nc.scalar.activation(br_sb[s][:, k, 0:256].rearrange("p (h f) -> p h f", h=2),
                                         ab_ps[:, k, :, 128:256], ACT.Copy).then_inc(ab_c, 1)
                act.wait_ge(e_c, i * 4 + 4)
                if positive(m * 64):
                    act.wait_ge(ss_out[s], m * 64)
                for at in (0, E1AT):
                    nc.scalar.activation(rec_s[s][:, :, at:at + 128], rec_d[s][:, :, at:at + 128], ACT.Copy).then_inc(recs_done, 1)

            turns(act, body)

        @block.tensor
        def _(pe):
            def body(m, s, ea_t, ea_sem, ea_n, x_t):
                i = m * 2 + s
                pe.wait_ge(norm_done, i * 4 + 4)
                for t in range(4):
                    last = nc.tensor.transpose(ht_ps[:, t * P:t * P + P], h[:, t, :], g["ident"][:, :])
                last.then_inc(ht_t, 1)
                pe.wait_ge(ea_sem, ea_n * (32 if ea_sem is ea_in[s] else 16))
                pe.nop(nofuse=True)
                for t in range(4):
                    last = nc.tensor.transpose(eat_ps[:, t * P:t * P + P], ea_t[:, t, :], g["ident"][:, :])
                last.then_inc(eat_t, 1)
                pe.wait_ge(ht_c, i + 1)
                nc.tensor.matmul(r1_ps[:, :], g["ne1"][:, :], ht[:, :], start=True, stop=True).then_inc(r1_m, 1)
                pe.wait_ge(eat_c, i + 1)
                nc.tensor.matmul(re_ps[:, :], g["ee1"][:, :], eat[:, :], start=True, stop=True).then_inc(re_m, 1)
                pe.wait_ge(r1_c, i + 1)
                if positive(i * 4):
                    pe.wait_ge(ab_c, i * 4)
                for k in range(2):
                    for hh in range(2):
                        last = nc.tensor.matmul(ab_ps[:, k, hh, :], br_sb[s][:, k, 256 + hh * P:384 + hh * P],
                                                g["f0"][:, 0:256], start=True, stop=True)
                    last.then_inc(ab_m, 1)
                pe.wait_ge(re_c, i + 1)
                if positive(i * 4):
                    pe.wait_ge(e_c, i * 4)
                for k in range(2):
                    for hh in range(2):
                        t = 2 * k + hh
                        last = nc.tensor.matmul(e_ps[:, k, hh, :], ret[:, t * P:t * P + P], g["fe"][:, :],
                                                start=True, stop=True)
                    last.then_inc(e_m, 1)

            turns(pe, body)

        @block.vector
        def _(dve):
            v = nc.vector

            def body(m, s, ea_t, ea_sem, ea_n, x_t):
                i = m * 2 + s
                if x_t is x[s]:
                    dve.wait_ge(x_in[s], m * 16 + 16)
                else:
                    dve.wait_ge(xlast_in, 32)
                if positive(i * 4):
                    dve.wait_ge(aggr_done, i * 4)
                for t in range(4):
                    v.bn_stats(stats[:, t, :], x_t[:, t, :]).then_inc(stats_done, 1)
                dve.wait_ge(stats_done, i * 4 + 4)
                if positive(i):
                    dve.wait_ge(shift_done, i)
                    dve.nop(nofuse=True)
                for t in range(4):
                    v.bn_aggr(mv[:, t, :], stats[:, t, :]).then_inc(aggr_done, 1)
                dve.wait_ge(aggr_done, i * 4 + 4)
                if positive(i * 4 - 4):
                    dve.wait_ge(norm_done, i * 4 - 4)
                v.tensor_scalar(var[:, s, :], mv[:, :, 1], EPS, None, ALU.add).then_inc(var_done, 1)
                dve.wait_ge(std_done, i + 1)
                v.reciprocal(rstd[:, s, :], std[:, s, :]).then_inc(rstd_done, 1)
                dve.wait_ge(rstd_done, i + 1)
                v.scalar_tensor_tensor(shift[:, s, :], mv[:, :, 0], -1.0, rstd[:, s, :], ALU.mult, ALU.mult).then_inc(shift_done, 1)
                if positive(i):
                    dve.wait_ge(pos_done, i)
                for t in range(4):
                    for j, (run, blk) in enumerate((("run_d", "blk_d"), ("run_s", "blk_s"))):
                        if positive(i * 16 + t * 4 + j - 1):
                            dve.wait_ge(rank, i * 16 + t * 4 + j - 1)
                        v.scalar_tensor_tensor(junk[:, j, :], g["iota0"][:, 0:NB], g[blk][:, bass.ds(i * 4 + t, 1)], g[run][:, :],
                                               ALU.is_equal, ALU.mult, accum_out=posf[:, 4 * j + t:4 * j + t + 1]).then_inc(rank, 1)
                    for j, (run, blk) in enumerate((("run_d", "blk_d"), ("run_s", "blk_s"))):
                        v.scalar_tensor_tensor(g[run][:, :], g["iota0"][:, 0:NB], g[blk][:, bass.ds(i * 4 + t, 1)], g[run][:, :],
                                               ALU.is_equal, ALU.add).then_inc(rank, 1)
                if positive(m * 64):
                    dve.wait_ge(sd_out[s], m * 64)
                if positive(m * 64):
                    dve.wait_ge(ss_out[s], m * 64)
                dve.wait_ge(rank, i * 16 + 16)
                v.tensor_copy(pos[s][:, :], posf[:, :]).then_inc(pos_done, 1)
                v.tensor_copy(rec_d[s][:, :, META:META + 4].bitcast(I32), g["meta_d"][:, bass.ds(i * 4, 4), :]).then_inc(meta_done, 1)
                v.tensor_copy(rec_s[s][:, :, META:META + 4].bitcast(I32), g["meta_s"][:, bass.ds(i * 4, 4), :]).then_inc(meta_done, 1)
                for t in range(4):
                    dve.wait_ge(e_m, i * 2 + t // 2 + 1)
                    for at, c in ((0, 0), (E1AT, 128)):
                        ins = v.tensor_tensor(rec_d[s][:, t, at:at + 128], e_ps[:, t // 2, t % 2, c:c + 128],
                                              g["ebias"][:, c:c + 128], ALU.add)
                    ins.then_inc(e_c, 1)

            turns(dve, body)

        @block.gpsimd
        def _(pool):
            def body(m, s, *_):
                i = m * 2 + s
                pool.wait_ge(e_c, i * 4 + 4)
                pool.wait_ge(meta_done, i * 2 + 2)
                pool.nop(nofuse=True)
                for t in range(4):
                    pool.indirect_dma_start(he[:, :], bass.IndirectOffsetOnAxis(ap=pos[s][:, t:t + 1], axis=0),
                                            rec_d[s][:, t, :], None).then_inc(sd_out[s], 16)
                pool.wait_ge(recs_done, i * 2 + 2)
                pool.nop(nofuse=True)
                for t in range(4):
                    pool.indirect_dma_start(he[:, :], bass.IndirectOffsetOnAxis(ap=pos[s][:, 4 + t:5 + t], axis=0),
                                            rec_s[s][:, t, :], None).then_inc(ss_out[s], 16)

            turns(pool, body)
            for s in range(2):
                pool.wait_ge(sd_out[s], 64 * (IT // 2))
                pool.wait_ge(ss_out[s], 64 * (IT // 2))


def edge_phase(nc, g, he, layer, a_tab, br_tab, out_a, out_br, out):
    msgs = layer < 2
    tag = f"l{layer}_"
    with ExitStack() as ctx:
        q = Pools(nc, ctx)
        width = {0: 132, 1: 132, 2: 4}[layer]
        col0 = {0: 0, 1: META, 2: META}[layer]
        meta_at = {0: 128, 1: 0, 2: 0}[layer]
        term_at = {0: 0, 1: 4}.get(layer)
        key = 1 if msgs else 2
        brw = 512 if msgs else 256
        ch = q.sb(tag + "ch", [P, UNR, width])
        nbr = q.sb(tag + "nbr", [P, UNR, P])
        metaf = q.sb(tag + "metaf", [P, UNR, 4])
        ohf = q.sb(tag + "ohf", [P, 4, BLK])
        ohb = q.sb(tag + "ohb", [P, 4, BLK], BF16)
        oht = q.sb(tag + "oht", [P, 2, P])
        pre = q.sb(tag + "pre", [P, 2, P])
        msg = q.sb(tag + "msg", [P, P])
        br = q.sb(tag + "br", [P, 4, brw])
        st = q.sb(tag + "st", [P, BLK])
        deg = q.sb(tag + "deg", [1, BLK])
        rt = q.sb(tag + "rt", [P, BLK])
        ra = q.sb(tag + "ra", [P, 4, 2, P])
        rb = q.sb(tag + "rb", [P, 4, 512])
        oht_ps = q.ps(tag + "oht_ps", [P, 8, P], BF16)
        pre_ps = q.ps(tag + "pre_ps", [P, 2, 512])
        s_ps = q.ps(tag + "s_ps", [P, 512])
        deg_ps = q.ps(tag + "deg_ps", [1, 512])
        r_ps = q.ps(tag + "r_ps", [P, 512])
        o_ps = q.ps(tag + "o_ps", [P, 2, 256])

        def sem(name):
            return q.sem(tag + name)

        ch_in, br_in, res_out = sem("ch_in"), sem("br_in"), sem("res_out")
        res2_out, stored = sem("res2_out"), sem("stored")
        nbr_in = g["nbr_in"]
        metaf_done, oh_done, sum_done, pre_done = sem("metaf_done"), sem("oh_done"), sem("sum_done"), sem("pre_done")
        oht_t, oht_c, look_done, msg_done, s_done = sem("oht_t"), sem("oht_c"), sem("look_done"), sem("msg_done"), sem("s_done")
        st_c, r_m, rt_c, o_m, o_c = sem("st_c"), sem("r_m"), sem("rt_c"), sem("o_m"), sem("o_c")

        used = sum_done if msgs else oh_done
        block = ctx.enter_context(nc.Block())
        he_v = he.rearrange("(c p) f -> p c f", p=P)

        @block.sync
        def _(sp):
            def load_block(b):
                if positive(b * 16):
                    sp.wait_ge(br_in, b * 16)
                    sp.nop(nofuse=True)
                if positive(b - 3):
                    sp.wait_ge(r_m, b - 3)
                    sp.nop(nofuse=True)
                sp.dma_start(br[:, bass.ds(b % 4, 1), :].rearrange("p a f -> p (a f)"),
                             br_tab[bass.ds(b, 1)].rearrange("a p f -> (a p) f")).then_inc(br_in, 16)

            def load_chunks(b):
                first = 0 if isinstance(b, int) and b == 0 else sp.value_load(g["gends"][0:1, bass.ds(b, 1)], min_val=1, max_val=TMAX // GRP - 1)
                end = sp.value_load(g["gends"][0:1, bass.ds(b + 1, 1)], min_val=1, max_val=TMAX // GRP)
                with sp.Fori(first, end) as k:
                    sp.wait_ge(ch_in, k * 16)
                    sp.nop(nofuse=True)
                    sp.wait_ge(used, k * GRP + GRP)
                    sp.nop(nofuse=True)
                    sp.dma_start(ch[:, bass.ds((k % (UNR // GRP)) * GRP, GRP), :],
                                 he_v[:, bass.ds(k * GRP, GRP), col0:col0 + width]).then_inc(ch_in, 16)

            sp.sem_inc(stored, PRIME)

            def store(b):
                sp.wait_ge(o_c, b + 1)
                sp.nop(nofuse=True)
                sp.wait_ge(res_out, b * 16)
                sp.nop(nofuse=True)
                if layer == 0:
                    sp.wait_ge(res2_out, b * 16)
                    sp.nop(nofuse=True)
                sp.sem_inc(stored, 1)
                if msgs:
                    sp.dma_start(out_a.rearrange("(b h p) f -> b p h f", h=2, p=P)[bass.ds(b, 1)].rearrange("a p h f -> (a p) h f"),
                                 ra[:, bass.ds(b % 4, 1), :, :].rearrange("p a h f -> p (a h) f")).then_inc(res_out, 16)
                    if layer == 0:
                        sp.dma_start(out_br[bass.ds(b, 1)].rearrange("a p f -> (a p) f"),
                                     rb[:, bass.ds(b % 4, 1), :].rearrange("p a f -> p (a f)")).then_inc(res2_out, 16)
                else:
                    if isinstance(b, int) and b == NB - 1:
                        rest = N - b * BLK
                        sp.dma_start(out[b * BLK:N, :], ra[0:rest, b % 4, 0, :]).then_inc(res_out, 16)
                    else:
                        sp.dma_start(out[bass.ds(b * BLK, BLK), :].rearrange("(h p) f -> p h f", p=P),
                                     ra[:, bass.ds(b % 4, 1), :, :].rearrange("p a h f -> p (a h) f")).then_inc(res_out, 16)

            for b in range(AHEAD):
                load_block(b)
                load_chunks(b)
            for b in range(2):
                load_block(b + AHEAD)
                load_chunks(b + AHEAD)
            with sp.Fori(2, NB - AHEAD) as b:
                load_block(b + AHEAD)
                load_chunks(b + AHEAD)
                store(b - 2)
            for b in range(NB - AHEAD - 2, NB):
                store(b)
            sp.wait_ge(res_out, 16 * NB)
            sp.nop(nofuse=True)
            if layer == 0:
                sp.wait_ge(res2_out, 16 * NB)
                sp.nop(nofuse=True)

        @block.gpsimd
        def _(pool):
            turns = pool.value_load(g["turns"][0:1, 0:1], min_val=2, max_val=TMAX // UNR)
            free = pre_done if msgs else msg_done

            def turn(k, k_later):
                for j in range(UNR):
                    c = k * UNR + j
                    if j % GRP == 0:
                        pool.wait_ge(ch_in, k * (UNR // GRP * 16) + (j // GRP + 1) * 16)
                        if positive(c - UNR + GRP + PRIME if k_later else 0):
                            pool.wait_ge(free, c - UNR + GRP + PRIME if k_later else 0)
                        pool.nop(nofuse=True)
                    pool.indirect_dma_start(nbr[:, j, :], None, a_tab[:, :], bass.IndirectOffsetOnAxis(
                        ap=ch[:, j, meta_at:meta_at + 1].bitcast(I32), axis=0)).then_inc(nbr_in[j], 16)

            turn(0, False)
            with pool.Fori(1, turns) as k:
                turn(k, True)

        @block.vector
        def _(dve):
            v = nc.vector
            dve.sem_inc(used, UNR)
            if msgs:
                dve.sem_inc(pre_done, PRIME)
            last_turn = dve.value_load(g["turns"][0:1, 1:2], min_val=1, max_val=TMAX // UNR - 1)

            earlier = (last_turn + 1) * layer if layer else 0

            def onehot(k, j):
                c = k * UNR + j
                if j % GRP == 0:
                    dve.wait_ge(ch_in, k * (UNR // GRP * 16) + (j // GRP + 1) * 16)
                    v.tensor_copy(metaf[:, j:j + GRP, :], ch[:, j:j + GRP, meta_at:meta_at + 4].bitcast(I32)).then_inc(metaf_done, 1)
                    dve.wait_ge(metaf_done, k * (UNR // GRP) + j // GRP + 1)
                dve.wait_ge(s_done, c + 1)
                if msgs:
                    v.tensor_scalar(ohb[:, j % 4, :], g["iota1b"][:, :], metaf[:, j, key:key + 1], None, ALU.is_equal)
                else:
                    dve.wait_ge(nbr_in[j], (earlier + k + 1) * 16)
                v.tensor_scalar(ohf[:, j % 4, :], g["iota1"][:, :], metaf[:, j, key:key + 1], None, ALU.is_equal).then_inc(oh_done, 1)
                if msgs:
                    dve.wait_ge(nbr_in[j], (earlier + k + 1) * 16)
                    v.tensor_tensor(nbr[:, j, :], nbr[:, j, :], ch[:, j, term_at:term_at + P], ALU.add).then_inc(sum_done, 1)

            def add_own(k, j):
                c = k * UNR + j
                dve.wait_ge(look_done, c + 1)
                dve.wait_ge(sum_done, c + UNR + 1)
                dve.wait_ge(msg_done, c - 1 + PRIME)
                v.tensor_tensor(pre[:, j % 2, :], pre_ps[:, j % 2, 0:P], nbr[:, j, :], ALU.add).then_inc(pre_done, 1)

            def turn(k, first, last):
                if first and msgs:
                    onehot(0, 0)
                    onehot(0, 1)
                for j in range(UNR):
                    if msgs:
                        if j < UNR - 2:
                            onehot(k, j + 2)
                        elif not last:
                            onehot(k + 1, j + 2 - UNR)
                        add_own(k, j)
                    else:
                        onehot(k, j)

            if msgs:
                turn(0, True, False)
                with dve.Fori(1, last_turn) as k:
                    turn(k, False, False)
                turn(last_turn, False, True)
            else:
                turn(0, True, False)
                with dve.Fori(1, last_turn + 1) as k:
                    turn(k, False, False)

        def bounds(eng, b):
            c0 = 0 if isinstance(b, int) and b == 0 else eng.value_load(g["ends"][0:1, bass.ds(b, 1)], min_val=MINCH, max_val=TMAX - MINCH)
            c1 = eng.value_load(g["ends"][0:1, bass.ds(b + 1, 1)], min_val=MINCH, max_val=TMAX)
            return c0, c1

        @block.tensor
        def _(pe):
            pe.sem_inc(s_done, PRIME)

            def sum_chunk(c, b, start, stop):
                pe.wait_ge(msg_done, c + 1 + PRIME)
                last = nc.tensor.matmul(s_ps[:, 0:BLK], msg[:, :], ohf[:, c % 4, :], start=start, stop=stop)
                if msgs:
                    last = nc.tensor.matmul(deg_ps[0:1, 0:BLK], g["onecol"][:, :], ohb[:, c % 4, :], start=start, stop=stop)
                last.then_inc(s_done, 1)

            def transpose_chunk(c):
                if msgs:
                    pe.wait_ge(oh_done, c + 1)
                    for hh in range(2):
                        last = nc.tensor.transpose(oht_ps[:, hh, :], ohb[:, c % 4, hh * P:hh * P + P], g["identb"][:, :])
                    last.then_inc(oht_t, 1)

            def look_up(c, b):
                if msgs:
                    pe.wait_ge(oht_c, c + 1)
                    pe.wait_ge(pre_done, c - 1 + PRIME)
                    for hh in range(2):
                        last = nc.tensor.matmul(pre_ps[:, c % 2, 0:P], oht[:, hh, :], br[:, b % 4, hh * P:hh * P + P],
                                                start=hh == 0, stop=hh == 1)
                    last.then_inc(look_done, 1)

            def update(b):
                pe.wait_ge(st_c, b + 1)
                pe.wait_ge(br_in, b * 16 + 16)
                if msgs:
                    if positive(b):
                        pe.wait_ge(rt_c, b)
                    nc.tensor.matmul(r_ps[:, 0:BLK], g["fq"][:, layer, :], st[:, :], start=True, stop=False)
                    nc.tensor.matmul(r_ps[:, 0:BLK], g["f0" if layer == 0 else "f1"][:, 256:384], br[:, b % 4, 256:512], start=False, stop=False)
                    nc.tensor.matmul(r_ps[:, 0:BLK], g["crow"][0:1, layer, :], deg[0:1, :], start=False, stop=True).then_inc(r_m, 1)
                else:
                    if positive(b):
                        pe.wait_ge(o_c, b)
                    for hh in range(2):
                        nc.tensor.matmul(o_ps[:, hh, 0:P], st[:, hh * P:hh * P + P], g["ident"][:, :], start=True, stop=False)
                        last = nc.tensor.matmul(o_ps[:, hh, 0:P], g["ident"][:, :], br[:, b % 4, hh * P:hh * P + P], start=False, stop=True)
                    last.then_inc(r_m, 1)

            def project(b):
                if msgs:
                    pe.wait_ge(rt_c, b + 1)
                    pe.wait_ge(o_c, b)
                    for hh in range(2):
                        rhs = g["f1"][:, 0:256] if layer == 0 else g["agw2"][:, :]
                        last = nc.tensor.matmul(o_ps[:, hh, 0:256 if layer == 0 else P], rt[:, hh * P:hh * P + P], rhs, start=True, stop=True)
                    last.then_inc(o_m, 1)

            def one_block(b, prev, prev2):
                c0, c1 = bounds(pe, b)
                pe.wait_ge(br_in, b * 16 + 16)
                transpose_chunk(c0)
                if prev:
                    sum_chunk(c0 - 2, b - 1, False, False)
                look_up(c0, b)
                transpose_chunk(c0 + 1)
                if prev:
                    sum_chunk(c0 - 1, b - 1, False, True)
                look_up(c0 + 1, b)
                if prev2:
                    project(b - 2)
                transpose_chunk(c0 + 2)
                if positive(b):
                    pe.wait_ge(st_c, b)
                sum_chunk(c0, b, True, False)
                look_up(c0 + 2, b)
                with pe.Fori(c0 + 3, c1) as c:
                    transpose_chunk(c)
                    sum_chunk(c - 2, b, False, False)
                    look_up(c, b)
                if prev:
                    update(b - 1)
                return c1

            one_block(0, False, False)
            one_block(1, True, False)
            with pe.Fori(2, NB) as b:
                one_block(b, True, True)
            total = pe.value_load(g["ends"][0:1, NB:NB + 1], min_val=MINCH, max_val=TMAX)
            b = NB - 1
            sum_chunk(total - 2, b, False, False)
            sum_chunk(total - 1, b, False, True)
            project(b - 1)
            update(b)
            project(b)

        @block.scalar
        def _(act):
            act.sem_inc(msg_done, PRIME)
            dummy = q.sb(tag + "dummy", [P, 1])
            nc.scalar.activation(dummy[:, :], g["iota0"][:, 0:1], ACT.Relu)

            def copy_onehot(c):
                if msgs:
                    act.wait_ge(oht_t, c + 1)
                    if positive(c):
                        act.wait_ge(look_done, c)
                    nc.scalar.activation(oht[:, :, :], oht_ps[:, 0:2, :], ACT.Copy).then_inc(oht_c, 1)

            def message(c):
                if isinstance(c, int) and c < 0:
                    return
                act.wait_ge(s_done, c + PRIME)
                if msgs:
                    act.wait_ge(pre_done, c + 1 + PRIME)
                    nc.scalar.activation(msg[:, :], pre[:, bass.ds(c % 2, 1), :].rearrange("p a f -> p (a f)"), ACT.Relu).then_inc(msg_done, 1)
                else:
                    act.wait_ge(oh_done, c + 1 + UNR)
                    nc.scalar.activation(msg[:, :], nbr[:, bass.ds(c % UNR, 1), :].rearrange("p a f -> p (a f)"), ACT.Copy).then_inc(msg_done, 1)

            def copy_sums(b, c0):
                act.wait_ge(s_done, c0 + PRIME)
                if positive(b):
                    act.wait_ge(r_m, b)
                last = nc.scalar.activation(st[:, :], s_ps[:, 0:BLK], ACT.Copy)
                if msgs:
                    last = nc.scalar.activation(deg[:, :], deg_ps[0:1, 0:BLK], ACT.Copy)
                last.then_inc(st_c, 1)

            def copy_out(b):
                act.wait_ge(o_m if msgs else r_m, b + 1)
                act.wait_ge(stored, b - 2 + PRIME)
                row = ra[:, bass.ds(b % 4, 1), :, :].rearrange("p a h f -> p (a h) f")
                ins = nc.scalar.activation(row, o_ps[:, :, 0:P], ACT.Copy)
                if layer == 0:
                    ins = nc.scalar.activation(rb[:, bass.ds(b % 4, 1), 0:256].rearrange("p a (h f) -> p (a h) f", h=2),
                                               o_ps[:, :, P:256], ACT.Copy)
                    ins = nc.scalar.activation(rb[:, bass.ds(b % 4, 1), 256:512].rearrange("p a f -> p (a f)"), rt[:, :], ACT.Copy)
                ins.then_inc(o_c, 1)

            def relu_nodes(b):
                if msgs:
                    act.wait_ge(r_m, b + 1)
                    if positive(b):
                        act.wait_ge(o_c, b)
                    nc.scalar.activation(rt[:, :], r_ps[:, 0:BLK], ACT.Relu, bias=g["pbias"][:, layer:layer + 1]).then_inc(rt_c, 1)
                    act.wait_ge(rt_c, b + 1)

            def one_block(b, prev, prev2):
                c0, c1 = bounds(act, b)
                copy_onehot(c0)
                message(c0 - 1)
                copy_onehot(c0 + 1)
                message(c0)
                if prev:
                    copy_sums(b - 1, c0)
                if prev2:
                    copy_out(b - 2) if msgs else None
                copy_onehot(c0 + 2)
                message(c0 + 1)
                with act.Fori(c0 + 3, c1) as c:
                    copy_onehot(c)
                    message(c - 1)
                if prev:
                    relu_nodes(b - 1) if msgs else copy_out(b - 1)

            one_block(0, False, False)
            one_block(1, True, False)
            with act.Fori(2, NB) as b:
                one_block(b, True, True)
            total = act.value_load(g["ends"][0:1, NB:NB + 1], min_val=MINCH, max_val=TMAX)
            b = NB - 1
            message(total - 1)
            copy_sums(b, total)
            if msgs:
                copy_out(b - 1)
                relu_nodes(b)
            copy_out(b)


def norm_phase(nc, w, g, y_tab, h_tab, xh_tab):
    with ExitStack() as ctx:
        q = Pools(nc, ctx)
        x = [q.sb(f"nx{s}", [P, 4, P]) for s in range(2)]
        y = [q.sb(f"ny{s}", [P, 4, P]) for s in range(2)]
        x1 = [q.sb(f"nx1{s}", [P, 4, P]) for s in range(2)]
        h = [q.sb(f"nh{s}", [P, 4, P]) for s in range(2)]
        xh = [q.sb(f"nxh{s}", [P, 4, P]) for s in range(2)]
        stats = q.sb("nstats", [P, 4, 6])
        mv = q.sb("nmv", [P, 4, 2])
        rstd = q.sb("nrstd", [P, 2, 4])
        var, std = q.sb("nvar", [P, 2, 4]), q.sb("nstd", [P, 2, 4])
        var_done, std_done = q.sem("nvar_done"), q.sem("nstd_done")
        shift = q.sb("nshift", [P, 2, 4])
        dummy = q.sb("ndummy", [P, 1])
        x_in = [q.sem(f"nx_in{s}") for s in range(2)]
        y_in = [q.sem(f"ny_in{s}") for s in range(2)]
        h_out = [q.sem(f"nh_out{s}") for s in range(2)]
        xh_out = [q.sem(f"nxh_out{s}") for s in range(2)]
        sum_done, bias_done, stats_done, aggr_done = q.sem("nsum"), q.sem("nbias"), q.sem("nstats_done"), q.sem("naggr")
        rstd_done, shift_done, norm_done, xh_done = q.sem("nrstd_done"), q.sem("nshift_done"), q.sem("nnorm"), q.sem("nxh_done")
        h_v = h_tab.rearrange("(i t p) f -> i p t f", t=4, p=P)
        y_v = y_tab.rearrange("(i t p) f -> i p t f", t=4, p=P)
        xh_v = xh_tab.rearrange("(i k) p (h f) -> i p k h f", k=2, h=2)

        def turns(eng, body):
            for s in range(2):
                body(0, s, x[s])
            with eng.Fori(1, IT // 2 - 1) as m:
                for s in range(2):
                    body(m, s, x[s])
            for s in range(2):
                body(IT // 2 - 1, s, x[s] if s == 0 else g["xlast"])

        block = ctx.enter_context(nc.Block())

        @block.sync
        def _(sp):
            def store(m, s):
                i = m * 2 + s
                sp.wait_ge(xh_done, i + 1)
                sp.nop(nofuse=True)
                sp.dma_start(h_v[bass.ds(i, 1)].rearrange("a p t f -> (a p) t f"), h[s][:, :, :]).then_inc(h_out[s], 16)
                sp.dma_start(xh_v[bass.ds(i, 1)].rearrange("a p k h f -> (a p) k (h f)"),
                             xh[s][:, :, :].rearrange("p (k h) f -> p k (h f)", k=2)).then_inc(xh_out[s], 16)

            def body(m, s, x_t):
                i = m * 2 + s
                if positive(i - 1):
                    sp.wait_ge(sum_done, i - 1)
                    sp.nop(nofuse=True)
                sp.dma_start(y[s][:, :, :], y_v[bass.ds(i, 1)].rearrange("a p t f -> (a p) t f")).then_inc(y_in[s], 16)
                if x_t is x[s]:
                    sp.dma_start(x_t[:, :, :], w["x"][bass.ds(i * 512, 512), :].rearrange("(t p) f -> p t f", p=P)).then_inc(x_in[s], 16)
                if s == 1:
                    store(m, 0)
                elif not (isinstance(m, int) and m == 0):
                    store(m - 1, 1)

            turns(sp, body)
            store(IT // 2 - 1, 1)
            for s in range(2):
                sp.wait_ge(h_out[s], 16 * (IT // 2))
                sp.nop(nofuse=True)
                sp.wait_ge(xh_out[s], 16 * (IT // 2))
                sp.nop(nofuse=True)

        @block.vector
        def _(dve):
            v = nc.vector

            def body(m, s, x_t):
                i = m * 2 + s
                dve.wait_ge(y_in[s], m * 16 + 16)
                if x_t is x[s]:
                    dve.wait_ge(x_in[s], m * 16 + 16)
                if positive(i * 4 - 4):
                    dve.wait_ge(norm_done, i * 4 - 4)
                v.tensor_tensor(x1[s][:, :, :], x_t[:, :, :], y[s][:, :, :], ALU.add).then_inc(sum_done, 1)
                dve.wait_ge(sum_done, i + 1)
                for t in range(4):
                    v.tensor_tensor(x1[s][:, t, :], x1[s][:, t, :], g["agb2b"][:, :], ALU.add).then_inc(bias_done, 1)
                dve.wait_ge(bias_done, i * 4 + 4)
                for t in range(4):
                    v.bn_stats(stats[:, t, :], x1[s][:, t, :]).then_inc(stats_done, 1)
                dve.wait_ge(stats_done, i * 4 + 4)
                dve.nop(nofuse=True)
                for t in range(4):
                    v.bn_aggr(mv[:, t, :], stats[:, t, :]).then_inc(aggr_done, 1)
                dve.wait_ge(aggr_done, i * 4 + 4)
                v.tensor_scalar(var[:, s, :], mv[:, :, 1], EPS, None, ALU.add).then_inc(var_done, 1)
                dve.wait_ge(std_done, i + 1)
                v.reciprocal(rstd[:, s, :], std[:, s, :]).then_inc(rstd_done, 1)
                dve.wait_ge(rstd_done, i + 1)
                v.scalar_tensor_tensor(shift[:, s, :], mv[:, :, 0], -1.0, rstd[:, s, :], ALU.mult, ALU.mult).then_inc(shift_done, 1)
                dve.wait_ge(shift_done, i + 1)
                if not (isinstance(i, int) and i == 0):
                    add(m if s == 1 else m - 1, 1 - s)

            def add(m, s):
                i = m * 2 + s
                dve.wait_ge(norm_done, i * 4 + 4)
                if positive(m * 16):
                    dve.wait_ge(xh_out[s], m * 16)
                v.tensor_tensor(xh[s][:, :, :], x1[s][:, :, :], h[s][:, :, :], ALU.add).then_inc(xh_done, 1)

            turns(dve, body)
            add(IT // 2 - 1, 1)

        @block.scalar
        def _(act):
            nc.scalar.activation(dummy[:, :], g["iota0"][:, 0:1], ACT.Sqrt)

            def body(m, s, x_t):
                i = m * 2 + s
                act.wait_ge(var_done, i + 1)
                nc.scalar.activation(std[:, s, :], var[:, s, :], ACT.Sqrt).then_inc(std_done, 1)
                act.wait_ge(shift_done, i + 1)
                if positive(i - 1):
                    act.wait_ge(xh_done, i - 1)
                if positive(m * 16):
                    act.wait_ge(h_out[s], m * 16)
                for t in range(4):
                    nc.scalar.activation(h[s][:, t, :], x1[s][:, t, :], ACT.Relu, bias=shift[:, s, t:t + 1],
                                         scale=rstd[:, s, t:t + 1]).then_inc(norm_done, 1)

            turns(act, body)


def gnn_program(nc, w, out):
    def dram(name, shape, dt=FP32):
        return nc.dram_tensor(name, shape, dt).ap()

    he = dram("he", [TMAX * P, REC])
    a0, a1 = dram("a0", [NP, P]), dram("a1", [NP, P])
    br0, br1 = dram("br0", [NB, P, 512]), dram("br1", [NB, P, 512])
    y_tab, h_tab, xh_tab = dram("y_tab", [NP, P]), dram("h_tab", [NP, P]), dram("xh_tab", [NB, P, 256])
    with ExitStack() as ctx:
        q = Pools(nc, ctx)
        g = {
            "ne1": q.sb("ne1", [P, P]), "ee1": q.sb("ee1", [FE, P]), "agw2": q.sb("agw2", [P, P]),
            "ne_b1": q.sb("ne_b1", [P, 1]), "ee_b1": q.sb("ee_b1", [P, 1]),
            "agb2": q.sb("agb2", [1, P]), "agb2b": q.sb("agb2b", [P, P]),
            "f0": q.sb("f0", [P, 384]), "f1": q.sb("f1", [P, 384]), "fe": q.sb("fe", [P, 256]),
            "fq": q.sb("fq", [P, 2, P]), "ebias": q.sb("ebias", [P, 256]), "crow": q.sb("crow", [1, 2, P]),
            "pbias": q.sb("pbias", [P, 2]),
            "ident": q.sb("ident", [P, P]), "identb": q.sb("identb", [P, P], BF16), "onecol": q.sb("onecol", [P, 1], BF16),
            "iota0": q.sb("iota0", [P, BLK]), "iota1": q.sb("iota1", [P, BLK]), "iota1b": q.sb("iota1b", [P, BLK], BF16),
            "xlast": q.sb("xlast", [P, 4, P]), "ealast": q.sb("ealast", [P, 2, 4, FE]),
            "meta_d": q.sb("meta_d", [P, EC, 4], I32), "meta_s": q.sb("meta_s", [P, EC, 4], I32),
            "blk_d": q.sb("blk_d", [P, EC]), "blk_s": q.sb("blk_s", [P, EC]),
            "run_d": q.sb("run_d", [P, NB]), "run_s": q.sb("run_s", [P, NB]),
            "ends": q.sb("ends", [P, NB + 1], I32), "gends": q.sb("gends", [P, NB + 1], I32),
            "nbr_in": [q.sem(f"nbr_in{j}") for j in range(UNR)],
            "turns": q.sb("turns", [P, 2], I32),
        }
        setup_phase(nc, w, g, he)
        dense_phase(nc, w, g, he, a0, br0)
        edge_phase(nc, g, he, 0, a0, br0, a1, br1, None)
        edge_phase(nc, g, he, 1, a1, br1, y_tab, None, None)
        norm_phase(nc, w, g, y_tab, h_tab, xh_tab)
        edge_phase(nc, g, he, 2, h_tab, xh_tab, None, None, out)


_INS = {"x": "x", "src": "src", "dst": "dst", "ea": "edge_attr_64"}
_INS.update({k: "L0_gnn_" + k for k in (
    "ne_w1", "ne_b1", "ne_w2", "ne_b2", "ee_w1", "ee_b1", "ee_w2", "ee_b2", "ml_w1", "ml_b1", "ml_w2", "ml_b2",
    "agg_w1", "agg_b1", "agg_w2", "agg_b2")})


def kernel(**inputs):
    import numpy as _np
    import concourse.bacc as _bacc
    from concourse import mybir as _mybir
    from concourse.bass_utils import run_bass_kernel_spmd as _run

    nc = _bacc.Bacc("TRN2", target_bir_lowering=False, num_devices=1)
    arrays, w = {}, {}
    for short, name in _INS.items():
        a = _np.ascontiguousarray(inputs[name])
        arrays[f"in_{name}"] = a
        w[short] = nc.dram_tensor(f"in_{name}", a.shape, _mybir.dt.from_np(a.dtype), kind="ExternalInput").ap()
    out = nc.dram_tensor("out_0", [N, P], _mybir.dt.float32, kind="ExternalOutput").ap()
    gnn_program(nc, w, out)
    r = _run(nc, [arrays], core_ids=[0])
    return r.results[0]["out_0"]
```

```python
import concourse.bass as bass
from concourse import mybir
from contextlib import ExitStack

FP32 = mybir.dt.float32
BF16 = mybir.dt.bfloat16
I32 = mybir.dt.int32
ALU = mybir.AluOpType
ACT = mybir.ActivationFunctionType

P = 128
N = 50000
FE = 64
SUB = 128
BLK = 2 * SUB
NB = -(-N // BLK)
NS = 2 * NB
NP = NB * BLK
EC = NP // P
IT = NP // (4 * P)
GRP = 4
UNR = 16
PAIRS = UNR // 2
TMAX = -(-(2 * NP // P + 2 * NS) // UNR) * UNR
BITS = (TMAX // 2).bit_length()
REC = 260
META = 128
E1AT = 132
PRIME = 4
AHEAD = 2
EPS = 1e-5


def positive(count):
    return not isinstance(count, int) or count > 0




class Pools:

    def __init__(self, nc, ctx):
        self.nc, self.ctx = nc, ctx

    def sb(self, name, shape, dt=FP32):
        return self.ctx.enter_context(self.nc.sbuf_tensor(name, shape, dt))

    def ps(self, name, shape, dt=FP32):
        return self.ctx.enter_context(self.nc.psum_tensor(name, shape, dt))

    def sem(self, name):
        return self.ctx.enter_context(self.nc.semaphore(name))


def setup_phase(nc, w, g, he):
    with ExitStack() as ctx:
        q = Pools(nc, ctx)
        src_i = q.sb("src_i", [P, EC], I32)
        dst_i = q.sb("dst_i", [P, EC], I32)
        wide = q.sb("wide", [P, UNR * REC])
        tmp_i = q.sb("tmp_i", [P, NS], I32)
        lower = q.sb("lower", [P, P])
        ones = q.sb("ones", [P, P])
        r0 = q.sb("r0", [P, 384])
        r1 = q.sb("r1", [P, 384])
        re = q.sb("re", [P, 256])
        raw = q.sb("raw", [P, 5, P])
        rawt = q.sb("rawt", [P, 5, P])
        cols = q.sb("cols", [P, 6])
        bcol = q.sb("bcol", [P, 3, P])
        rows = q.sb("rows", [1, 2, P])
        work = q.sb("work", [P, 6, NS])
        work_i = q.sb("work_i", [P, 6, NS], I32)
        tps = q.ps("tps", [P, 4, P])
        fps = q.ps("fps", [P, 5, 512])
        tps2 = fps[:, 4, 256:384]
        hps = q.ps("hps", [P, 2, 512])

        idx_clear, idx_in = q.sem("idx_clear"), q.sem("idx_in")
        w_in, const_done = q.sem("w_in"), q.sem("const_done")
        vec, act_done = q.sem("vec"), q.sem("act_done")
        wt_ps, wt_sb, fold_ps, col_sb = q.sem("wt_ps"), q.sem("wt_sb"), q.sem("fold_ps"), q.sem("col_sb")
        hist_done, hist_ps = q.sem("hist_done"), q.sem("hist_ps")
        zero_done, count_done, he_zeroed = q.sem("zero_done"), q.sem("count_done"), q.sem("he_zeroed")
        tail = NP - N
        full_p = P - 1
        last_c = EC - tail
        block = ctx.enter_context(nc.Block())

        @block.sync
        def _(sp):
            sp.wait_ge(idx_clear, 2)
            sp.nop(nofuse=True)
            for t, a in ((dst_i, w["dst"]), (src_i, w["src"])):
                sp.dma_start(t[0:full_p, :], a[0:full_p * EC].rearrange("(p c) -> p c", p=full_p)).then_inc(idx_in, 16)
                sp.dma_start(t[full_p:P, 0:last_c],
                             a[full_p * EC:N].rearrange("(p c) -> p c", p=1)).then_inc(idx_in, 16)
            sp.wait_ge(count_done, 1)
            sp.nop(nofuse=True)
            turns = sp.value_load(g["turns"][0:1, 0:1], min_val=1, max_val=TMAX // UNR)
            sp.wait_ge(zero_done, 1)
            sp.nop(nofuse=True)
            with sp.Fori(0, turns) as k:
                sp.dma_start(he[bass.ds(k * (UNR * P), UNR * P), :].rearrange("(p r) f -> p (r f)", p=P),
                             wide[:, :]).then_inc(he_zeroed, 16)
            sp.wait_ge(he_zeroed, turns * 16)
            sp.nop(nofuse=True)

        @block.scalar
        def _(act):
            loads = [(g["ne1"][:, :], w["ne_w1"]), (g["ee1"][:, :], w["ee_w1"]), (g["agw2"][:, :], w["agg_w2"]),
                     (r0[:, 0:128], w["ml_w1"][0, 0:128, :]), (r0[:, 128:256], w["ml_w1"][0, 256:384, :]),
                     (r0[:, 256:384], w["agg_w1"]),
                     (r1[:, 0:128], w["ml_w1"][1, 0:128, :]), (r1[:, 128:256], w["ml_w1"][1, 256:384, :]),
                     (r1[:, 256:384], w["agg_w1"]),
                     (re[:, 0:128], w["ml_w1"][0, 128:256, :]), (re[:, 128:256], w["ml_w1"][1, 128:256, :]),
                     (raw[:, 0, :], w["ne_w2"]), (raw[:, 1, :], w["agg_w2"]), (raw[:, 2, :], w["ee_w2"]),
                     (raw[:, 3, :], w["ml_w2"][0]), (raw[:, 4, :], w["ml_w2"][1])]
            columns = [w["ne_b2"], w["agg_b2"], w["ee_b2"], w["ml_b2"][0], w["ml_b2"][1], w["agg_b1"]]
            loads += [(cols[:, k:k + 1], c.rearrange("(p a) -> p a", a=1)) for k, c in enumerate(columns)]
            loads += [(g["ne_b1"][:, :], w["ne_b1"].rearrange("(p a) -> p a", a=1)),
                      (g["ee_b1"][:, :], w["ee_b1"].rearrange("(p a) -> p a", a=1)),
                      (rows[:, 0, :], w["ml_b1"][0:1, :]), (rows[:, 1, :], w["ml_b1"][1:2, :]),
                      (g["agb2"][0:1, :], w["agg_b2"].rearrange("(a n) -> a n", a=1))]
            for to, frm in loads:
                act.dma_start(to, frm).then_inc(w_in, 16)
            act.wait_ge(w_in, 16 * len(loads))
            act.wait_ge(const_done, 5)
            for k in range(3):
                nc.scalar.activation(bcol[:, k, :], ones[:, :], ACT.Copy, scale=cols[:, k:k + 1]).then_inc(col_sb, 1)
            act.wait_ge(wt_ps, 1)
            nc.scalar.activation(rawt[:, 0:4, :], tps[:, :, :], ACT.Copy).then_inc(wt_sb, 1)
            nc.scalar.activation(rawt[:, 4, :], tps2, ACT.Copy).then_inc(wt_sb, 1)
            act.wait_ge(fold_ps, 1)
            nc.scalar.activation(g["f0"][:, :], fps[:, 0, 0:384], ACT.Copy)
            nc.scalar.activation(g["f1"][:, :], fps[:, 1, 0:384], ACT.Copy)
            nc.scalar.activation(g["fe"][:, :], fps[:, 2, 0:256], ACT.Copy)
            nc.scalar.activation(g["fq"][:, 0, :], fps[:, 2, 256:384], ACT.Copy)
            nc.scalar.activation(g["fq"][:, 1, :], fps[:, 2, 384:512], ACT.Copy)
            nc.scalar.activation(g["ebias"][:, :], fps[:, 3, 0:256], ACT.Copy)
            nc.scalar.activation(g["crow"][:, 0, :], fps[0:1, 3, 256:384], ACT.Copy)
            nc.scalar.activation(g["crow"][:, 1, :], fps[0:1, 3, 384:512], ACT.Copy)
            for t in range(4):
                nc.scalar.activation(g["agb2b"][:, t, :], fps[:, 4, 128:256], ACT.Copy)
            for k in range(2):
                nc.scalar.activation(g["pbias"][:, k:k + 1], fps[:, 4, k:k + 1], ACT.Identity,
                                     bias=cols[:, 5:6]).then_inc(act_done, 1)

        @block.tensor
        def _(pe):
            pe.wait_ge(w_in, 16 * 27)
            pe.wait_ge(const_done, 5)
            for k in range(4):
                nc.tensor.transpose(tps[:, k, :], raw[:, k, :], g["ident"][:, :])
            nc.tensor.transpose(tps2, raw[:, 4, :], g["ident"][:, :]).then_inc(wt_ps, 1)
            pe.wait_ge(wt_sb, 2)
            pe.wait_ge(col_sb, 3)

            def mm(out, a, b, start=True, stop=True):
                return nc.tensor.matmul(out, a, b, start=start, stop=stop)

            mm(fps[:, 0, 0:384], rawt[:, 0, :], r0[:, :])
            mm(fps[:, 1, 0:384], rawt[:, 1, :], r1[:, :])
            mm(fps[:, 2, 0:256], rawt[:, 2, :], re[:, :])
            mm(fps[:, 2, 256:384], rawt[:, 3, :], r0[:, 256:384])
            mm(fps[:, 2, 384:512], rawt[:, 4, :], r0[:, 256:384])
            for k, (r, b) in enumerate(((r0, 0), (r1, 1))):
                o = fps[:, 3, 128 * k:128 * k + 128]
                mm(o, bcol[:, 2, :], re[:, 128 * k:128 * k + 128], True, False)
                mm(o, bcol[:, b, :], r[:, 0:128], False, False)
                mm(o, bcol[:, b, :], r[:, 128:256], False, False)
                mm(o, ones[0:1, :], rows[:, k, :], False, True)
            for k in range(2):
                mm(fps[0:1, 3, 256 + 128 * k:384 + 128 * k], cols[:, 3 + k:4 + k], r0[:, 256:384])
            mm(fps[:, 4, 0:1], r0[:, 256:384], cols[:, 0:1])
            mm(fps[:, 4, 1:2], r0[:, 256:384], cols[:, 1:2])
            mm(fps[:, 4, 128:256], ones[0:1, :], g["agb2"][0:1, :]).then_inc(fold_ps, 1)
            pe.wait_ge(hist_done, 2 * EC)
            mm(hps[:, 0, 0:NS], lower[:, :], g["run_d"][:, :])
            mm(hps[:, 1, 0:NS], lower[:, :], g["run_s"][:, :])
            pe.wait_ge(act_done, 2)
            mm(fps[:, 0, 0:NS], ones[:, :], g["run_d"][:, :])
            mm(fps[:, 1, 0:NS], ones[:, :], g["run_s"][:, :]).then_inc(hist_ps, 1)

        @block.gpsimd
        def _(pool):
            made = q.sem("made")
            nc.gpsimd.memset(dst_i[:, :], NP - 1).then_inc(idx_clear, 1)
            nc.gpsimd.memset(src_i[:, :], NP - 1).then_inc(idx_clear, 1)
            nc.gpsimd.iota(tmp_i[:, :], pattern=[[1, NS]], base=0, channel_multiplier=0).then_inc(const_done, 1)
            nc.gpsimd.memset(g["ident"][:, :], 0.0).then_inc(made, 1)
            nc.gpsimd.memset(g["identb"][:, :], 0.0).then_inc(made, 1)
            nc.gpsimd.memset(lower[:, :], 1.0).then_inc(made, 1)
            nc.gpsimd.memset(ones[:, :], 1.0).then_inc(const_done, 1)
            pool.wait_ge(made, 3)
            for m in (g["ident"], g["identb"]):
                nc.gpsimd.affine_select(out=m[:, :], in_=m[:, :], compare_op=ALU.not_equal, fill=1.0, base=0,
                                        pattern=[[-1, P]], channel_multiplier=1).then_inc(const_done, 1)
            nc.gpsimd.affine_select(out=lower[:, :], in_=lower[:, :], compare_op=ALU.is_gt, fill=0.0, base=0,
                                    pattern=[[1, P]], channel_multiplier=-1).then_inc(const_done, 1)
            nc.gpsimd.memset(wide[:, :], 0.0).then_inc(zero_done, 1)
            nc.gpsimd.memset(g["onecol"][:, :], 1.0)
            nc.gpsimd.memset(g["zrow"][:, :], 0.0)
            nc.gpsimd.memset(g["xlast"][:, :, :], 0.0)
            nc.gpsimd.memset(g["ealast"][:, :, :, :], 0.0)
            nc.gpsimd.memset(g["meta_d"][:, :, 3:4], 0)
            nc.gpsimd.memset(g["meta_s"][:, :, 2:4], 0).then_inc(made, 1)
            pool.wait_ge(made, 4)

        @block.vector
        def _(dve):
            v = nc.vector
            n = [0]

            def step(ins):
                n[0] += 1
                ins.then_inc(vec, 1)
                dve.wait_ge(vec, n[0])

            v.memset(g["run_d"][:, :], 0.0)
            v.memset(g["run_s"][:, :], 0.0)
            dve.wait_ge(const_done, 1)
            step(v.tensor_copy(g["iota0"][:, :], tmp_i[:, :]))
            v.tensor_scalar(g["iota1"][:, :], g["iota0"][:, 0:SUB], 1.0, None, ALU.add)
            step(v.tensor_scalar(g["iota1b"][:, :], g["iota0"][:, 0:SUB], 1.0, None, ALU.add))
            dve.wait_ge(idx_in, 64)
            work_c = q.sb("work_c", [P, EC], I32)
            for m, own, other, blk in (("meta_d", dst_i, src_i, "blk_d"), ("meta_s", src_i, dst_i, "blk_s")):
                step(v.tensor_scalar(work_c[:, :], own[:, :], SUB.bit_length() - 1, None, ALU.logical_shift_right))
                v.tensor_copy(g[blk][:, :], work_c[:, :])
                v.tensor_copy(g[m][:, :, 0], other[:, :])
                step(v.scalar_tensor_tensor(work_c[:, :], work_c[:, :], float(-SUB), own[:, :], ALU.mult, ALU.add))
                step(v.tensor_scalar(g[m][:, :, 1], work_c[:, :], 1.0, None, ALU.add))
            step(v.tensor_copy(g["meta_d"][:, :, 2], g["meta_d"][:, :, 1]))
            with dve.Fori(0, EC // 4) as m:
                for k in range(4):
                    for j, (run, blk) in enumerate((("run_d", "blk_d"), ("run_s", "blk_s"))):
                        if k > 0:
                            dve.wait_ge(hist_done, m * 8 + k * 2 + j - 1)
                        v.scalar_tensor_tensor(g[run][:, :], g["iota0"][:, :], g[blk][:, bass.ds(m * 4 + k, 1)],
                                               g[run][:, :], ALU.is_equal, ALU.add).then_inc(hist_done, 1)
                dve.wait_ge(hist_done, m * 8 + 8)
            dve.wait_ge(hist_ps, 1)
            step(v.tensor_copy(work[:, 0, :], fps[:, 0, 0:NS]))
            step(v.tensor_tensor(work_i[:, 0, :], work[:, 0, :], fps[:, 1, 0:NS], ALU.add))
            step(v.tensor_scalar(work_i[:, 1, :], work_i[:, 0, :], 8, None, ALU.logical_shift_right))
            step(v.tensor_scalar(work[:, 1, :], work_i[:, 1, :], 1.0, None, ALU.add))
            v.memset(work[:, 3, :], 1.0)
            step(v.memset(work[:, 5, :], 0.0))
            step(v.tensor_tensor_scan(work[:, 2, :], work[:, 3, :], work[:, 1, :], 0.0, ALU.mult, ALU.add))
            step(v.tensor_tensor(work[:, 4, :], work[:, 2, :], work[:, 1, :], ALU.subtract))
            step(v.scalar_tensor_tensor(g["run_d"][:, :], work[:, 4, :], float(2 * P), hps[:, 0, 0:NS], ALU.mult, ALU.add))
            step(v.scalar_tensor_tensor(work[:, 3, :], work[:, 4, :], float(2 * P), hps[:, 1, 0:NS], ALU.mult, ALU.add))
            step(v.tensor_tensor(g["run_s"][:, :], work[:, 3, :], work[:, 0, :], ALU.add))
            step(v.tensor_copy(work_i[:, 2, :], work[:, 2, :]))
            step(v.tensor_scalar(work_i[:, 3, 0:1], work_i[:, 2, NS - 1:NS], float(PAIRS - 1), None, ALU.add))
            step(v.tensor_scalar(work_i[:, 4, 0:1], work_i[:, 3, 0:1], PAIRS.bit_length() - 1, None,
                                 ALU.logical_shift_right))
            v.tensor_copy(g["turns"][:, 0:1], work_i[:, 4, 0:1])
            v.tensor_scalar(g["turns"][:, 1:2], work_i[:, 4, 0:1], -1.0, None, ALU.add)
            step(v.tensor_scalar(work_i[:, 2, NS - 1:NS], work_i[:, 4, 0:1], float(PAIRS), None, ALU.mult))
            v.tensor_copy(g["ends"][:, 1:NS + 1], work_i[:, 2, :])
            step(v.memset(g["ends"][:, 0:1], 0))
            step(v.tensor_scalar(work_i[:, 5, 0:NB], work_i[:, 2, 1:NS:2], float(GRP // 2 - 1), None, ALU.add))
            v.memset(g["gends"][:, 0:1], 0)
            step(v.tensor_scalar(g["gends"][:, 1:NB + 1], work_i[:, 5, 0:NB], (GRP // 2).bit_length() - 1, None,
                                 ALU.logical_shift_right))
            step(v.tensor_scalar(work_i[:, 0, 0:NB], g["ends"][:, 1:NS:2], BITS, None, ALU.logical_shift_left))
            step(v.tensor_scalar(work_i[:, 1, 0:NB], g["ends"][:, 2:NS + 1:2], 2 * BITS, None, ALU.logical_shift_left))
            step(v.tensor_tensor(work_i[:, 3, 0:NB], work_i[:, 0, 0:NB], work_i[:, 1, 0:NB], ALU.bitwise_or))
            step(v.tensor_tensor(g["bounds"][:, :], work_i[:, 3, 0:NB], g["ends"][:, 0:NS:2], ALU.bitwise_or))
            v.tensor_copy(work[:, 5, 0:1], work[:, 4, 0:1]).then_inc(count_done, 1)
            dve.wait_ge(count_done, 1)


def dense_phase(nc, w, g, he, a_tab, br_tab):
    with ExitStack() as ctx:
        q = Pools(nc, ctx)
        x = [q.sb(f"x{s}", [P, 4, P]) for s in range(2)]
        ea = [q.sb(f"ea{s}", [P, 4, FE]) for s in range(2)]
        stats = q.sb("stats", [P, 4, 6])
        mv = q.sb("mv", [P, 4, 2])
        rstd = q.sb("rstd", [P, 2, 4])
        var, std = q.sb("var", [P, 2, 4]), q.sb("std", [P, 2, 4])
        var_done, std_done = q.sem("var_done"), q.sem("std_done")
        shift = q.sb("shift", [P, 2, 4])
        h = q.sb("h", [P, 4, P])
        ht = q.sb("ht", [P, 512])
        eat = q.sb("eat", [FE, 512])
        ret = q.sb("ret", [P, 512])
        a_sb = [q.sb(f"a_sb{s}", [P, 4, P]) for s in range(2)]
        br_sb = [q.sb(f"br_sb{s}", [P, 2, 512]) for s in range(2)]
        rec_d = [q.sb(f"rec_d{s}", [P, 4, REC]) for s in range(2)]
        rec_s = [q.sb(f"rec_s{s}", [P, 4, REC]) for s in range(2)]
        junk = q.sb("junk", [P, 2, NS])
        warm = q.sb("warm", [P, 1])
        posf = q.sb("posf", [P, 8])
        pos = [q.sb(f"pos{s}", [P, 8], I32) for s in range(2)]
        ht_ps = q.ps("ht_ps", [P, 512])
        r1_ps = q.ps("r1_ps", [P, 512])
        eat_ps = q.ps("eat_ps", [FE, 512])
        re_ps = q.ps("re_ps", [P, 512])
        ab_ps = q.ps("ab_ps", [P, 2, 2, 256])
        e_ps = q.ps("e_ps", [P, 2, 2, 256])

        x_in = [q.sem(f"x_in{s}") for s in range(2)]
        ea_in = [q.sem(f"ea_in{s}") for s in range(2)]
        ealast_in = [q.sem(f"ealast_in{s}") for s in range(2)]
        xlast_in = q.sem("xlast_in")
        a_out = [q.sem(f"a_out{s}") for s in range(2)]
        br_out = [q.sem(f"br_out{s}") for s in range(2)]
        sd_out = [q.sem(f"sd_out{s}") for s in range(2)]
        ss_out = [q.sem(f"ss_out{s}") for s in range(2)]
        stats_done, aggr_done, rstd_done = q.sem("stats_done"), q.sem("aggr_done"), q.sem("rstd_done")
        shift_done, norm_done = q.sem("shift_done"), q.sem("norm_done")
        ht_t, ht_c, r1_m, r1_c = q.sem("ht_t"), q.sem("ht_c"), q.sem("r1_m"), q.sem("r1_c")
        eat_t, eat_c, re_m, re_c = q.sem("eat_t"), q.sem("eat_c"), q.sem("re_m"), q.sem("re_c")
        ab_m, ab_c, e_m, e_c = q.sem("ab_m"), q.sem("ab_c"), q.sem("e_m"), q.sem("e_c")
        rank, pos_done, meta_done, recs_done = q.sem("rank"), q.sem("pos_done"), q.sem("meta_done"), q.sem("recs_done")

        x_v = w["x"]
        ea_v = w["ea"][0:(P - 1) * EC, :].rearrange("(p c) f -> p c f", p=P - 1)
        a_v = a_tab.rearrange("(i t p) f -> i p t f", t=4, p=P)
        br_v = br_tab.rearrange("(i k) p f -> i p k f", k=2)
        last_c = EC - (NP - N)
        m_full = last_c // 8
        assert last_c % 8 == 0 and IT % 2 == 0

        def turns(eng, body):
            for s in range(2):
                body(0, s, ea[s], ea_in[s], 1, x[s])
            with eng.Fori(1, m_full) as m:
                for s in range(2):
                    body(m, s, ea[s], ea_in[s], m + 1, x[s])
            with eng.Fori(m_full, IT // 2 - 1) as m:
                for s in range(2):
                    body(m, s, g["ealast"][:, s], ealast_in[s], (m - m_full) * 2 + 2, x[s])
            m = IT // 2 - 1
            for s in range(2):
                body(m, s, g["ealast"][:, s], ealast_in[s], (m - m_full) * 2 + 2, x[s] if s == 0 else g["xlast"])

        block = ctx.enter_context(nc.Block())

        @block.sync
        def _(sp):
            def store(m, s):
                i = m * 2 + s
                sp.wait_ge(ab_c, i * 4 + 4)
                sp.nop(nofuse=True)
                sp.dma_start(a_v[bass.ds(i, 1)].rearrange("a p t f -> (a p) t f"), a_sb[s][:, :, :]).then_inc(a_out[s], 16)
                sp.dma_start(br_v[bass.ds(i, 1)].rearrange("a p k f -> (a p) k f"), br_sb[s][:, :, :]).then_inc(br_out[s], 16)

            def body(m, s, ea_t, ea_sem, _, x_t):
                i = m * 2 + s
                if positive(i * 4 - 4):
                    sp.wait_ge(norm_done, i * 4 - 4)
                    sp.nop(nofuse=True)
                if x_t is x[s]:
                    sp.dma_start(x_t[:, :, :], x_v[bass.ds(i * 512, 512), :].rearrange("(t p) f -> p t f", p=P)).then_inc(x_in[s], 16)
                else:
                    at, part = i * 512, N - i * 512 - 256
                    sp.dma_start(x_t[:, 0:2, :], x_v[at:at + 256, :].rearrange("(t p) f -> p t f", p=P)).then_inc(xlast_in, 16)
                    sp.dma_start(x_t[0:part, 2, :], x_v[at + 256:N, :]).then_inc(xlast_in, 16)
                if positive(i - 1):
                    sp.wait_ge(eat_t, i - 1)
                    sp.nop(nofuse=True)
                if ea_sem is ea_in[s]:
                    sp.dma_start(ea_t[0:P - 1, :, :], ea_v[:, bass.ds(i * 4, 4), :]).then_inc(ea_sem, 16)
                    sp.dma_start(ea_t[P - 1:P, :, :], w["ea"][bass.ds(i * 4 + (P - 1) * EC, 4), :].rearrange("(p c) f -> p c f", p=1)).then_inc(ea_sem, 16)
                else:
                    sp.dma_start(ea_t[0:112, :, :], ea_v[0:112, bass.ds(i * 4, 4), :]).then_inc(ea_sem, 16)
                    sp.dma_start(ea_t[112:P - 1, :, :], ea_v[112:P - 1, bass.ds(i * 4, 4), :]).then_inc(ea_sem, 16)
                if s == 1:
                    store(m, 0)
                elif not (isinstance(m, int) and m == 0):
                    store(m - 1, 1)

            turns(sp, body)
            store(IT // 2 - 1, 1)
            for s in range(2):
                sp.wait_ge(a_out[s], 16 * (IT // 2))
                sp.nop(nofuse=True)
                sp.wait_ge(br_out[s], 16 * (IT // 2))
                sp.nop(nofuse=True)

        @block.scalar
        def _(act):
            nc.scalar.activation(warm[:, :], g["iota0"][:, 0:1], ACT.Sqrt)

            def body(m, s, *_):
                x_t = _[3]
                i = m * 2 + s
                act.wait_ge(var_done, i + 1)
                nc.scalar.activation(std[:, s, :], var[:, s, :], ACT.Sqrt).then_inc(std_done, 1)
                act.wait_ge(shift_done, i + 1)
                if positive(i):
                    act.wait_ge(ht_t, i)
                for t in range(4):
                    nc.scalar.activation(h[:, t, :], x_t[:, t, :], ACT.Relu, bias=shift[:, s, t:t + 1],
                                         scale=rstd[:, s, t:t + 1]).then_inc(norm_done, 1)
                act.wait_ge(ht_t, i + 1)
                nc.scalar.activation(ht[:, :], ht_ps[:, :], ACT.Copy).then_inc(ht_c, 1)
                act.wait_ge(eat_t, i + 1)
                nc.scalar.activation(eat[:, :], eat_ps[:, :], ACT.Copy).then_inc(eat_c, 1)
                act.wait_ge(r1_m, i + 1)
                if positive(m * 16):
                    act.wait_ge(br_out[s], m * 16)
                nc.scalar.activation(br_sb[s][:, :, 256:512], r1_ps[:, :].rearrange("p (k n) -> p k n", k=2),
                                     ACT.Relu, bias=g["ne_b1"][:, 0:1]).then_inc(r1_c, 1)
                act.wait_ge(re_m, i + 1)
                if positive(i * 2):
                    act.wait_ge(e_m, i * 2)
                nc.scalar.activation(ret[:, :], re_ps[:, :], ACT.Relu, bias=g["ee_b1"][:, 0:1]).then_inc(re_c, 1)
                if positive(m * 16):
                    act.wait_ge(a_out[s], m * 16)
                for k in range(2):
                    act.wait_ge(ab_m, i * 2 + k + 1)
                    nc.scalar.activation(a_sb[s][:, 2 * k:2 * k + 2, :], ab_ps[:, k, :, 0:128], ACT.Copy).then_inc(ab_c, 1)
                    nc.scalar.activation(br_sb[s][:, k, 0:256].rearrange("p (h f) -> p h f", h=2),
                                         ab_ps[:, k, :, 128:256], ACT.Copy).then_inc(ab_c, 1)
                act.wait_ge(e_c, i * 4 + 4)
                if positive(m * 64):
                    act.wait_ge(ss_out[s], m * 64)
                for at in (0, E1AT):
                    nc.scalar.activation(rec_s[s][:, :, at:at + 128], rec_d[s][:, :, at:at + 128], ACT.Copy).then_inc(recs_done, 1)

            turns(act, body)

        @block.tensor
        def _(pe):
            def body(m, s, ea_t, ea_sem, ea_n, x_t):
                i = m * 2 + s
                pe.wait_ge(norm_done, i * 4 + 4)
                for t in range(4):
                    last = nc.tensor.transpose(ht_ps[:, t * P:t * P + P], h[:, t, :], g["ident"][:, :])
                last.then_inc(ht_t, 1)
                pe.wait_ge(ea_sem, ea_n * (32 if ea_sem is ea_in[s] else 16))
                pe.nop(nofuse=True)
                for t in range(4):
                    last = nc.tensor.transpose(eat_ps[:, t * P:t * P + P], ea_t[:, t, :], g["ident"][:, :])
                last.then_inc(eat_t, 1)
                pe.wait_ge(ht_c, i + 1)
                nc.tensor.matmul(r1_ps[:, :], g["ne1"][:, :], ht[:, :], start=True, stop=True).then_inc(r1_m, 1)
                pe.wait_ge(eat_c, i + 1)
                nc.tensor.matmul(re_ps[:, :], g["ee1"][:, :], eat[:, :], start=True, stop=True).then_inc(re_m, 1)
                pe.wait_ge(r1_c, i + 1)
                if positive(i * 4):
                    pe.wait_ge(ab_c, i * 4)
                for k in range(2):
                    for hh in range(2):
                        last = nc.tensor.matmul(ab_ps[:, k, hh, :], br_sb[s][:, k, 256 + hh * P:384 + hh * P],
                                                g["f0"][:, 0:256], start=True, stop=True)
                    last.then_inc(ab_m, 1)
                pe.wait_ge(re_c, i + 1)
                if positive(i * 4):
                    pe.wait_ge(e_c, i * 4)
                for k in range(2):
                    for hh in range(2):
                        t = 2 * k + hh
                        last = nc.tensor.matmul(e_ps[:, k, hh, :], ret[:, t * P:t * P + P], g["fe"][:, :],
                                                start=True, stop=True)
                    last.then_inc(e_m, 1)

            turns(pe, body)

        @block.vector
        def _(dve):
            v = nc.vector

            def body(m, s, ea_t, ea_sem, ea_n, x_t):
                i = m * 2 + s
                if x_t is x[s]:
                    dve.wait_ge(x_in[s], m * 16 + 16)
                else:
                    dve.wait_ge(xlast_in, 32)
                if positive(i * 4):
                    dve.wait_ge(aggr_done, i * 4)
                for t in range(4):
                    v.bn_stats(stats[:, t, :], x_t[:, t, :]).then_inc(stats_done, 1)
                dve.wait_ge(stats_done, i * 4 + 4)
                if positive(i):
                    dve.wait_ge(shift_done, i)
                    dve.nop(nofuse=True)
                for t in range(4):
                    v.bn_aggr(mv[:, t, :], stats[:, t, :]).then_inc(aggr_done, 1)
                dve.wait_ge(aggr_done, i * 4 + 4)
                if positive(i * 4 - 4):
                    dve.wait_ge(norm_done, i * 4 - 4)
                v.tensor_scalar(var[:, s, :], mv[:, :, 1], EPS, None, ALU.add).then_inc(var_done, 1)
                dve.wait_ge(std_done, i + 1)
                v.reciprocal(rstd[:, s, :], std[:, s, :]).then_inc(rstd_done, 1)
                dve.wait_ge(rstd_done, i + 1)
                v.scalar_tensor_tensor(shift[:, s, :], mv[:, :, 0], -1.0, rstd[:, s, :], ALU.mult, ALU.mult).then_inc(shift_done, 1)
                if positive(i):
                    dve.wait_ge(pos_done, i)
                for t in range(4):
                    for j, (run, blk) in enumerate((("run_d", "blk_d"), ("run_s", "blk_s"))):
                        if positive(i * 16 + t * 4 + j - 1):
                            dve.wait_ge(rank, i * 16 + t * 4 + j - 1)
                        v.scalar_tensor_tensor(junk[:, j, :], g["iota0"][:, :], g[blk][:, bass.ds(i * 4 + t, 1)], g[run][:, :],
                                               ALU.is_equal, ALU.mult, accum_out=posf[:, 4 * j + t:4 * j + t + 1]).then_inc(rank, 1)
                    for j, (run, blk) in enumerate((("run_d", "blk_d"), ("run_s", "blk_s"))):
                        v.scalar_tensor_tensor(g[run][:, :], g["iota0"][:, :], g[blk][:, bass.ds(i * 4 + t, 1)], g[run][:, :],
                                               ALU.is_equal, ALU.add).then_inc(rank, 1)
                if positive(m * 64):
                    dve.wait_ge(sd_out[s], m * 64)
                if positive(m * 64):
                    dve.wait_ge(ss_out[s], m * 64)
                dve.wait_ge(rank, i * 16 + 16)
                v.tensor_copy(pos[s][:, :], posf[:, :]).then_inc(pos_done, 1)
                v.tensor_copy(rec_d[s][:, :, META:META + 4].bitcast(I32), g["meta_d"][:, bass.ds(i * 4, 4), :]).then_inc(meta_done, 1)
                v.tensor_copy(rec_s[s][:, :, META:META + 4].bitcast(I32), g["meta_s"][:, bass.ds(i * 4, 4), :]).then_inc(meta_done, 1)
                for t in range(4):
                    dve.wait_ge(e_m, i * 2 + t // 2 + 1)
                    for at, c in ((0, 0), (E1AT, 128)):
                        ins = v.tensor_tensor(rec_d[s][:, t, at:at + 128], e_ps[:, t // 2, t % 2, c:c + 128],
                                              g["ebias"][:, c:c + 128], ALU.add)
                    ins.then_inc(e_c, 1)

            turns(dve, body)

        @block.gpsimd
        def _(pool):
            def body(m, s, *_):
                i = m * 2 + s
                pool.wait_ge(e_c, i * 4 + 4)
                pool.wait_ge(meta_done, i * 2 + 2)
                pool.nop(nofuse=True)
                for t in range(4):
                    pool.indirect_dma_start(he[:, :], bass.IndirectOffsetOnAxis(ap=pos[s][:, t:t + 1], axis=0),
                                            rec_d[s][:, t, :], None).then_inc(sd_out[s], 16)
                pool.wait_ge(recs_done, i * 2 + 2)
                pool.nop(nofuse=True)
                for t in range(4):
                    pool.indirect_dma_start(he[:, :], bass.IndirectOffsetOnAxis(ap=pos[s][:, 4 + t:5 + t], axis=0),
                                            rec_s[s][:, t, :], None).then_inc(ss_out[s], 16)

            turns(pool, body)
            for s in range(2):
                pool.wait_ge(sd_out[s], 64 * (IT // 2))
                pool.wait_ge(ss_out[s], 64 * (IT // 2))


def edge_phase(nc, g, he, layer, a_tab, br_tab, out_a, out_br, out):
    msgs = layer < 2
    tag = f"l{layer}_"
    with ExitStack() as ctx:
        q = Pools(nc, ctx)
        width = {0: 132, 1: 132, 2: 4}[layer]
        col0 = {0: 0, 1: META, 2: META}[layer]
        meta_at = {0: 128, 1: 0, 2: 0}[layer]
        term_at = {0: 0, 1: 4}.get(layer)
        key = 1 if msgs else 2
        brw = 512 if msgs else 256
        ch = q.sb(tag + "ch", [P, UNR, width])
        nbr = q.sb(tag + "nbr", [P, UNR, P])
        metaf = q.sb(tag + "metaf", [P, UNR, 4])
        ohf = q.sb(tag + "ohf", [P, 4, 2, SUB])
        ohb = q.sb(tag + "ohb", [P, 4, 2, SUB], BF16)
        oht = q.sb(tag + "oht", [P, 2, P])
        pre = q.sb(tag + "pre", [P, 2, P])
        msg = q.sb(tag + "msg", [P, 2, P])
        br = q.sb(tag + "br", [P, 4, brw])
        st = q.sb(tag + "st", [P, 512])
        rt = q.sb(tag + "rt", [P, BLK])
        ra = q.sb(tag + "ra", [P, 4, 2, P])
        rb = q.sb(tag + "rb", [P, 4, 512])
        oht_ps = q.ps(tag + "oht_ps", [P, 8, P], BF16)
        pre_ps = q.ps(tag + "pre_ps", [P, 2, P])
        s_ps = q.ps(tag + "s_ps", [P, 2, 512])
        r_ps = q.ps(tag + "r_ps", [P, 512])
        o_ps = q.ps(tag + "o_ps", [P, 2, 256])

        def sem(name):
            return q.sem(tag + name)

        ch_in, br_in, res_out = sem("ch_in"), sem("br_in"), sem("res_out")
        res2_out, stored = sem("res2_out"), sem("stored")
        nbr_in = g["nbr_in"]
        metaf_done, oh_done, sum_done, pre_done = sem("metaf_done"), sem("oh_done"), sem("sum_done"), sem("pre_done")
        oht_t, oht_c, look_done, msg_done, s_done = sem("oht_t"), sem("oht_c"), sem("look_done"), sem("msg_done"), sem("s_done")
        st_c, r_m, rt_c, o_m, o_c = sem("st_c"), sem("r_m"), sem("rt_c"), sem("o_m"), sem("o_c")

        s0, msg0, pre0, t0 = 4, 2, 2, 1
        oh0 = t0 if msgs else PAIRS
        used = sum_done if msgs else oh_done
        block = ctx.enter_context(nc.Block())
        he_v = he.rearrange("(c p) f -> p c f", p=P)

        @block.sync
        def _(sp):
            def load_block(b):
                if positive(b * 16):
                    sp.wait_ge(br_in, b * 16)
                    sp.nop(nofuse=True)
                if positive(b - 3):
                    sp.wait_ge(r_m, b - 3)
                    sp.nop(nofuse=True)
                sp.dma_start(br[:, bass.ds(b % 4, 1), :].rearrange("p a f -> p (a f)"),
                             br_tab[bass.ds(b, 1)].rearrange("a p f -> (a p) f")).then_inc(br_in, 16)

            def load_chunks(b):
                first = 0 if isinstance(b, int) and b == 0 else sp.value_load(g["gends"][0:1, bass.ds(b, 1)], min_val=1, max_val=TMAX // GRP - 1)
                end = sp.value_load(g["gends"][0:1, bass.ds(b + 1, 1)], min_val=1, max_val=TMAX // GRP)
                with sp.Fori(first, end) as k:
                    sp.wait_ge(ch_in, k * 16)
                    sp.nop(nofuse=True)
                    sp.wait_ge(used, k * (GRP // 2) + GRP // 2)
                    sp.nop(nofuse=True)
                    sp.dma_start(ch[:, bass.ds((k % (UNR // GRP)) * GRP, GRP), :],
                                 he_v[:, bass.ds(k * GRP, GRP), col0:col0 + width]).then_inc(ch_in, 16)

            sp.sem_inc(stored, PRIME)

            def store(b):
                sp.wait_ge(o_c, b + 1)
                sp.nop(nofuse=True)
                sp.wait_ge(res_out, b * 16)
                sp.nop(nofuse=True)
                if layer == 0:
                    sp.wait_ge(res2_out, b * 16)
                    sp.nop(nofuse=True)
                sp.sem_inc(stored, 1)
                if msgs:
                    sp.dma_start(out_a.rearrange("(b h p) f -> b p h f", h=2, p=P)[bass.ds(b, 1)].rearrange("a p h f -> (a p) h f"),
                                 ra[:, bass.ds(b % 4, 1), :, :].rearrange("p a h f -> p (a h) f")).then_inc(res_out, 16)
                    if layer == 0:
                        sp.dma_start(out_br[bass.ds(b, 1)].rearrange("a p f -> (a p) f"),
                                     rb[:, bass.ds(b % 4, 1), :].rearrange("p a f -> p (a f)")).then_inc(res2_out, 16)
                else:
                    if isinstance(b, int) and b == NB - 1:
                        rest = N - b * BLK
                        sp.dma_start(out[b * BLK:N, :], ra[0:rest, b % 4, 0, :]).then_inc(res_out, 16)
                    else:
                        sp.dma_start(out[bass.ds(b * BLK, BLK), :].rearrange("(h p) f -> p h f", p=P),
                                     ra[:, bass.ds(b % 4, 1), :, :].rearrange("p a h f -> p (a h) f")).then_inc(res_out, 16)

            for b in range(AHEAD):
                load_block(b)
                load_chunks(b)
            for b in range(2):
                load_block(b + AHEAD)
                load_chunks(b + AHEAD)
            with sp.Fori(2, NB - AHEAD) as b:
                load_block(b + AHEAD)
                load_chunks(b + AHEAD)
                store(b - 2)
            for b in range(NB - AHEAD - 2, NB):
                store(b)
            sp.wait_ge(res_out, 16 * NB)
            sp.nop(nofuse=True)
            if layer == 0:
                sp.wait_ge(res2_out, 16 * NB)
                sp.nop(nofuse=True)

        @block.gpsimd
        def _(pool):
            turns = pool.value_load(g["turns"][0:1, 0:1], min_val=2, max_val=TMAX // UNR)
            free, free0 = (pre_done, pre0) if msgs else (msg_done, msg0)

            def turn(k, k_later):
                for j in range(PAIRS):
                    p = k * PAIRS + j
                    if j % 2 == 0:
                        pool.wait_ge(ch_in, k * (UNR // GRP * 16) + (j // 2 + 1) * 16)
                        if k_later:
                            pool.wait_ge(free, p - PAIRS + 2 + free0)
                        pool.nop(nofuse=True)
                    for c in (2 * j, 2 * j + 1):
                        pool.indirect_dma_start(nbr[:, c, :], None, a_tab[:, :], bass.IndirectOffsetOnAxis(
                            ap=ch[:, c, meta_at:meta_at + 1].bitcast(I32), axis=0)).then_inc(nbr_in[j], 16)

            turn(0, False)
            with pool.Fori(1, turns) as k:
                turn(k, True)

        @block.vector
        def _(dve):
            v = nc.vector
            dve.sem_inc(used, PAIRS)
            if msgs:
                dve.sem_inc(oh_done, oh0)
                dve.sem_inc(pre_done, pre0)
            last_turn = dve.value_load(g["turns"][0:1, 1:2], min_val=1, max_val=TMAX // UNR - 1)

            earlier = (last_turn + 1) * layer if layer else 0

            def onehot(k, j):
                p, c = k * PAIRS + j, 2 * j
                if j % 2 == 0:
                    dve.wait_ge(ch_in, k * (UNR // GRP * 16) + (j // 2 + 1) * 16)
                    v.tensor_copy(metaf[:, c:c + GRP, :], ch[:, c:c + GRP, meta_at:meta_at + 4].bitcast(I32)).then_inc(metaf_done, 1)
                    dve.wait_ge(metaf_done, k * (UNR // GRP) + j // 2 + 1)
                dve.wait_ge(s_done, p - 3 + s0)
                if msgs:
                    for i in range(2):
                        v.tensor_scalar(ohb[:, j % 4, i, :], g["iota1b"][:, :], metaf[:, c + i, key:key + 1], None, ALU.is_equal)
                else:
                    dve.wait_ge(nbr_in[j], (earlier + k + 1) * 32)
                for i in range(2):
                    last = v.tensor_scalar(ohf[:, j % 4, i, :], g["iota1"][:, :], metaf[:, c + i, key:key + 1], None, ALU.is_equal)
                last.then_inc(oh_done, 1)
                if msgs:
                    dve.wait_ge(nbr_in[j], (earlier + k + 1) * 32)
                    v.tensor_tensor(nbr[:, c:c + 2, :], nbr[:, c:c + 2, :], ch[:, c:c + 2, term_at:term_at + P],
                                    ALU.add).then_inc(sum_done, 1)

            def add_own(k, j):
                p, c = k * PAIRS + j, 2 * j
                dve.wait_ge(look_done, p + 1 + t0)
                dve.wait_ge(msg_done, p + msg0)
                dve.wait_ge(sum_done, p + PAIRS + 1)
                v.tensor_tensor(pre[:, :, :], pre_ps[:, :, :], nbr[:, c:c + 2, :], ALU.add).then_inc(pre_done, 1)

            def turn(k, first, last):
                if first and msgs:
                    onehot(0, 0)
                for j in range(PAIRS):
                    if msgs:
                        if j < PAIRS - 1:
                            onehot(k, j + 1)
                        elif not last:
                            onehot(k + 1, 0)
                        add_own(k, j)
                    else:
                        onehot(k, j)

            if msgs:
                turn(0, True, False)
                with dve.Fori(1, last_turn) as k:
                    turn(k, False, False)
                turn(last_turn, False, True)
            else:
                turn(0, True, False)
                with dve.Fori(1, last_turn + 1) as k:
                    turn(k, False, False)

        def bounds(eng, b):
            word = eng.value_load(g["bounds"][0:1, bass.ds(b, 1)], min_val=0, max_val=(1 << 3 * BITS) - 1)
            p0 = 0 if isinstance(b, int) and b == 0 else eng.snap(word & ((1 << BITS) - 1))
            p1 = eng.snap((word >> BITS) & ((1 << BITS) - 1))
            return p0, p1, eng.snap(word >> 2 * BITS)

        @block.tensor
        def _(pe):
            pe.sem_inc(s_done, s0)
            if msgs:
                pe.sem_inc(oht_t, t0)
                pe.sem_inc(look_done, t0)

            def clear_sums(b):
                if positive(b - 1):
                    pe.wait_ge(st_c, b - 1)
                nc.tensor.matmul(s_ps[:, b % 2, :], g["zrow"][0:1, 0:P], g["zrow"][:, :], start=True, stop=False)

            def transpose_pair(p):
                if msgs:
                    pe.wait_ge(oh_done, p + 1 + oh0)
                    for i in range(2):
                        last = nc.tensor.transpose(oht_ps[:, i, :], ohb[:, p % 4, i, :], g["identb"][:, :])
                    last.then_inc(oht_t, 1)

            def look_up(p, b, h):
                if msgs:
                    pe.wait_ge(pre_done, p + pre0)
                    pe.wait_ge(oht_c, p + 1 + t0)
                    for i in range(2):
                        last = nc.tensor.matmul(pre_ps[:, i, :], oht[:, i, :], br[:, b % 4, h * SUB:(h + 1) * SUB],
                                                start=True, stop=True)
                    last.then_inc(look_done, 1)

            def sum_pair(p, b, h, stop):
                pe.wait_ge(msg_done, p + 1 + msg0)
                for i in range(2):
                    last = nc.tensor.matmul(s_ps[:, b % 2, h * SUB:(h + 1) * SUB], msg[:, i, :], ohf[:, p % 4, i, :],
                                            start=False, stop=False)
                if msgs:
                    for i in range(2):
                        last = nc.tensor.matmul(s_ps[0:1, b % 2, BLK + h * SUB:BLK + (h + 1) * SUB], g["onecol"][:, :],
                                                ohb[:, p % 4, i, :], start=False, stop=False)
                if stop:
                    last = nc.tensor.matmul(s_ps[:, b % 2, :], g["zrow"][0:1, 0:P], g["zrow"][:, :], start=False, stop=True)
                last.then_inc(s_done, 1)

            def update(b):
                pe.wait_ge(st_c, b + 1)
                pe.wait_ge(br_in, b * 16 + 16)
                if msgs:
                    if positive(b):
                        pe.wait_ge(rt_c, b)
                    nc.tensor.matmul(r_ps[:, 0:BLK], g["fq"][:, layer, :], st[:, 0:BLK], start=True, stop=False)
                    nc.tensor.matmul(r_ps[:, 0:BLK], g["f0" if layer == 0 else "f1"][:, 256:384], br[:, b % 4, 256:512], start=False, stop=False)
                    nc.tensor.matmul(r_ps[:, 0:BLK], g["crow"][0:1, layer, :], st[0:1, BLK:2 * BLK], start=False, stop=True).then_inc(r_m, 1)
                else:
                    if positive(b):
                        pe.wait_ge(o_c, b)
                    for hh in range(2):
                        nc.tensor.matmul(o_ps[:, hh, 0:P], st[:, hh * P:hh * P + P], g["ident"][:, :], start=True, stop=False)
                        last = nc.tensor.matmul(o_ps[:, hh, 0:P], g["ident"][:, :], br[:, b % 4, hh * P:hh * P + P], start=False, stop=True)
                    last.then_inc(r_m, 1)

            def project(b):
                if msgs:
                    pe.wait_ge(rt_c, b + 1)
                    pe.wait_ge(o_c, b)
                    for hh in range(2):
                        rhs = g["f1"][:, 0:256] if layer == 0 else g["agw2"][:, :]
                        last = nc.tensor.matmul(o_ps[:, hh, 0:256 if layer == 0 else P], rt[:, hh * P:hh * P + P], rhs, start=True, stop=True)
                    last.then_inc(o_m, 1)

            def inner(p0, p1, b, h):
                with pe.If(p1 > p0 + 1):
                    with pe.Fori(p0 + 1, p1) as p:
                        transpose_pair(p)
                        look_up(p, b, h)
                        sum_pair(p - 1, b, h, False)

            def one_block(b, prev, prev2):
                p0, p1, p2 = bounds(pe, b)
                pe.wait_ge(br_in, b * 16 + 16)
                transpose_pair(p0)
                if prev2:
                    project(b - 2)
                look_up(p0, b, 0)
                if prev:
                    sum_pair(p0 - 1, b - 1, 1, True)
                clear_sums(b)
                inner(p0, p1, b, 0)
                transpose_pair(p1)
                if prev:
                    update(b - 1)
                look_up(p1, b, 1)
                sum_pair(p1 - 1, b, 0, False)
                inner(p1, p2, b, 1)

            one_block(0, False, False)
            one_block(1, True, False)
            with pe.Fori(2, NB) as b:
                one_block(b, True, True)
            b = NB - 1
            total = bounds(pe, b)[2]
            sum_pair(total - 1, b, 1, True)
            project(b - 1)
            update(b)
            project(b)

        @block.scalar
        def _(act):
            act.sem_inc(msg_done, msg0)
            if msgs:
                act.sem_inc(oht_c, t0)
            dummy = q.sb(tag + "dummy", [P, 1])
            nc.scalar.activation(dummy[:, :], g["iota0"][:, 0:1], ACT.Relu)

            def copy_onehot(p):
                if msgs:
                    act.wait_ge(oht_t, p + 1 + t0)
                    nc.scalar.activation(oht[:, :, :], oht_ps[:, 0:2, :], ACT.Copy).then_inc(oht_c, 1)

            def message(p):
                if isinstance(p, int) and p < 0:
                    return
                act.wait_ge(s_done, p + s0)
                if msgs:
                    act.wait_ge(pre_done, p + 1 + pre0)
                    nc.scalar.activation(msg[:, :, :], pre[:, :, :], ACT.Relu).then_inc(msg_done, 1)
                else:
                    act.wait_ge(oh_done, p + 1 + oh0)
                    nc.scalar.activation(msg[:, :, :], nbr[:, bass.ds((p % PAIRS) * 2, 2), :], ACT.Copy).then_inc(msg_done, 1)

            def copy_sums(b, p0):
                act.wait_ge(s_done, p0 + s0)
                if positive(b):
                    act.wait_ge(r_m, b)
                n = 512 if msgs else BLK
                nc.scalar.activation(st[:, 0:n], s_ps[:, bass.ds(b % 2, 1), 0:n].rearrange("p a f -> p (a f)"), ACT.Copy).then_inc(st_c, 1)

            def copy_out(b):
                act.wait_ge(o_m if msgs else r_m, b + 1)
                act.wait_ge(stored, b - 2 + PRIME)
                row = ra[:, bass.ds(b % 4, 1), :, :].rearrange("p a h f -> p (a h) f")
                ins = nc.scalar.activation(row, o_ps[:, :, 0:P], ACT.Copy)
                if layer == 0:
                    ins = nc.scalar.activation(rb[:, bass.ds(b % 4, 1), 0:256].rearrange("p a (h f) -> p (a h) f", h=2),
                                               o_ps[:, :, P:256], ACT.Copy)
                    ins = nc.scalar.activation(rb[:, bass.ds(b % 4, 1), 256:512].rearrange("p a f -> p (a f)"), rt[:, :], ACT.Copy)
                ins.then_inc(o_c, 1)

            def relu_nodes(b):
                if msgs:
                    act.wait_ge(r_m, b + 1)
                    if positive(b):
                        act.wait_ge(o_c, b)
                    nc.scalar.activation(rt[:, :], r_ps[:, 0:BLK], ACT.Relu, bias=g["pbias"][:, layer:layer + 1]).then_inc(rt_c, 1)
                    act.wait_ge(rt_c, b + 1)

            def inner(p0, p1):
                with act.If(p1 > p0 + 1):
                    with act.Fori(p0 + 1, p1) as p:
                        copy_onehot(p)
                        message(p - 1)

            def one_block(b, prev, prev2):
                p0, p1, p2 = bounds(act, b)
                copy_onehot(p0)
                message(p0 - 1)
                if prev2 and msgs:
                    copy_out(b - 2)
                if prev:
                    copy_sums(b - 1, p0)
                inner(p0, p1)
                copy_onehot(p1)
                message(p1 - 1)
                if prev:
                    relu_nodes(b - 1) if msgs else copy_out(b - 1)
                inner(p1, p2)

            one_block(0, False, False)
            one_block(1, True, False)
            with act.Fori(2, NB) as b:
                one_block(b, True, True)
            b = NB - 1
            total = bounds(act, b)[2]
            message(total - 1)
            copy_sums(b, total)
            if msgs:
                copy_out(b - 1)
                relu_nodes(b)
            copy_out(b)


def norm_phase(nc, w, g, y_tab, h_tab, xh_tab):
    with ExitStack() as ctx:
        q = Pools(nc, ctx)
        x = [q.sb(f"nx{s}", [P, 4, P]) for s in range(2)]
        y = [q.sb(f"ny{s}", [P, 4, P]) for s in range(2)]
        x1 = [q.sb(f"nx1{s}", [P, 4, P]) for s in range(2)]
        h = [q.sb(f"nh{s}", [P, 4, P]) for s in range(2)]
        xh = [q.sb(f"nxh{s}", [P, 4, P]) for s in range(2)]
        stats = q.sb("nstats", [P, 4, 6])
        mv = q.sb("nmv", [P, 2, 4, 2])
        rstd = q.sb("nrstd", [P, 2, 4])
        var, std = q.sb("nvar", [P, 2, 4]), q.sb("nstd", [P, 2, 4])
        var_done, std_done = q.sem("nvar_done"), q.sem("nstd_done")
        shift = q.sb("nshift", [P, 2, 4])
        dummy = q.sb("ndummy", [P, 1])
        x_in = [q.sem(f"nx_in{s}") for s in range(2)]
        y_in = [q.sem(f"ny_in{s}") for s in range(2)]
        h_out = [q.sem(f"nh_out{s}") for s in range(2)]
        xh_out = [q.sem(f"nxh_out{s}") for s in range(2)]
        sum_done, bias_done, stats_done, aggr_done = q.sem("nsum"), q.sem("nbias"), q.sem("nstats_done"), q.sem("naggr")
        rstd_done, shift_done, norm_done, xh_done = q.sem("nrstd_done"), q.sem("nshift_done"), q.sem("nnorm"), q.sem("nxh_done")
        h_v = h_tab.rearrange("(i t p) f -> i p t f", t=4, p=P)
        y_v = y_tab.rearrange("(i t p) f -> i p t f", t=4, p=P)
        xh_v = xh_tab.rearrange("(i k) p (h f) -> i p k h f", k=2, h=2)


        def turns(eng, body):
            for s in range(2):
                body(0, s, x[s])
            with eng.Fori(1, IT // 2 - 1) as m:
                for s in range(2):
                    body(m, s, x[s])
            for s in range(2):
                body(IT // 2 - 1, s, x[s] if s == 0 else g["xlast"])

        def earlier(m, s, back):
            turn, slot = (m, s) if back == 0 else (m - (back - s + 1) // 2, (s - back) % 2)
            return (None if isinstance(turn, int) and turn < 0 else turn), slot

        block = ctx.enter_context(nc.Block())

        @block.sync
        def _(sp):
            def body(m, s, x_t):
                i = m * 2 + s
                if positive(i - 1):
                    sp.wait_ge(sum_done, i - 1)
                    sp.nop(nofuse=True)
                sp.dma_start(y[s][:, :, :], y_v[bass.ds(i, 1)].rearrange("a p t f -> (a p) t f")).then_inc(y_in[s], 16)
                if x_t is x[s]:
                    sp.dma_start(x_t[:, :, :], w["x"][bass.ds(i * 512, 512), :].rearrange("(t p) f -> p t f", p=P)).then_inc(x_in[s], 16)

            turns(sp, body)

        @block.vector
        def _(dve):
            v = nc.vector

            def statistics(m, s, x_t):
                i = m * 2 + s
                dve.wait_ge(y_in[s], m * 16 + 16)
                if x_t is x[s]:
                    dve.wait_ge(x_in[s], m * 16 + 16)
                if positive(i - 1):
                    dve.wait_ge(xh_done, i - 1)
                v.tensor_tensor(x1[s][:, :, :], x_t[:, :, :], y[s][:, :, :], ALU.add).then_inc(sum_done, 1)
                dve.wait_ge(sum_done, i + 1)
                v.tensor_tensor(x1[s][:, :, :], x1[s][:, :, :], g["agb2b"][:, :, :], ALU.add).then_inc(bias_done, 1)
                dve.wait_ge(bias_done, i + 1)
                for t in range(4):
                    v.bn_stats(stats[:, t, :], x1[s][:, t, :]).then_inc(stats_done, 1)
                dve.wait_ge(stats_done, i * 4 + 4)
                dve.nop(nofuse=True)
                for t in range(4):
                    v.bn_aggr(mv[:, s, t, :], stats[:, t, :]).then_inc(aggr_done, 1)
                dve.wait_ge(aggr_done, i * 4 + 4)
                v.tensor_scalar(var[:, s, :], mv[:, s, :, 1], EPS, None, ALU.add).then_inc(var_done, 1)

            def scale(m, s):
                i = m * 2 + s
                dve.wait_ge(std_done, i + 1)
                v.reciprocal(rstd[:, s, :], std[:, s, :]).then_inc(rstd_done, 1)
                dve.wait_ge(rstd_done, i + 1)
                v.scalar_tensor_tensor(shift[:, s, :], mv[:, s, :, 0], -1.0, rstd[:, s, :], ALU.mult, ALU.mult).then_inc(shift_done, 1)

            def add(m, s):
                i = m * 2 + s
                dve.wait_ge(norm_done, i * 4 + 4)
                if positive(m * 16):
                    dve.wait_ge(xh_out[s], m * 16)
                v.tensor_tensor(xh[s][:, :, :], x1[s][:, :, :], h[s][:, :, :], ALU.add).then_inc(xh_done, 1)

            def body(m, s, x_t):
                m2, s2 = earlier(m, s, 2)
                if m2 is not None:
                    add(m2, s2)
                m1, s1 = earlier(m, s, 1)
                if m1 is not None:
                    scale(m1, s1)
                statistics(m, s, x_t)

            turns(dve, body)
            add(IT // 2 - 1, 0)
            scale(IT // 2 - 1, 1)
            add(IT // 2 - 1, 1)

        @block.scalar
        def _(act):
            nc.scalar.activation(dummy[:, :], g["iota0"][:, 0:1], ACT.Sqrt)

            def normalise(m, s):
                i = m * 2 + s
                act.wait_ge(shift_done, i + 1)
                if positive(m * 16):
                    act.wait_ge(h_out[s], m * 16)
                if positive(i - 1):
                    act.wait_ge(xh_done, i - 1)
                for t in range(4):
                    nc.scalar.activation(h[s][:, t, :], x1[s][:, t, :], ACT.Relu, bias=shift[:, s, t:t + 1],
                                         scale=rstd[:, s, t:t + 1]).then_inc(norm_done, 1)

            def store(m, s):
                i = m * 2 + s
                act.wait_ge(xh_done, i + 1)
                act.nop(nofuse=True)
                act.dma_start(h_v[bass.ds(i, 1)].rearrange("a p t f -> (a p) t f"), h[s][:, :, :]).then_inc(h_out[s], 16)
                act.dma_start(xh_v[bass.ds(i, 1)].rearrange("a p k h f -> (a p) k (h f)"),
                              xh[s][:, :, :].rearrange("p (k h) f -> p k (h f)", k=2)).then_inc(xh_out[s], 16)

            def body(m, s, x_t):
                i = m * 2 + s
                m1, s1 = earlier(m, s, 1)
                if m1 is not None:
                    normalise(m1, s1)
                m2, s2 = earlier(m, s, 2)
                if m2 is not None:
                    store(m2, s2)
                act.wait_ge(var_done, i + 1)
                nc.scalar.activation(std[:, s, :], var[:, s, :], ACT.Sqrt).then_inc(std_done, 1)

            turns(act, body)
            normalise(IT // 2 - 1, 1)
            store(IT // 2 - 1, 0)
            store(IT // 2 - 1, 1)
            for s in range(2):
                act.wait_ge(h_out[s], 16 * (IT // 2))
                act.nop(nofuse=True)
                act.wait_ge(xh_out[s], 16 * (IT // 2))
                act.nop(nofuse=True)


def gnn_program(nc, w, out):
    def dram(name, shape, dt=FP32):
        return nc.dram_tensor(name, shape, dt).ap()

    he = dram("he", [TMAX * P, REC])
    a0, a1 = dram("a0", [NP, P]), dram("a1", [NP, P])
    br0, br1 = dram("br0", [NB, P, 512]), dram("br1", [NB, P, 512])
    y_tab, h_tab, xh_tab = dram("y_tab", [NP, P]), dram("h_tab", [NP, P]), dram("xh_tab", [NB, P, 256])
    with ExitStack() as ctx:
        q = Pools(nc, ctx)
        g = {
            "ne1": q.sb("ne1", [P, P]), "ee1": q.sb("ee1", [FE, P]), "agw2": q.sb("agw2", [P, P]),
            "ne_b1": q.sb("ne_b1", [P, 1]), "ee_b1": q.sb("ee_b1", [P, 1]),
            "agb2": q.sb("agb2", [1, P]), "agb2b": q.sb("agb2b", [P, 4, P]),
            "f0": q.sb("f0", [P, 384]), "f1": q.sb("f1", [P, 384]), "fe": q.sb("fe", [P, 256]),
            "fq": q.sb("fq", [P, 2, P]), "ebias": q.sb("ebias", [P, 256]), "crow": q.sb("crow", [1, 2, P]),
            "pbias": q.sb("pbias", [P, 2]),
            "ident": q.sb("ident", [P, P]), "identb": q.sb("identb", [P, P], BF16), "onecol": q.sb("onecol", [P, 1], BF16),
            "iota0": q.sb("iota0", [P, NS]), "iota1": q.sb("iota1", [P, SUB]), "iota1b": q.sb("iota1b", [P, SUB], BF16),
            "zrow": q.sb("zrow", [1, 512], BF16),
            "xlast": q.sb("xlast", [P, 4, P]), "ealast": q.sb("ealast", [P, 2, 4, FE]),
            "meta_d": q.sb("meta_d", [P, EC, 4], I32), "meta_s": q.sb("meta_s", [P, EC, 4], I32),
            "blk_d": q.sb("blk_d", [P, EC]), "blk_s": q.sb("blk_s", [P, EC]),
            "run_d": q.sb("run_d", [P, NS]), "run_s": q.sb("run_s", [P, NS]),
            "ends": q.sb("ends", [P, NS + 1], I32), "gends": q.sb("gends", [P, NB + 1], I32),
            "bounds": q.sb("bounds", [P, NB], I32),
            "nbr_in": [q.sem(f"nbr_in{j}") for j in range(PAIRS)],
            "turns": q.sb("turns", [P, 2], I32),
        }
        setup_phase(nc, w, g, he)
        dense_phase(nc, w, g, he, a0, br0)
        edge_phase(nc, g, he, 0, a0, br0, a1, br1, None)
        edge_phase(nc, g, he, 1, a1, br1, y_tab, None, None)
        norm_phase(nc, w, g, y_tab, h_tab, xh_tab)
        edge_phase(nc, g, he, 2, h_tab, xh_tab, None, None, out)


_INS = {"x": "x", "src": "src", "dst": "dst", "ea": "edge_attr_64"}
_INS.update({k: "L0_gnn_" + k for k in (
    "ne_w1", "ne_b1", "ne_w2", "ne_b2", "ee_w1", "ee_b1", "ee_w2", "ee_b2", "ml_w1", "ml_b1", "ml_w2", "ml_b2",
    "agg_w1", "agg_b1", "agg_w2", "agg_b2")})


def kernel(**inputs):
    import numpy as _np
    import concourse.bacc as _bacc
    from concourse import mybir as _mybir
    from concourse.bass_utils import run_bass_kernel_spmd as _run

    nc = _bacc.Bacc("TRN2", target_bir_lowering=False, num_devices=1)
    arrays, w = {}, {}
    for short, name in _INS.items():
        a = _np.ascontiguousarray(inputs[name])
        arrays[f"in_{name}"] = a
        w[short] = nc.dram_tensor(f"in_{name}", a.shape, _mybir.dt.from_np(a.dtype), kind="ExternalInput").ap()
    out = nc.dram_tensor("out_0", [N, P], _mybir.dt.float32, kind="ExternalOutput").ap()
    gnn_program(nc, w, out)
    r = _run(nc, [arrays], core_ids=[0])
    return r.results[0]["out_0"]
```

```python
import concourse.bass as bass
from concourse import mybir
from contextlib import ExitStack

FP32 = mybir.dt.float32
BF16 = mybir.dt.bfloat16
FP16 = mybir.dt.float16
I32 = mybir.dt.int32
ALU = mybir.AluOpType
ACT = mybir.ActivationFunctionType

P = 128
N = 50000
FE = 64
SUB = 128
BLK = 2 * SUB
NB = -(-N // BLK)
NS = 2 * NB
NP = NB * BLK
EC = NP // P
IT = NP // (4 * P)
GRP = 4
UNR = 16
PAIRS = UNR // 2
TMAX = -(-(2 * NP // P + 2 * NS) // UNR) * UNR
TMIN = 2 * NP // P // UNR
BITS = (TMAX // 2).bit_length()
REC = 260
META = 128
E1AT = 132
PRIME = 8
AHEAD = 3
EPS = 1e-5


def positive(count):
    return not isinstance(count, int) or count > 0




class Pools:

    def __init__(self, nc, ctx):
        self.nc, self.ctx = nc, ctx

    def sb(self, name, shape, dt=FP32):
        return self.ctx.enter_context(self.nc.sbuf_tensor(name, shape, dt))

    def ps(self, name, shape, dt=FP32):
        return self.ctx.enter_context(self.nc.psum_tensor(name, shape, dt))

    def sem(self, name):
        return self.ctx.enter_context(self.nc.semaphore(name))


def setup_phase(nc, w, g, he):
    with ExitStack() as ctx:
        q = Pools(nc, ctx)
        src_i = q.sb("src_i", [P, EC], I32)
        dst_i = q.sb("dst_i", [P, EC], I32)
        wide = q.sb("wide", [P, UNR * REC])
        tmp_i = q.sb("tmp_i", [P, NS], I32)
        iotah = q.sb("iotah", [P, NS], FP16)
        onehot = q.sb("onehot", [P, 4, 2, NS], BF16)
        lower = q.sb("lower", [P, P])
        ones = q.sb("ones", [P, P])
        r0 = q.sb("r0", [P, 384])
        r1 = q.sb("r1", [P, 384])
        re = q.sb("re", [P, 256])
        raw = q.sb("raw", [P, 5, P])
        rawt = q.sb("rawt", [P, 5, P])
        cols = q.sb("cols", [P, 6])
        bcol = q.sb("bcol", [P, 3, P])
        rows = q.sb("rows", [1, 2, P])
        work = q.sb("work", [P, 6, NS])
        work_i = q.sb("work_i", [P, 6, NS], I32)
        tps = q.ps("tps", [P, 4, P])
        fps = q.ps("fps", [P, 5, 512])
        tps2 = fps[:, 4, 256:384]
        hps = q.ps("hps", [P, 2, 512])

        idx_clear, idx_in = q.sem("idx_clear"), q.sem("idx_in")
        w_in, const_done = q.sem("w_in"), q.sem("const_done")
        vec, act_done = q.sem("vec"), q.sem("act_done")
        wt_ps, wt_sb, fold_ps, col_sb = q.sem("wt_ps"), q.sem("wt_sb"), q.sem("fold_ps"), q.sem("col_sb")
        hist_done, hist_ps = q.sem("hist_done"), q.sem("hist_ps")
        onehot_done, hist_added = q.sem("onehot_done"), q.sem("hist_added")
        zero_done, count_done, he_zeroed = q.sem("zero_done"), q.sem("count_done"), q.sem("he_zeroed")
        tail = NP - N
        full_p = P - 1
        last_c = EC - tail
        block = ctx.enter_context(nc.Block())

        @block.sync
        def _(sp):
            sp.wait_ge(idx_clear, 2)
            sp.nop(nofuse=True)
            for t, a in ((dst_i, w["dst"]), (src_i, w["src"])):
                sp.dma_start(t[0:full_p, :], a[0:full_p * EC].rearrange("(p c) -> p c", p=full_p)).then_inc(idx_in, 16)
                sp.dma_start(t[full_p:P, 0:last_c],
                             a[full_p * EC:N].rearrange("(p c) -> p c", p=1)).then_inc(idx_in, 16)
            def clear(k):
                sp.dma_start(he[bass.ds(k * (UNR * P), UNR * P), :].rearrange("(p r) f -> p (r f)", p=P),
                             wide[:, :]).then_inc(he_zeroed, 16)

            sp.wait_ge(zero_done, 1)
            sp.nop(nofuse=True)
            with sp.Fori(0, TMIN) as k:
                clear(k)
            sp.wait_ge(count_done, 1)
            sp.nop(nofuse=True)
            turns = sp.value_load(g["turns"][0:1, 0:1], min_val=TMIN + 1, max_val=TMAX // UNR)
            with sp.Fori(TMIN, turns) as k:
                clear(k)
            sp.wait_ge(he_zeroed, turns * 16)
            sp.nop(nofuse=True)

        @block.scalar
        def _(act):
            loads = [(g["ne1"][:, :], w["ne_w1"]), (g["ee1"][:, :], w["ee_w1"]), (g["agw2"][:, :], w["agg_w2"]),
                     (r0[:, 0:128], w["ml_w1"][0, 0:128, :]), (r0[:, 128:256], w["ml_w1"][0, 256:384, :]),
                     (r0[:, 256:384], w["agg_w1"]),
                     (r1[:, 0:128], w["ml_w1"][1, 0:128, :]), (r1[:, 128:256], w["ml_w1"][1, 256:384, :]),
                     (r1[:, 256:384], w["agg_w1"]),
                     (re[:, 0:128], w["ml_w1"][0, 128:256, :]), (re[:, 128:256], w["ml_w1"][1, 128:256, :]),
                     (raw[:, 0, :], w["ne_w2"]), (raw[:, 1, :], w["agg_w2"]), (raw[:, 2, :], w["ee_w2"]),
                     (raw[:, 3, :], w["ml_w2"][0]), (raw[:, 4, :], w["ml_w2"][1])]
            columns = [w["ne_b2"], w["agg_b2"], w["ee_b2"], w["ml_b2"][0], w["ml_b2"][1], w["agg_b1"]]
            loads += [(cols[:, k:k + 1], c.rearrange("(p a) -> p a", a=1)) for k, c in enumerate(columns)]
            loads += [(g["ne_b1"][:, :], w["ne_b1"].rearrange("(p a) -> p a", a=1)),
                      (g["ee_b1"][:, :], w["ee_b1"].rearrange("(p a) -> p a", a=1)),
                      (rows[:, 0, :], w["ml_b1"][0:1, :]), (rows[:, 1, :], w["ml_b1"][1:2, :]),
                      (g["agb2"][0:1, :], w["agg_b2"].rearrange("(a n) -> a n", a=1))]
            for to, frm in loads:
                act.dma_start(to, frm).then_inc(w_in, 16)
            act.wait_ge(w_in, 16 * len(loads))
            act.wait_ge(const_done, 5)
            for k in range(3):
                nc.scalar.activation(bcol[:, k, :], ones[:, :], ACT.Copy, scale=cols[:, k:k + 1]).then_inc(col_sb, 1)
            act.wait_ge(wt_ps, 1)
            nc.scalar.activation(rawt[:, 0:4, :], tps[:, :, :], ACT.Copy).then_inc(wt_sb, 1)
            nc.scalar.activation(rawt[:, 4, :], tps2, ACT.Copy).then_inc(wt_sb, 1)
            act.wait_ge(fold_ps, 1)
            nc.scalar.activation(g["f0"][:, :], fps[:, 0, 0:384], ACT.Copy)
            nc.scalar.activation(g["f1"][:, :], fps[:, 1, 0:384], ACT.Copy)
            nc.scalar.activation(g["fe"][:, :], fps[:, 2, 0:256], ACT.Copy)
            nc.scalar.activation(g["fq"][:, 0, :], fps[:, 2, 256:384], ACT.Copy)
            nc.scalar.activation(g["fq"][:, 1, :], fps[:, 2, 384:512], ACT.Copy)
            nc.scalar.activation(g["ebias"][:, :], fps[:, 3, 0:256], ACT.Copy)
            nc.scalar.activation(g["crow"][:, 0, :], fps[0:1, 3, 256:384], ACT.Copy)
            nc.scalar.activation(g["crow"][:, 1, :], fps[0:1, 3, 384:512], ACT.Copy)
            for t in range(4):
                nc.scalar.activation(g["agb2b"][:, t, :], fps[:, 4, 128:256], ACT.Copy)
            for k in range(2):
                nc.scalar.activation(g["pbias"][:, k:k + 1], fps[:, 4, k:k + 1], ACT.Identity,
                                     bias=cols[:, 5:6]).then_inc(act_done, 1)

        @block.tensor
        def _(pe):
            pe.wait_ge(w_in, 16 * 27)
            pe.wait_ge(const_done, 5)
            for k in range(4):
                nc.tensor.transpose(tps[:, k, :], raw[:, k, :], g["ident"][:, :])
            nc.tensor.transpose(tps2, raw[:, 4, :], g["ident"][:, :]).then_inc(wt_ps, 1)
            pe.wait_ge(wt_sb, 2)
            pe.wait_ge(col_sb, 3)

            def mm(out, a, b, start=True, stop=True):
                return nc.tensor.matmul(out, a, b, start=start, stop=stop)

            mm(fps[:, 0, 0:384], rawt[:, 0, :], r0[:, :])
            mm(fps[:, 1, 0:384], rawt[:, 1, :], r1[:, :])
            mm(fps[:, 2, 0:256], rawt[:, 2, :], re[:, :])
            mm(fps[:, 2, 256:384], rawt[:, 3, :], r0[:, 256:384])
            mm(fps[:, 2, 384:512], rawt[:, 4, :], r0[:, 256:384])
            for k, (r, b) in enumerate(((r0, 0), (r1, 1))):
                o = fps[:, 3, 128 * k:128 * k + 128]
                mm(o, bcol[:, 2, :], re[:, 128 * k:128 * k + 128], True, False)
                mm(o, bcol[:, b, :], r[:, 0:128], False, False)
                mm(o, bcol[:, b, :], r[:, 128:256], False, False)
                mm(o, ones[0:1, :], rows[:, k, :], False, True)
            for k in range(2):
                mm(fps[0:1, 3, 256 + 128 * k:384 + 128 * k], cols[:, 3 + k:4 + k], r0[:, 256:384])
            mm(fps[:, 4, 0:1], r0[:, 256:384], cols[:, 0:1])
            mm(fps[:, 4, 1:2], r0[:, 256:384], cols[:, 1:2])
            mm(fps[:, 4, 128:256], ones[0:1, :], g["agb2"][0:1, :]).then_inc(fold_ps, 1)
            def add_columns(m, first, last):
                for k in range(4):
                    pe.wait_ge(onehot_done, m * 4 + k + 1)
                    for j in range(2):
                        ins = mm(hps[:, j, 0:NS], g["identb"][:, :], onehot[:, k, j, :], first and k == 0, last and k == 3)
                    ins.then_inc(hist_added, 1)

            add_columns(0, True, False)
            with pe.Fori(1, EC // 4 - 1) as m:
                add_columns(m, False, False)
            add_columns(EC // 4 - 1, False, True)
            pe.wait_ge(hist_done, 1)
            pe.wait_ge(act_done, 2)
            mm(fps[:, 2, 0:NS], lower[:, :], g["run_d"][:, :])
            mm(fps[:, 3, 0:NS], lower[:, :], g["run_s"][:, :])
            mm(fps[:, 0, 0:NS], ones[:, :], g["run_d"][:, :])
            mm(fps[:, 1, 0:NS], ones[:, :], g["run_s"][:, :]).then_inc(hist_ps, 1)

        @block.gpsimd
        def _(pool):
            made = q.sem("made")
            nc.gpsimd.memset(dst_i[:, :], NP - 1).then_inc(idx_clear, 1)
            nc.gpsimd.memset(src_i[:, :], NP - 1).then_inc(idx_clear, 1)
            nc.gpsimd.iota(tmp_i[:, :], pattern=[[1, NS]], base=0, channel_multiplier=0).then_inc(const_done, 1)
            nc.gpsimd.memset(g["ident"][:, :], 0.0).then_inc(made, 1)
            nc.gpsimd.memset(g["identb"][:, :], 0.0).then_inc(made, 1)
            nc.gpsimd.memset(lower[:, :], 1.0).then_inc(made, 1)
            nc.gpsimd.memset(ones[:, :], 1.0).then_inc(const_done, 1)
            pool.wait_ge(made, 3)
            for m in (g["ident"], g["identb"]):
                nc.gpsimd.affine_select(out=m[:, :], in_=m[:, :], compare_op=ALU.not_equal, fill=1.0, base=0,
                                        pattern=[[-1, P]], channel_multiplier=1).then_inc(const_done, 1)
            nc.gpsimd.affine_select(out=lower[:, :], in_=lower[:, :], compare_op=ALU.is_gt, fill=0.0, base=0,
                                    pattern=[[1, P]], channel_multiplier=-1).then_inc(const_done, 1)
            nc.gpsimd.memset(wide[:, :], 0.0).then_inc(zero_done, 1)
            nc.gpsimd.memset(g["onecol"][:, :], 1.0)
            nc.gpsimd.memset(g["onesrow"][:, :], 1.0)
            nc.gpsimd.memset(g["zrow"][:, :], 0.0)
            nc.gpsimd.memset(g["zwide"][:, :], 0.0)
            nc.gpsimd.memset(g["xlast"][:, :, :], 0.0)
            nc.gpsimd.memset(g["ealast"][:, :, :, :], 0.0)
            nc.gpsimd.memset(g["meta_d"][:, :, 3:4], 0)
            nc.gpsimd.memset(g["meta_s"][:, :, 2:4], 0).then_inc(made, 1)
            pool.wait_ge(made, 4)

        @block.vector
        def _(dve):
            v = nc.vector
            n = [0]

            def step(ins):
                n[0] += 1
                ins.then_inc(vec, 1)
                dve.wait_ge(vec, n[0])

            dve.wait_ge(const_done, 1)
            v.tensor_copy(iotah[:, :], tmp_i[:, :])
            step(v.tensor_copy(g["iota0"][:, :], tmp_i[:, :]))
            v.tensor_scalar(g["iota1"][:, :], g["iota0"][:, 0:SUB], 1.0, None, ALU.add)
            step(v.tensor_scalar(g["iota1b"][:, :], g["iota0"][:, 0:SUB], 1.0, None, ALU.add))
            dve.wait_ge(idx_in, 64)
            work_c = q.sb("work_c", [P, EC], I32)
            for m, own, other, blk in (("meta_d", dst_i, src_i, "blk_d"), ("meta_s", src_i, dst_i, "blk_s")):
                step(v.tensor_scalar(work_c[:, :], own[:, :], SUB.bit_length() - 1, None, ALU.logical_shift_right))
                v.tensor_copy(g[blk][:, :], work_c[:, :])
                v.tensor_copy(g[m][:, :, 0], other[:, :])
                step(v.scalar_tensor_tensor(work_c[:, :], work_c[:, :], float(-SUB), own[:, :], ALU.mult, ALU.add))
                step(v.tensor_scalar(g[m][:, :, 1], work_c[:, :], 1.0, None, ALU.add))
            step(v.tensor_copy(g["meta_d"][:, :, 2], g["meta_d"][:, :, 1]))
            def mark_columns(m):
                for k in range(4):
                    if positive(m * 4 + k - 3):
                        dve.wait_ge(hist_added, m * 4 + k - 3)
                    for j, blk in enumerate(("blk_d", "blk_s")):
                        ins = v.tensor_scalar(onehot[:, k, j, :], iotah[:, :], g[blk][:, bass.ds(m * 4 + k, 1)], None, ALU.is_equal)
                    ins.then_inc(onehot_done, 1)

            mark_columns(0)
            with dve.Fori(1, EC // 4) as m:
                mark_columns(m)
            dve.wait_ge(hist_added, EC)
            v.tensor_copy(g["run_d"][:, :], hps[:, 0, 0:NS])
            v.tensor_copy(g["run_s"][:, :], hps[:, 1, 0:NS]).then_inc(hist_done, 1)
            dve.wait_ge(hist_ps, 1)
            step(v.tensor_copy(work[:, 0, :], fps[:, 0, 0:NS]))
            step(v.tensor_tensor(work_i[:, 0, :], work[:, 0, :], fps[:, 1, 0:NS], ALU.add))
            step(v.tensor_scalar(work_i[:, 1, :], work_i[:, 0, :], 8, None, ALU.logical_shift_right))
            step(v.tensor_scalar(work[:, 1, :], work_i[:, 1, :], 1.0, None, ALU.add))
            v.memset(work[:, 3, :], 1.0)
            step(v.memset(work[:, 5, :], 0.0))
            step(v.tensor_tensor_scan(work[:, 2, :], work[:, 3, :], work[:, 1, :], 0.0, ALU.mult, ALU.add))
            step(v.tensor_tensor(work[:, 4, :], work[:, 2, :], work[:, 1, :], ALU.subtract))
            step(v.scalar_tensor_tensor(g["run_d"][:, :], work[:, 4, :], float(2 * P), fps[:, 2, 0:NS], ALU.mult, ALU.add))
            step(v.scalar_tensor_tensor(work[:, 3, :], work[:, 4, :], float(2 * P), fps[:, 3, 0:NS], ALU.mult, ALU.add))
            step(v.tensor_tensor(g["run_s"][:, :], work[:, 3, :], work[:, 0, :], ALU.add))
            step(v.tensor_copy(work_i[:, 2, :], work[:, 2, :]))
            step(v.tensor_scalar(work_i[:, 3, 0:1], work_i[:, 2, NS - 1:NS], float(PAIRS - 1), None, ALU.add))
            step(v.tensor_scalar(work_i[:, 4, 0:1], work_i[:, 3, 0:1], PAIRS.bit_length() - 1, None,
                                 ALU.logical_shift_right))
            v.tensor_copy(g["turns"][:, 0:1], work_i[:, 4, 0:1])
            v.tensor_scalar(g["turns"][:, 1:2], work_i[:, 4, 0:1], -1.0, None, ALU.add)
            step(v.tensor_scalar(work_i[:, 2, NS - 1:NS], work_i[:, 4, 0:1], float(PAIRS), None, ALU.mult))
            v.tensor_copy(g["ends"][:, 1:NS + 1], work_i[:, 2, :])
            step(v.memset(g["ends"][:, 0:1], 0))
            step(v.tensor_scalar(work_i[:, 5, 0:NB], work_i[:, 2, 1:NS:2], float(GRP // 2 - 1), None, ALU.add))
            v.memset(g["gends"][:, 0:1], 0)
            step(v.tensor_scalar(g["gends"][:, 1:NB + 1], work_i[:, 5, 0:NB], (GRP // 2).bit_length() - 1, None,
                                 ALU.logical_shift_right))
            step(v.tensor_scalar(work_i[:, 0, 0:NB], g["ends"][:, 1:NS:2], BITS, None, ALU.logical_shift_left))
            step(v.tensor_scalar(work_i[:, 1, 0:NB], g["ends"][:, 2:NS + 1:2], 2 * BITS, None, ALU.logical_shift_left))
            step(v.tensor_tensor(work_i[:, 3, 0:NB], work_i[:, 0, 0:NB], work_i[:, 1, 0:NB], ALU.bitwise_or))
            step(v.tensor_tensor(g["bounds"][:, :], work_i[:, 3, 0:NB], g["ends"][:, 0:NS:2], ALU.bitwise_or))
            v.tensor_copy(work[:, 5, 0:1], work[:, 4, 0:1]).then_inc(count_done, 1)
            dve.wait_ge(count_done, 1)


def dense_phase(nc, w, g, he, a_tab, br_tab):
    with ExitStack() as ctx:
        q = Pools(nc, ctx)
        x = [q.sb(f"x{s}", [P, 4, P]) for s in range(2)]
        ea = [q.sb(f"ea{s}", [P, 4, FE]) for s in range(2)]
        stats = q.sb("stats", [P, 4, 6])
        mv = q.sb("mv", [P, 2, 4, 2])
        rstd = q.sb("rstd", [P, 2, 4])
        var, std = q.sb("var", [P, 2, 4]), q.sb("std", [P, 2, 4])
        var_done, std_done = q.sem("var_done"), q.sem("std_done")
        shift = q.sb("shift", [P, 2, 4])
        h = q.sb("h", [P, 4, P])
        ht = q.sb("ht", [P, 512])
        eat = q.sb("eat", [FE, 512])
        ret = q.sb("ret", [P, 512])
        a_sb = [q.sb(f"a_sb{s}", [P, 4, P]) for s in range(2)]
        br_sb = [q.sb(f"br_sb{s}", [P, 2, 512]) for s in range(2)]
        rec_d = [q.sb(f"rec_d{s}", [P, 4, REC]) for s in range(2)]
        rec_s = [q.sb(f"rec_s{s}", [P, 4, REC]) for s in range(2)]
        junk = q.sb("junk", [P, 2, NS])
        warm = q.sb("warm", [P, 1])
        posf = q.sb("posf", [P, 8])
        pos = [q.sb(f"pos{s}", [P, 8], I32) for s in range(2)]
        ht_ps = q.ps("ht_ps", [P, 512])
        r1_ps = q.ps("r1_ps", [P, 512])
        eat_ps = q.ps("eat_ps", [FE, 512])
        re_ps = q.ps("re_ps", [P, 512])
        ab_ps = q.ps("ab_ps", [P, 2, 2, 256])
        e_ps = q.ps("e_ps", [P, 2, 2, 256])

        x_in = [q.sem(f"x_in{s}") for s in range(2)]
        ea_in = [q.sem(f"ea_in{s}") for s in range(2)]
        ealast_in = [q.sem(f"ealast_in{s}") for s in range(2)]
        xlast_in = q.sem("xlast_in")
        a_out = [q.sem(f"a_out{s}") for s in range(2)]
        br_out = [q.sem(f"br_out{s}") for s in range(2)]
        sd_out = [q.sem(f"sd_out{s}") for s in range(2)]
        ss_out = [q.sem(f"ss_out{s}") for s in range(2)]
        stats_done, aggr_done, rstd_done = q.sem("stats_done"), q.sem("aggr_done"), q.sem("rstd_done")
        shift_done, norm_done = q.sem("shift_done"), q.sem("norm_done")
        ht_t, ht_c, r1_m, r1_c = q.sem("ht_t"), q.sem("ht_c"), q.sem("r1_m"), q.sem("r1_c")
        eat_t, eat_c, re_m, re_c = q.sem("eat_t"), q.sem("eat_c"), q.sem("re_m"), q.sem("re_c")
        ab_m, ab_c, e_m, e_c = q.sem("ab_m"), q.sem("ab_c"), q.sem("e_m"), q.sem("e_c")
        rank, pos_done, meta_done, recs_done = q.sem("rank"), q.sem("pos_done"), q.sem("meta_done"), q.sem("recs_done")

        x_v = w["x"]
        ea_v = w["ea"][0:(P - 1) * EC, :].rearrange("(p c) f -> p c f", p=P - 1)
        a_v = a_tab.rearrange("(i t p) f -> i p t f", t=4, p=P)
        br_v = br_tab.rearrange("(i k) p f -> i p k f", k=2)
        last_c = EC - (NP - N)
        m_full = last_c // 8
        assert last_c % 8 == 0 and IT % 2 == 0

        def turns(eng, body):
            for s in range(2):
                body(0, s, ea[s], ea_in[s], 1, x[s])
            with eng.Fori(1, m_full) as m:
                for s in range(2):
                    body(m, s, ea[s], ea_in[s], m + 1, x[s])
            with eng.Fori(m_full, IT // 2 - 1) as m:
                for s in range(2):
                    body(m, s, g["ealast"][:, s], ealast_in[s], (m - m_full) * 2 + 2, x[s])
            m = IT // 2 - 1
            for s in range(2):
                body(m, s, g["ealast"][:, s], ealast_in[s], (m - m_full) * 2 + 2, x[s] if s == 0 else g["xlast"])

        def following(m, s):
            if isinstance(m, int) and m == IT // 2 - 1:
                return (m, 1, g["xlast"]) if s == 0 else None
            return (m, 1, x[1]) if s == 0 else (m + 1, 0, x[0])

        block = ctx.enter_context(nc.Block())

        @block.sync
        def _(sp):
            def store(m, s):
                i = m * 2 + s
                sp.wait_ge(ab_c, i * 4 + 4)
                sp.nop(nofuse=True)
                sp.dma_start(a_v[bass.ds(i, 1)].rearrange("a p t f -> (a p) t f"), a_sb[s][:, :, :]).then_inc(a_out[s], 16)
                sp.dma_start(br_v[bass.ds(i, 1)].rearrange("a p k f -> (a p) k f"), br_sb[s][:, :, :]).then_inc(br_out[s], 16)

            def body(m, s, ea_t, ea_sem, _, x_t):
                i = m * 2 + s
                if positive(i * 4 - 4):
                    sp.wait_ge(norm_done, i * 4 - 4)
                    sp.nop(nofuse=True)
                if x_t is x[s]:
                    sp.dma_start(x_t[:, :, :], x_v[bass.ds(i * 512, 512), :].rearrange("(t p) f -> p t f", p=P)).then_inc(x_in[s], 16)
                else:
                    at, part = i * 512, N - i * 512 - 256
                    sp.dma_start(x_t[:, 0:2, :], x_v[at:at + 256, :].rearrange("(t p) f -> p t f", p=P)).then_inc(xlast_in, 16)
                    sp.dma_start(x_t[0:part, 2, :], x_v[at + 256:N, :]).then_inc(xlast_in, 16)
                if positive(i - 1):
                    sp.wait_ge(eat_t, i - 1)
                    sp.nop(nofuse=True)
                if ea_sem is ea_in[s]:
                    sp.dma_start(ea_t[0:P - 1, :, :], ea_v[:, bass.ds(i * 4, 4), :]).then_inc(ea_sem, 16)
                    sp.dma_start(ea_t[P - 1:P, :, :], w["ea"][bass.ds(i * 4 + (P - 1) * EC, 4), :].rearrange("(p c) f -> p c f", p=1)).then_inc(ea_sem, 16)
                else:
                    sp.dma_start(ea_t[0:112, :, :], ea_v[0:112, bass.ds(i * 4, 4), :]).then_inc(ea_sem, 16)
                    sp.dma_start(ea_t[112:P - 1, :, :], ea_v[112:P - 1, bass.ds(i * 4, 4), :]).then_inc(ea_sem, 16)
                if s == 1:
                    store(m, 0)
                elif not (isinstance(m, int) and m == 0):
                    store(m - 1, 1)

            turns(sp, body)
            store(IT // 2 - 1, 1)
            for s in range(2):
                sp.wait_ge(a_out[s], 16 * (IT // 2))
                sp.nop(nofuse=True)
                sp.wait_ge(br_out[s], 16 * (IT // 2))
                sp.nop(nofuse=True)

        @block.scalar
        def _(act):
            nc.scalar.activation(warm[:, :], g["iota0"][:, 0:1], ACT.Sqrt)

            def root(m, s):
                i = m * 2 + s
                act.wait_ge(var_done, i + 1)
                nc.scalar.activation(std[:, s, :], var[:, s, :], ACT.Sqrt).then_inc(std_done, 1)

            def normalise(m, s, x_t):
                i = m * 2 + s
                act.wait_ge(shift_done, i + 1)
                if positive(i):
                    act.wait_ge(ht_t, i)
                for t in range(4):
                    nc.scalar.activation(h[:, t, :], x_t[:, t, :], ACT.Relu, bias=shift[:, s, t:t + 1],
                                         scale=rstd[:, s, t:t + 1]).then_inc(norm_done, 1)

            root(0, 0)
            normalise(0, 0, x[0])

            def body(m, s, *_):
                i, after = m * 2 + s, following(m, s)
                act.wait_ge(ht_t, i + 1)
                nc.scalar.activation(ht[:, :], ht_ps[:, :], ACT.Copy).then_inc(ht_c, 1)
                act.wait_ge(eat_t, i + 1)
                nc.scalar.activation(eat[:, :], eat_ps[:, :], ACT.Copy).then_inc(eat_c, 1)
                if after:
                    root(after[0], after[1])
                act.wait_ge(r1_m, i + 1)
                if positive(m * 16):
                    act.wait_ge(br_out[s], m * 16)
                nc.scalar.activation(br_sb[s][:, :, 256:512], r1_ps[:, :].rearrange("p (k n) -> p k n", k=2),
                                     ACT.Relu, bias=g["ne_b1"][:, 0:1]).then_inc(r1_c, 1)
                act.wait_ge(re_m, i + 1)
                if positive(i * 2):
                    act.wait_ge(e_m, i * 2)
                nc.scalar.activation(ret[:, :], re_ps[:, :], ACT.Relu, bias=g["ee_b1"][:, 0:1]).then_inc(re_c, 1)
                if positive(m * 16):
                    act.wait_ge(a_out[s], m * 16)
                for k in range(2):
                    act.wait_ge(ab_m, i * 2 + k + 1)
                    nc.scalar.activation(a_sb[s][:, 2 * k:2 * k + 2, :], ab_ps[:, k, :, 0:128], ACT.Copy).then_inc(ab_c, 1)
                    nc.scalar.activation(br_sb[s][:, k, 0:256].rearrange("p (h f) -> p h f", h=2),
                                         ab_ps[:, k, :, 128:256], ACT.Copy).then_inc(ab_c, 1)
                if after:
                    normalise(*after)
                if positive(m * 64):
                    act.wait_ge(sd_out[s], m * 64)
                    act.wait_ge(ss_out[s], m * 64)
                act.wait_ge(e_m, i * 2 + 2)
                for rec, done in ((rec_d[s], e_c), (rec_s[s], recs_done)):
                    for at, c in ((0, 0), (E1AT, 128)):
                        nc.scalar.activation(rec[:, :, at:at + 128], e_ps[:, :, :, c:c + 128].rearrange("p k h f -> p (k h) f"),
                                             ACT.Copy).then_inc(done, 1)

            turns(act, body)

        @block.tensor
        def _(pe):
            def body(m, s, ea_t, ea_sem, ea_n, x_t):
                i = m * 2 + s
                pe.wait_ge(norm_done, i * 4 + 4)
                for t in range(4):
                    last = nc.tensor.transpose(ht_ps[:, t * P:t * P + P], h[:, t, :], g["ident"][:, :])
                last.then_inc(ht_t, 1)
                pe.wait_ge(ea_sem, ea_n * (32 if ea_sem is ea_in[s] else 16))
                pe.nop(nofuse=True)
                for t in range(4):
                    last = nc.tensor.transpose(eat_ps[:, t * P:t * P + P], ea_t[:, t, :], g["ident"][:, :])
                last.then_inc(eat_t, 1)
                pe.wait_ge(ht_c, i + 1)
                nc.tensor.matmul(r1_ps[:, :], g["ne1"][:, :], ht[:, :], start=True, stop=True).then_inc(r1_m, 1)
                pe.wait_ge(eat_c, i + 1)
                nc.tensor.matmul(re_ps[:, :], g["ee1"][:, :], eat[:, :], start=True, stop=True).then_inc(re_m, 1)
                pe.wait_ge(r1_c, i + 1)
                if positive(i * 4):
                    pe.wait_ge(ab_c, i * 4)
                for k in range(2):
                    for hh in range(2):
                        last = nc.tensor.matmul(ab_ps[:, k, hh, :], br_sb[s][:, k, 256 + hh * P:384 + hh * P],
                                                g["f0"][:, 0:256], start=True, stop=True)
                    last.then_inc(ab_m, 1)
                pe.wait_ge(re_c, i + 1)
                if positive(i * 2):
                    pe.wait_ge(recs_done, i * 2)
                for k in range(2):
                    for hh in range(2):
                        t = 2 * k + hh
                        nc.tensor.matmul(e_ps[:, k, hh, :], g["onesrow"][0:1, :], g["ebias"][0:1, :], start=True, stop=False)
                        last = nc.tensor.matmul(e_ps[:, k, hh, :], ret[:, t * P:t * P + P], g["fe"][:, :],
                                                start=False, stop=True)
                    last.then_inc(e_m, 1)

            turns(pe, body)

        @block.vector
        def _(dve):
            v = nc.vector

            def statistics(m, s, x_t):
                i = m * 2 + s
                if x_t is x[s]:
                    dve.wait_ge(x_in[s], m * 16 + 16)
                else:
                    dve.wait_ge(xlast_in, 32)
                if positive(i * 4):
                    dve.wait_ge(aggr_done, i * 4)
                for t in range(4):
                    v.bn_stats(stats[:, t, :], x_t[:, t, :]).then_inc(stats_done, 1)
                dve.wait_ge(stats_done, i * 4 + 4)
                if positive(i - 1):
                    dve.wait_ge(shift_done, i - 1)
                dve.nop(nofuse=True)
                for t in range(4):
                    v.bn_aggr(mv[:, s, t, :], stats[:, t, :]).then_inc(aggr_done, 1)
                dve.wait_ge(aggr_done, i * 4 + 4)
                v.tensor_scalar(var[:, s, :], mv[:, s, :, 1], EPS, None, ALU.add).then_inc(var_done, 1)

            def scale(m, s, _):
                i = m * 2 + s
                dve.wait_ge(std_done, i + 1)
                if positive(i * 4 - 4):
                    dve.wait_ge(norm_done, i * 4 - 4)
                v.reciprocal(rstd[:, s, :], std[:, s, :]).then_inc(rstd_done, 1)
                dve.wait_ge(rstd_done, i + 1)
                v.scalar_tensor_tensor(shift[:, s, :], mv[:, s, :, 0], -1.0, rstd[:, s, :], ALU.mult, ALU.mult).then_inc(shift_done, 1)

            statistics(0, 0, x[0])
            scale(0, 0, x[0])

            def body(m, s, *_):
                i, after = m * 2 + s, following(m, s)
                if after:
                    statistics(*after)
                if positive(i):
                    dve.wait_ge(pos_done, i)
                for t in range(4):
                    if t == 2 and after:
                        scale(*after)
                    for j, (run, blk) in enumerate((("run_d", "blk_d"), ("run_s", "blk_s"))):
                        if positive(i * 16 + t * 4 + j - 1):
                            dve.wait_ge(rank, i * 16 + t * 4 + j - 1)
                        v.scalar_tensor_tensor(junk[:, j, :], g["iota0"][:, :], g[blk][:, bass.ds(i * 4 + t, 1)], g[run][:, :],
                                               ALU.is_equal, ALU.mult, accum_out=posf[:, 4 * j + t:4 * j + t + 1]).then_inc(rank, 1)
                    for j, (run, blk) in enumerate((("run_d", "blk_d"), ("run_s", "blk_s"))):
                        v.scalar_tensor_tensor(g[run][:, :], g["iota0"][:, :], g[blk][:, bass.ds(i * 4 + t, 1)], g[run][:, :],
                                               ALU.is_equal, ALU.add).then_inc(rank, 1)
                if positive(m * 64):
                    dve.wait_ge(sd_out[s], m * 64)
                if positive(m * 64):
                    dve.wait_ge(ss_out[s], m * 64)
                dve.wait_ge(rank, i * 16 + 16)
                v.tensor_copy(pos[s][:, :], posf[:, :]).then_inc(pos_done, 1)
                v.tensor_copy(rec_d[s][:, :, META:META + 4].bitcast(I32), g["meta_d"][:, bass.ds(i * 4, 4), :]).then_inc(meta_done, 1)
                v.tensor_copy(rec_s[s][:, :, META:META + 4].bitcast(I32), g["meta_s"][:, bass.ds(i * 4, 4), :]).then_inc(meta_done, 1)

            turns(dve, body)

        @block.gpsimd
        def _(pool):
            def body(m, s, *_):
                i = m * 2 + s
                pool.wait_ge(e_c, i * 2 + 2)
                pool.wait_ge(meta_done, i * 2 + 2)
                pool.nop(nofuse=True)
                for t in range(4):
                    pool.indirect_dma_start(he[:, :], bass.IndirectOffsetOnAxis(ap=pos[s][:, t:t + 1], axis=0),
                                            rec_d[s][:, t, :], None).then_inc(sd_out[s], 16)
                pool.wait_ge(recs_done, i * 2 + 2)
                pool.nop(nofuse=True)
                for t in range(4):
                    pool.indirect_dma_start(he[:, :], bass.IndirectOffsetOnAxis(ap=pos[s][:, 4 + t:5 + t], axis=0),
                                            rec_s[s][:, t, :], None).then_inc(ss_out[s], 16)

            turns(pool, body)
            for s in range(2):
                pool.wait_ge(sd_out[s], 64 * (IT // 2))
                pool.wait_ge(ss_out[s], 64 * (IT // 2))


def edge_phase(nc, g, he, layer, a_tab, br_tab, out_a, out_br, out):
    msgs = layer < 2
    tag = f"l{layer}_"
    with ExitStack() as ctx:
        q = Pools(nc, ctx)
        width = {0: 132, 1: 132, 2: 4}[layer]
        col0 = {0: 0, 1: META, 2: META}[layer]
        meta_at = {0: 128, 1: 0, 2: 0}[layer]
        term_at = {0: 0, 1: 4}.get(layer)
        key = 1 if msgs else 2
        brw = 512 if msgs else 256
        ch = q.sb(tag + "ch", [P, UNR, width])
        nbr = q.sb(tag + "nbr", [P, UNR, P])
        metaf = q.sb(tag + "metaf", [P, UNR, 4])
        ohf = q.sb(tag + "ohf", [P, 2, SUB])
        ohb = q.sb(tag + "ohb", [P, 2, SUB], BF16)
        oht = q.sb(tag + "oht", [P, 2, P])
        pre = q.sb(tag + "pre", [P, 2, P])
        msg = q.sb(tag + "msg", [P, 2, P])
        br = q.sb(tag + "br", [P, 5, brw])
        st = q.sb(tag + "st", [P, BLK])
        deg = q.sb(tag + "deg", [1, BLK])
        rt = q.sb(tag + "rt", [P, BLK])
        ra = q.sb(tag + "ra", [P, 8, 2, P])
        rb = q.sb(tag + "rb", [P, 8, 512])
        oht_ps = q.ps(tag + "oht_ps", [P, 8, P], BF16)
        pre_ps = q.ps(tag + "pre_ps", [P, 2, P])
        s_ps = q.ps(tag + "s_ps", [P, 2, 512])
        deg_ps = q.ps(tag + "deg_ps", [1, 2, 512])
        r_ps = q.ps(tag + "r_ps", [P, 512])
        o_ps = q.ps(tag + "o_ps", [P, 2, 256])

        def sem(name):
            return q.sem(tag + name)

        ch_in, br_in, res_out = sem("ch_in"), sem("br_in"), sem("res_out")
        res2_out, stored = sem("res2_out"), sem("stored")
        nbr_in = g["nbr_in"]
        metaf_done, sum_done, pre_done = sem("metaf_done"), sem("sum_done"), sem("pre_done")
        ohb_done, ohf_done, deg_done = sem("ohb_done"), sem("ohf_done"), sem("deg_done")
        oht_t, oht_c, look_done, msg_done, s_done = sem("oht_t"), sem("oht_c"), sem("look_done"), sem("msg_done"), sem("s_done")
        block_summed, arrived = sem("block_summed"), sem("arrived")
        st_c, r_m, rt_c, o_m, o_c = sem("st_c"), sem("r_m"), sem("rt_c"), sem("o_m"), sem("o_c")

        s0, msg0, pre0, t0 = 3, 2, 2, 1
        ohf0 = 2 if msgs else PAIRS
        used = sum_done if msgs else ohf_done
        block = ctx.enter_context(nc.Block())
        he_v = he.rearrange("(c p) f -> p c f", p=P)

        @block.sync
        def _(sp):
            def load_block(b):
                if positive(b * 16):
                    sp.wait_ge(br_in, b * 16)
                    sp.nop(nofuse=True)
                if positive(b - 4):
                    sp.wait_ge(r_m, b - 4)
                    sp.nop(nofuse=True)
                sp.dma_start(br[:, bass.ds(b % 5, 1), :].rearrange("p a f -> p (a f)"),
                             br_tab[bass.ds(b, 1)].rearrange("a p f -> (a p) f")).then_inc(br_in, 16)

            def load_chunks(b):
                first = 0 if isinstance(b, int) and b == 0 else sp.value_load(g["gends"][0:1, bass.ds(b, 1)], min_val=1, max_val=TMAX // GRP - 1)
                end = sp.value_load(g["gends"][0:1, bass.ds(b + 1, 1)], min_val=1, max_val=TMAX // GRP)
                with sp.Fori(first, end) as k:
                    sp.wait_ge(ch_in, k * 16)
                    sp.nop(nofuse=True)
                    sp.wait_ge(used, k * (GRP // 2) + GRP // 2)
                    sp.nop(nofuse=True)
                    sp.dma_start(ch[:, bass.ds((k % (UNR // GRP)) * GRP, GRP), :],
                                 he_v[:, bass.ds(k * GRP, GRP), col0:col0 + width]).then_inc(ch_in, 16)

            sp.sem_inc(stored, PRIME)

            def store(b):
                sp.wait_ge(o_c, b + 1)
                sp.nop(nofuse=True)
                sp.wait_ge(res_out, b * 16)
                sp.nop(nofuse=True)
                if layer == 0:
                    sp.wait_ge(res2_out, b * 16)
                    sp.nop(nofuse=True)
                sp.sem_inc(stored, 1)
                if msgs:
                    sp.dma_start(out_a.rearrange("(b h p) f -> b p h f", h=2, p=P)[bass.ds(b, 1)].rearrange("a p h f -> (a p) h f"),
                                 ra[:, bass.ds(b % 8, 1), :, :].rearrange("p a h f -> p (a h) f")).then_inc(res_out, 16)
                    if layer == 0:
                        sp.dma_start(out_br[bass.ds(b, 1)].rearrange("a p f -> (a p) f"),
                                     rb[:, bass.ds(b % 8, 1), :].rearrange("p a f -> p (a f)")).then_inc(res2_out, 16)
                else:
                    if isinstance(b, int) and b == NB - 1:
                        rest = N - b * BLK
                        sp.dma_start(out[b * BLK:N, :], ra[0:rest, b % 8, 0, :]).then_inc(res_out, 16)
                    else:
                        sp.dma_start(out[bass.ds(b * BLK, BLK), :].rearrange("(h p) f -> p h f", p=P),
                                     ra[:, bass.ds(b % 8, 1), :, :].rearrange("p a h f -> p (a h) f")).then_inc(res_out, 16)

            for b in range(AHEAD):
                load_block(b)
                load_chunks(b)
            for b in range(2):
                load_block(b + AHEAD)
                load_chunks(b + AHEAD)
            with sp.Fori(2, NB - AHEAD) as b:
                load_block(b + AHEAD)
                load_chunks(b + AHEAD)
                store(b - 2)
            for b in range(NB - AHEAD - 2, NB):
                store(b)
            sp.wait_ge(res_out, 16 * NB)
            sp.nop(nofuse=True)
            if layer == 0:
                sp.wait_ge(res2_out, 16 * NB)
                sp.nop(nofuse=True)

        @block.gpsimd
        def _(pool):
            turns = pool.value_load(g["turns"][0:1, 0:1], min_val=2, max_val=TMAX // UNR)
            free, free0 = (pre_done, pre0) if msgs else (msg_done, msg0)

            def turn(k, k_later):
                for j in range(PAIRS):
                    p = k * PAIRS + j
                    if j % 2 == 0:
                        pool.wait_ge(ch_in, k * (UNR // GRP * 16) + (j // 2 + 1) * 16)
                        if k_later:
                            pool.wait_ge(free, p - PAIRS + 2 + free0)
                        pool.nop(nofuse=True)
                    for c in (2 * j, 2 * j + 1):
                        pool.indirect_dma_start(nbr[:, c, :], None, a_tab[:, :], bass.IndirectOffsetOnAxis(
                            ap=ch[:, c, meta_at:meta_at + 1].bitcast(I32), axis=0)).then_inc(nbr_in[j], 16)

            turn(0, False)
            with pool.Fori(1, turns) as k:
                turn(k, True)

        @block.vector
        def _(dve):
            v = nc.vector
            dve.sem_inc(used, PAIRS)
            if not msgs:
                dve.sem_inc(arrived, msg0)
            if msgs:
                dve.sem_inc(ohb_done, t0)
                dve.sem_inc(ohf_done, ohf0)
                dve.sem_inc(pre_done, pre0)
            last_turn = dve.value_load(g["turns"][0:1, 1:2], min_val=1, max_val=TMAX // UNR - 1)

            earlier = (last_turn + 1) * layer if layer else 0

            def prepare(k, j):
                p, c = k * PAIRS + j, 2 * j
                if j % 2 == 0:
                    dve.wait_ge(ch_in, k * (UNR // GRP * 16) + (j // 2 + 1) * 16)
                    v.tensor_copy(metaf[:, c:c + GRP, :], ch[:, c:c + GRP, meta_at:meta_at + 4].bitcast(I32)).then_inc(metaf_done, 1)
                    dve.wait_ge(metaf_done, k * (UNR // GRP) + j // 2 + 1)
                if msgs:
                    dve.wait_ge(deg_done, p + t0)
                    for i in range(2):
                        last = v.tensor_scalar(ohb[:, i, :], g["iota1b"][:, :], metaf[:, c + i, key:key + 1], None, ALU.is_equal)
                    last.then_inc(ohb_done, 1)
                    dve.wait_ge(nbr_in[j], (earlier + k + 1) * 32)
                    v.tensor_tensor(nbr[:, c:c + 2, :], nbr[:, c:c + 2, :], ch[:, c:c + 2, term_at:term_at + P],
                                    ALU.add).then_inc(sum_done, 1)
                else:
                    dve.wait_ge(nbr_in[j], (earlier + k + 1) * 32)
                    dve.sem_inc(arrived, 1)

            def select(k, j):
                p, c = k * PAIRS + j, 2 * j
                dve.wait_ge(s_done, p + s0)
                for i in range(2):
                    last = v.tensor_scalar(ohf[:, i, :], g["iota1"][:, :], metaf[:, c + i, key:key + 1], None, ALU.is_equal)
                last.then_inc(ohf_done, 1)

            def add_own(k, j):
                p, c = k * PAIRS + j, 2 * j
                dve.wait_ge(look_done, p + 1 + t0)
                dve.wait_ge(msg_done, p + msg0)
                dve.wait_ge(sum_done, p + PAIRS + 1)
                v.tensor_tensor(pre[:, :, :], pre_ps[:, :, :], nbr[:, c:c + 2, :], ALU.add).then_inc(pre_done, 1)

            def turn(k, first, last):
                if first and msgs:
                    prepare(0, 0)
                for j in range(PAIRS):
                    if msgs:
                        if j < PAIRS - 1:
                            prepare(k, j + 1)
                        elif not last:
                            prepare(k + 1, 0)
                        add_own(k, j)
                    else:
                        prepare(k, j)
                    select(k, j)

            if msgs:
                turn(0, True, False)
                with dve.Fori(1, last_turn) as k:
                    turn(k, False, False)
                turn(last_turn, False, True)
            else:
                turn(0, True, False)
                with dve.Fori(1, last_turn + 1) as k:
                    turn(k, False, False)

        def bounds(eng, b):
            word = eng.value_load(g["bounds"][0:1, bass.ds(b, 1)], min_val=0, max_val=(1 << 3 * BITS) - 1)
            p0 = 0 if isinstance(b, int) and b == 0 else eng.snap(word & ((1 << BITS) - 1))
            p1 = eng.snap((word >> BITS) & ((1 << BITS) - 1))
            return p0, p1, eng.snap(word >> 2 * BITS)

        @block.tensor
        def _(pe):
            pe.sem_inc(s_done, s0)
            if msgs:
                pe.sem_inc(oht_t, t0)
                pe.sem_inc(look_done, t0)
                pe.sem_inc(deg_done, t0)

            def clear_sums(b):
                if positive(b - 1):
                    pe.wait_ge(st_c, b - 1)
                nc.tensor.matmul(s_ps[:, b % 2, 0:BLK], g["zrow"][0:1, 0:P], g["zrow"][:, 0:BLK], start=True, stop=False)
                if msgs:
                    nc.tensor.matmul(deg_ps[0:1, b % 2, 0:BLK], g["onecol"][:, :], g["zwide"][:, :], start=True, stop=False)

            def transpose_pair(p, b, h):
                if msgs:
                    pe.wait_ge(ohb_done, p + 1 + t0)
                    for i in range(2):
                        last = nc.tensor.transpose(oht_ps[:, i, :], ohb[:, i, :], g["identb"][:, :])
                    last.then_inc(oht_t, 1)
                    for i in range(2):
                        last = nc.tensor.matmul(deg_ps[0:1, b % 2, h * SUB:(h + 1) * SUB], g["onecol"][:, :], ohb[:, i, :],
                                                start=False, stop=False)
                    last.then_inc(deg_done, 1)

            def look_up(p, b, h):
                if msgs:
                    pe.wait_ge(pre_done, p + pre0)
                    pe.wait_ge(oht_c, p + 1 + t0)
                    for i in range(2):
                        last = nc.tensor.matmul(pre_ps[:, i, :], oht[:, i, :], br[:, b % 5, h * SUB:(h + 1) * SUB],
                                                start=True, stop=True)
                    last.then_inc(look_done, 1)

            def sum_pair(p, b, h):
                pe.wait_ge(ohf_done, p + 1 + ohf0)
                pe.wait_ge(msg_done, p + 1 + msg0)
                for i in range(2):
                    last = nc.tensor.matmul(s_ps[:, b % 2, h * SUB:(h + 1) * SUB], msg[:, i, :], ohf[:, i, :],
                                            start=False, stop=False)
                last.then_inc(s_done, 1)

            def finish_sums(b):
                last = nc.tensor.matmul(s_ps[:, b % 2, 0:BLK], g["zrow"][0:1, 0:P], g["zrow"][:, 0:BLK], start=False, stop=True)
                if msgs:
                    last = nc.tensor.matmul(deg_ps[0:1, b % 2, 0:BLK], g["onecol"][:, :], g["zwide"][:, :], start=False, stop=True)
                last.then_inc(block_summed, 1)

            def update(b):
                pe.wait_ge(st_c, b + 1)
                pe.wait_ge(br_in, b * 16 + 16)
                if msgs:
                    if positive(b):
                        pe.wait_ge(rt_c, b)
                    nc.tensor.matmul(r_ps[:, 0:BLK], g["fq"][:, layer, :], st[:, :], start=True, stop=False)
                    nc.tensor.matmul(r_ps[:, 0:BLK], g["f0" if layer == 0 else "f1"][:, 256:384], br[:, b % 5, 256:512], start=False, stop=False)
                    nc.tensor.matmul(r_ps[:, 0:BLK], g["crow"][0:1, layer, :], deg[0:1, :], start=False, stop=True).then_inc(r_m, 1)
                else:
                    if positive(b):
                        pe.wait_ge(o_c, b)
                    for hh in range(2):
                        nc.tensor.matmul(o_ps[:, hh, 0:P], st[:, hh * P:hh * P + P], g["ident"][:, :], start=True, stop=False)
                        last = nc.tensor.matmul(o_ps[:, hh, 0:P], g["ident"][:, :], br[:, b % 5, hh * P:hh * P + P], start=False, stop=True)
                    last.then_inc(r_m, 1)

            def project(b):
                if msgs:
                    pe.wait_ge(rt_c, b + 1)
                    pe.wait_ge(o_c, b)
                    for hh in range(2):
                        rhs = g["f1"][:, 0:256] if layer == 0 else g["agw2"][:, :]
                        last = nc.tensor.matmul(o_ps[:, hh, 0:256 if layer == 0 else P], rt[:, hh * P:hh * P + P], rhs, start=True, stop=True)
                    last.then_inc(o_m, 1)

            def inner(p0, p1, b, h):
                with pe.If(p1 > p0 + 1):
                    with pe.Fori(p0 + 1, p1) as p:
                        transpose_pair(p, b, h)
                        look_up(p, b, h)
                        sum_pair(p - 1, b, h)

            def one_block(b, prev, prev2):
                p0, p1, p2 = bounds(pe, b)
                pe.wait_ge(br_in, b * 16 + 16)
                clear_sums(b)
                transpose_pair(p0, b, 0)
                if prev2:
                    project(b - 2)
                look_up(p0, b, 0)
                if prev:
                    sum_pair(p0 - 1, b - 1, 1)
                    finish_sums(b - 1)
                inner(p0, p1, b, 0)
                transpose_pair(p1, b, 1)
                if prev:
                    update(b - 1)
                look_up(p1, b, 1)
                sum_pair(p1 - 1, b, 0)
                inner(p1, p2, b, 1)

            one_block(0, False, False)
            one_block(1, True, False)
            with pe.Fori(2, NB) as b:
                one_block(b, True, True)
            b = NB - 1
            total = bounds(pe, b)[2]
            sum_pair(total - 1, b, 1)
            finish_sums(b)
            project(b - 1)
            update(b)
            project(b)

        @block.scalar
        def _(act):
            act.sem_inc(msg_done, msg0)
            if msgs:
                act.sem_inc(oht_c, t0)
            dummy = q.sb(tag + "dummy", [P, 1])
            nc.scalar.activation(dummy[:, :], g["iota0"][:, 0:1], ACT.Relu)

            def copy_onehot(p):
                if msgs:
                    act.wait_ge(oht_t, p + 1 + t0)
                    nc.scalar.activation(oht[:, :, :], oht_ps[:, 0:2, :], ACT.Copy).then_inc(oht_c, 1)

            def message(p):
                if isinstance(p, int) and p < 0:
                    return
                act.wait_ge(s_done, p + s0)
                if msgs:
                    act.wait_ge(pre_done, p + 1 + pre0)
                    nc.scalar.activation(msg[:, :, :], pre[:, :, :], ACT.Relu).then_inc(msg_done, 1)
                else:
                    act.wait_ge(arrived, p + 1 + msg0)
                    nc.scalar.activation(msg[:, :, :], nbr[:, bass.ds((p % PAIRS) * 2, 2), :], ACT.Copy).then_inc(msg_done, 1)

            def copy_sums(b):
                act.wait_ge(block_summed, b + 1)
                if positive(b):
                    act.wait_ge(r_m, b)
                last = nc.scalar.activation(st[:, :], s_ps[:, bass.ds(b % 2, 1), 0:BLK].rearrange("p a f -> p (a f)"), ACT.Copy)
                if msgs:
                    last = nc.scalar.activation(deg[:, :], deg_ps[0:1, bass.ds(b % 2, 1), 0:BLK].rearrange("p a f -> p (a f)"), ACT.Copy)
                last.then_inc(st_c, 1)

            def copy_out(b):
                act.wait_ge(o_m if msgs else r_m, b + 1)
                act.wait_ge(stored, b - 6 + PRIME)
                row = ra[:, bass.ds(b % 8, 1), :, :].rearrange("p a h f -> p (a h) f")
                ins = nc.scalar.activation(row, o_ps[:, :, 0:P], ACT.Copy)
                if layer == 0:
                    ins = nc.scalar.activation(rb[:, bass.ds(b % 8, 1), 0:256].rearrange("p a (h f) -> p (a h) f", h=2),
                                               o_ps[:, :, P:256], ACT.Copy)
                    ins = nc.scalar.activation(rb[:, bass.ds(b % 8, 1), 256:512].rearrange("p a f -> p (a f)"), rt[:, :], ACT.Copy)
                ins.then_inc(o_c, 1)

            def relu_nodes(b):
                if msgs:
                    act.wait_ge(r_m, b + 1)
                    if positive(b):
                        act.wait_ge(o_c, b)
                    nc.scalar.activation(rt[:, :], r_ps[:, 0:BLK], ACT.Relu, bias=g["pbias"][:, layer:layer + 1]).then_inc(rt_c, 1)
                    act.wait_ge(rt_c, b + 1)

            def inner(p0, p1):
                with act.If(p1 > p0 + 1):
                    with act.Fori(p0 + 1, p1) as p:
                        copy_onehot(p)
                        message(p - 1)

            def one_block(b, prev, prev2):
                p0, p1, p2 = bounds(act, b)
                copy_onehot(p0)
                message(p0 - 1)
                if prev2 and msgs:
                    copy_out(b - 2)
                if prev:
                    copy_sums(b - 1)
                inner(p0, p1)
                copy_onehot(p1)
                message(p1 - 1)
                if prev:
                    relu_nodes(b - 1) if msgs else copy_out(b - 1)
                inner(p1, p2)

            one_block(0, False, False)
            one_block(1, True, False)
            with act.Fori(2, NB) as b:
                one_block(b, True, True)
            b = NB - 1
            total = bounds(act, b)[2]
            message(total - 1)
            copy_sums(b)
            if msgs:
                copy_out(b - 1)
                relu_nodes(b)
            copy_out(b)


def norm_phase(nc, w, g, y_tab, h_tab, xh_tab):
    with ExitStack() as ctx:
        q = Pools(nc, ctx)
        x = [q.sb(f"nx{s}", [P, 4, P]) for s in range(2)]
        y = [q.sb(f"ny{s}", [P, 4, P]) for s in range(2)]
        x1 = [q.sb(f"nx1{s}", [P, 4, P]) for s in range(2)]
        h = [q.sb(f"nh{s}", [P, 4, P]) for s in range(2)]
        xh = [q.sb(f"nxh{s}", [P, 4, P]) for s in range(2)]
        stats = q.sb("nstats", [P, 4, 6])
        mv = q.sb("nmv", [P, 2, 4, 2])
        rstd = q.sb("nrstd", [P, 2, 4])
        var, std = q.sb("nvar", [P, 2, 4]), q.sb("nstd", [P, 2, 4])
        var_done, std_done = q.sem("nvar_done"), q.sem("nstd_done")
        shift = q.sb("nshift", [P, 2, 4])
        dummy = q.sb("ndummy", [P, 1])
        x_in = [q.sem(f"nx_in{s}") for s in range(2)]
        y_in = [q.sem(f"ny_in{s}") for s in range(2)]
        h_out = [q.sem(f"nh_out{s}") for s in range(2)]
        xh_out = [q.sem(f"nxh_out{s}") for s in range(2)]
        sum_done, bias_done, stats_done, aggr_done = q.sem("nsum"), q.sem("nbias"), q.sem("nstats_done"), q.sem("naggr")
        rstd_done, shift_done, norm_done, xh_done = q.sem("nrstd_done"), q.sem("nshift_done"), q.sem("nnorm"), q.sem("nxh_done")
        h_v = h_tab.rearrange("(i t p) f -> i p t f", t=4, p=P)
        y_v = y_tab.rearrange("(i t p) f -> i p t f", t=4, p=P)
        xh_v = xh_tab.rearrange("(i k) p (h f) -> i p k h f", k=2, h=2)


        def turns(eng, body):
            for s in range(2):
                body(0, s, x[s])
            with eng.Fori(1, IT // 2 - 1) as m:
                for s in range(2):
                    body(m, s, x[s])
            for s in range(2):
                body(IT // 2 - 1, s, x[s] if s == 0 else g["xlast"])

        def earlier(m, s, back):
            turn, slot = (m, s) if back == 0 else (m - (back - s + 1) // 2, (s - back) % 2)
            return (None if isinstance(turn, int) and turn < 0 else turn), slot

        block = ctx.enter_context(nc.Block())

        @block.sync
        def _(sp):
            def body(m, s, x_t):
                i = m * 2 + s
                if positive(i - 1):
                    sp.wait_ge(sum_done, i - 1)
                    sp.nop(nofuse=True)
                sp.dma_start(y[s][:, :, :], y_v[bass.ds(i, 1)].rearrange("a p t f -> (a p) t f")).then_inc(y_in[s], 16)
                if x_t is x[s]:
                    sp.dma_start(x_t[:, :, :], w["x"][bass.ds(i * 512, 512), :].rearrange("(t p) f -> p t f", p=P)).then_inc(x_in[s], 16)

            turns(sp, body)

        @block.vector
        def _(dve):
            v = nc.vector

            def statistics(m, s, x_t):
                i = m * 2 + s
                dve.wait_ge(y_in[s], m * 16 + 16)
                if x_t is x[s]:
                    dve.wait_ge(x_in[s], m * 16 + 16)
                if positive(i - 1):
                    dve.wait_ge(xh_done, i - 1)
                v.tensor_tensor(x1[s][:, :, :], x_t[:, :, :], y[s][:, :, :], ALU.add).then_inc(sum_done, 1)
                dve.wait_ge(sum_done, i + 1)
                v.tensor_tensor(x1[s][:, :, :], x1[s][:, :, :], g["agb2b"][:, :, :], ALU.add).then_inc(bias_done, 1)
                dve.wait_ge(bias_done, i + 1)
                for t in range(4):
                    v.bn_stats(stats[:, t, :], x1[s][:, t, :]).then_inc(stats_done, 1)
                dve.wait_ge(stats_done, i * 4 + 4)
                dve.nop(nofuse=True)
                for t in range(4):
                    v.bn_aggr(mv[:, s, t, :], stats[:, t, :]).then_inc(aggr_done, 1)
                dve.wait_ge(aggr_done, i * 4 + 4)
                v.tensor_scalar(var[:, s, :], mv[:, s, :, 1], EPS, None, ALU.add).then_inc(var_done, 1)

            def scale(m, s):
                i = m * 2 + s
                dve.wait_ge(std_done, i + 1)
                v.reciprocal(rstd[:, s, :], std[:, s, :]).then_inc(rstd_done, 1)
                dve.wait_ge(rstd_done, i + 1)
                v.scalar_tensor_tensor(shift[:, s, :], mv[:, s, :, 0], -1.0, rstd[:, s, :], ALU.mult, ALU.mult).then_inc(shift_done, 1)

            def add(m, s):
                i = m * 2 + s
                dve.wait_ge(norm_done, i * 4 + 4)
                if positive(m * 16):
                    dve.wait_ge(xh_out[s], m * 16)
                v.tensor_tensor(xh[s][:, :, :], x1[s][:, :, :], h[s][:, :, :], ALU.add).then_inc(xh_done, 1)

            def body(m, s, x_t):
                m2, s2 = earlier(m, s, 2)
                if m2 is not None:
                    add(m2, s2)
                m1, s1 = earlier(m, s, 1)
                if m1 is not None:
                    scale(m1, s1)
                statistics(m, s, x_t)

            turns(dve, body)
            add(IT // 2 - 1, 0)
            scale(IT // 2 - 1, 1)
            add(IT // 2 - 1, 1)

        @block.scalar
        def _(act):
            nc.scalar.activation(dummy[:, :], g["iota0"][:, 0:1], ACT.Sqrt)

            def normalise(m, s):
                i = m * 2 + s
                act.wait_ge(shift_done, i + 1)
                if positive(m * 16):
                    act.wait_ge(h_out[s], m * 16)
                if positive(i - 1):
                    act.wait_ge(xh_done, i - 1)
                for t in range(4):
                    nc.scalar.activation(h[s][:, t, :], x1[s][:, t, :], ACT.Relu, bias=shift[:, s, t:t + 1],
                                         scale=rstd[:, s, t:t + 1]).then_inc(norm_done, 1)

            def store(m, s):
                i = m * 2 + s
                act.wait_ge(xh_done, i + 1)
                act.nop(nofuse=True)
                act.dma_start(h_v[bass.ds(i, 1)].rearrange("a p t f -> (a p) t f"), h[s][:, :, :]).then_inc(h_out[s], 16)
                act.dma_start(xh_v[bass.ds(i, 1)].rearrange("a p k h f -> (a p) k (h f)"),
                              xh[s][:, :, :].rearrange("p (k h) f -> p k (h f)", k=2)).then_inc(xh_out[s], 16)

            def body(m, s, x_t):
                i = m * 2 + s
                m1, s1 = earlier(m, s, 1)
                if m1 is not None:
                    normalise(m1, s1)
                m2, s2 = earlier(m, s, 2)
                if m2 is not None:
                    store(m2, s2)
                act.wait_ge(var_done, i + 1)
                nc.scalar.activation(std[:, s, :], var[:, s, :], ACT.Sqrt).then_inc(std_done, 1)

            turns(act, body)
            normalise(IT // 2 - 1, 1)
            store(IT // 2 - 1, 0)
            store(IT // 2 - 1, 1)
            for s in range(2):
                act.wait_ge(h_out[s], 16 * (IT // 2))
                act.nop(nofuse=True)
                act.wait_ge(xh_out[s], 16 * (IT // 2))
                act.nop(nofuse=True)


def gnn_program(nc, w, out):
    def dram(name, shape, dt=FP32):
        return nc.dram_tensor(name, shape, dt).ap()

    he = dram("he", [TMAX * P, REC])
    a0, a1 = dram("a0", [NP, P]), dram("a1", [NP, P])
    br0, br1 = dram("br0", [NB, P, 512]), dram("br1", [NB, P, 512])
    y_tab, h_tab, xh_tab = dram("y_tab", [NP, P]), dram("h_tab", [NP, P]), dram("xh_tab", [NB, P, 256])
    with ExitStack() as ctx:
        q = Pools(nc, ctx)
        g = {
            "ne1": q.sb("ne1", [P, P]), "ee1": q.sb("ee1", [FE, P]), "agw2": q.sb("agw2", [P, P]),
            "ne_b1": q.sb("ne_b1", [P, 1]), "ee_b1": q.sb("ee_b1", [P, 1]),
            "agb2": q.sb("agb2", [1, P]), "agb2b": q.sb("agb2b", [P, 4, P]),
            "f0": q.sb("f0", [P, 384]), "f1": q.sb("f1", [P, 384]), "fe": q.sb("fe", [P, 256]),
            "fq": q.sb("fq", [P, 2, P]), "ebias": q.sb("ebias", [P, 256]), "crow": q.sb("crow", [1, 2, P]),
            "pbias": q.sb("pbias", [P, 2]),
            "ident": q.sb("ident", [P, P]), "identb": q.sb("identb", [P, P], BF16), "onecol": q.sb("onecol", [P, 1], BF16),
            "iota0": q.sb("iota0", [P, NS]), "iota1": q.sb("iota1", [P, SUB]), "iota1b": q.sb("iota1b", [P, SUB], BF16),
            "onesrow": q.sb("onesrow", [1, P]), "zrow": q.sb("zrow", [1, BLK], BF16), "zwide": q.sb("zwide", [P, BLK], BF16),
            "xlast": q.sb("xlast", [P, 4, P]), "ealast": q.sb("ealast", [P, 2, 4, FE]),
            "meta_d": q.sb("meta_d", [P, EC, 4], I32), "meta_s": q.sb("meta_s", [P, EC, 4], I32),
            "blk_d": q.sb("blk_d", [P, EC]), "blk_s": q.sb("blk_s", [P, EC]),
            "run_d": q.sb("run_d", [P, NS]), "run_s": q.sb("run_s", [P, NS]),
            "ends": q.sb("ends", [P, NS + 1], I32), "gends": q.sb("gends", [P, NB + 1], I32),
            "bounds": q.sb("bounds", [P, NB], I32),
            "nbr_in": [q.sem(f"nbr_in{j}") for j in range(PAIRS)],
            "turns": q.sb("turns", [P, 2], I32),
        }
        setup_phase(nc, w, g, he)
        dense_phase(nc, w, g, he, a0, br0)
        edge_phase(nc, g, he, 0, a0, br0, a1, br1, None)
        edge_phase(nc, g, he, 1, a1, br1, y_tab, None, None)
        norm_phase(nc, w, g, y_tab, h_tab, xh_tab)
        edge_phase(nc, g, he, 2, h_tab, xh_tab, None, None, out)


_INS = {"x": "x", "src": "src", "dst": "dst", "ea": "edge_attr_64"}
_INS.update({k: "L0_gnn_" + k for k in (
    "ne_w1", "ne_b1", "ne_w2", "ne_b2", "ee_w1", "ee_b1", "ee_w2", "ee_b2", "ml_w1", "ml_b1", "ml_w2", "ml_b2",
    "agg_w1", "agg_b1", "agg_w2", "agg_b2")})


def kernel(**inputs):
    import numpy as _np
    import concourse.bacc as _bacc
    from concourse import mybir as _mybir
    from concourse.bass_utils import run_bass_kernel_spmd as _run

    nc = _bacc.Bacc("TRN2", target_bir_lowering=False, num_devices=1)
    arrays, w = {}, {}
    for short, name in _INS.items():
        a = _np.ascontiguousarray(inputs[name])
        arrays[f"in_{name}"] = a
        w[short] = nc.dram_tensor(f"in_{name}", a.shape, _mybir.dt.from_np(a.dtype), kind="ExternalInput").ap()
    out = nc.dram_tensor("out_0", [N, P], _mybir.dt.float32, kind="ExternalOutput").ap()
    gnn_program(nc, w, out)
    r = _run(nc, [arrays], core_ids=[0])
    return r.results[0]["out_0"]
```
